# Optimizing a Trainium2 kernel written in Bass

```python
import numpy as np
import jax
import jax.numpy as jnp

def _softmax(x, axis=-1):
    return jax.nn.softmax(x, axis=axis)

def _gelu(x):
    return jax.nn.gelu(x, approximate=True)

def _silu(x):
    return jax.nn.silu(x)

def _sigmoid(x):
    return jax.nn.sigmoid(x)

def _layernorm(x, axis=-1, eps=1e-05):
    m = jnp.mean(x, axis=axis, keepdims=True)
    v = jnp.var(x, axis=axis, keepdims=True)
    return (x - m) / jnp.sqrt(v + eps)

def _scatter_add(tgt, idx, src, axis=0):
    return tgt.at[idx].add(src)

def _segment_sum(src, seg, n):
    return jax.ops.segment_sum(src, seg, n)
kernel_name = 'mk_adaln_ffn_d2_seqx_r4_f4bc80'

def setup_inputs(seed: int=0):
    np.random.seed(seed)
    _w = jnp.asarray

    def _rec_inputs():
        import jax
        import jax.numpy as jnp
        _rk = jax.random.key(seed)
        x = -0.000125 + 0.9999 * jax.random.normal(jax.random.fold_in(_rk, 1), (32, 256, 256), jnp.float32)
        _lenS = 256 - jax.random.randint(jax.random.fold_in(_rk, 7), (32,), 0, max(1, 256 // 4) + 1, jnp.int32)
        _lenS2 = 256 - jax.random.randint(jax.random.fold_in(_rk, 8), (32,), 0, max(1, 256 // 4) + 1, jnp.int32)
        cond_8 = jax.random.uniform(jax.random.fold_in(_rk, 11), (32, 8), jnp.float32, 0.0, 0.983423)
        return (x, cond_8)
    x, cond_8 = _rec_inputs()

    def _L0_cond_setup():
        import jax, jax.numpy as jnp
        import numpy as np
        B, S, D = (16, 512, 256)
        E, H = (8, 512)
        key = jax.random.key(seed)
        ks = jax.random.split(key, 8)
        scale = 0.02
        x = jax.random.normal(ks[0], (B, S, D), dtype=jnp.float32)
        opcode_onehot = jax.random.uniform(ks[1], (B, E), dtype=jnp.float32)
        W_up = jax.random.normal(ks[2], (E, H, D), dtype=jnp.float32) * scale
        b_up = jnp.zeros((E, H), dtype=jnp.float32)
        W_gate = jax.random.normal(ks[3], (E, H, D), dtype=jnp.float32) * scale
        b_gate = jnp.zeros((E, H), dtype=jnp.float32)
        W_down = jax.random.normal(ks[4], (E, D, H), dtype=jnp.float32) * scale
        b_down = jnp.zeros((E, D), dtype=jnp.float32)
        return {'x': x, 'opcode_onehot': opcode_onehot, 'W_up': W_up, 'b_up': b_up, 'W_gate': W_gate, 'b_gate': b_gate, 'W_down': W_down, 'b_down': b_down}
    _L0_cond_all = _L0_cond_setup()
    _L0_cond_in = {k: v for k, v in _L0_cond_all.items() if k in ('W_up', 'b_up', 'W_gate', 'b_gate', 'W_down', 'b_down')}
    del _L0_cond_all

    def _L0_ffn_setup():
        import jax, jax.numpy as jnp
        import numpy as np
        N_HEADS = 16
        N_KV_HEADS = 4
        N_EMBD = 256
        HEAD_DIM = N_EMBD // N_HEADS
        N_EXPERTS = 8
        TOP_K = 2
        EPS = 1e-06

        def _rmsnorm(x, w):
            xf = x.astype(jnp.float32)
            n = xf * jax.lax.rsqrt(jnp.mean(xf * xf, axis=-1, keepdims=True) + EPS)
            return n.astype(x.dtype) * w

        def _gqa(x, wq, wk, wv, wo):
            B, S, C = x.shape
            n_rep = N_HEADS // N_KV_HEADS
            q = (x @ wq.T).reshape(B, S, N_HEADS, HEAD_DIM)
            k = (x @ wk.T).reshape(B, S, N_KV_HEADS, HEAD_DIM)
            v = (x @ wv.T).reshape(B, S, N_KV_HEADS, HEAD_DIM)
            k = jnp.repeat(k, n_rep, axis=2)
            v = jnp.repeat(v, n_rep, axis=2)
            scale = 1.0 / np.sqrt(HEAD_DIM).astype(np.float32)
            attn = jnp.einsum('bqhd,bkhd->bhqk', q, k) * scale
            causal = jnp.tril(jnp.ones((S, S), dtype=bool))
            attn = jnp.where(causal, attn, jnp.float32(-jnp.inf))
            attn = jax.nn.softmax(attn, axis=-1)
            out = jnp.einsum('bhqk,bkhd->bqhd', attn, v).reshape(B, S, C)
            return out @ wo.T

        def _moe(x, gate_w, expert_w):
            B, S, C = x.shape
            t = x.reshape(B * S, C)
            logits = t @ gate_w.T
            w, sel = jax.lax.top_k(logits, TOP_K)
            w = jax.nn.softmax(w.astype(jnp.float32), axis=1).astype(t.dtype)
            comb = jnp.sum(w[..., None] * jax.nn.one_hot(sel, N_EXPERTS, dtype=t.dtype), axis=1)
            out = jnp.zeros_like(t)
            for e in range(N_EXPERTS):
                out = out + comb[:, e, None] * (t @ expert_w[e].T)
            return out.reshape(B, S, C)
        key = jax.random.key(seed)
        ks = jax.random.split(key, 10)
        B, S, C = (4, 512, N_EMBD)
        s = 0.02
        return {'x': jax.random.normal(ks[0], (B, S, C), dtype=jnp.float32), 'attn_norm_w': jnp.ones((C,), dtype=jnp.float32), 'ffn_norm_w': jnp.ones((C,), dtype=jnp.float32), 'wq': jax.random.normal(ks[1], (C, C), dtype=jnp.float32) * s, 'wk': jax.random.normal(ks[2], (N_KV_HEADS * HEAD_DIM, C), dtype=jnp.float32) * s, 'wv': jax.random.normal(ks[3], (N_KV_HEADS * HEAD_DIM, C), dtype=jnp.float32) * s, 'wo': jax.random.normal(ks[4], (C, C), dtype=jnp.float32) * s, 'gate_w': jax.random.normal(ks[5], (N_EXPERTS, C), dtype=jnp.float32) * s, 'expert_w': jax.random.normal(ks[6], (N_EXPERTS, C, C), dtype=jnp.float32) * s}
    _L0_ffn_all = _L0_ffn_setup()
    _L0_ffn_in = {k: v for k, v in _L0_ffn_all.items() if k in ('attn_norm_w', 'ffn_norm_w', 'wq', 'wk', 'wv', 'wo', 'gate_w', 'expert_w')}
    del _L0_ffn_all

    def _L1_cond_setup():
        import jax, jax.numpy as jnp
        import numpy as np
        R = 16
        ALPHA = 32.0
        SCALING = ALPHA / R
        key = jax.random.key(seed)
        ks = jax.random.split(key, 6)
        B, T, C, O, E = (16, 375, 256, 256, 8)
        x = jax.random.normal(ks[0], (B, T, C), dtype=jnp.float32)
        w = jax.random.uniform(ks[1], (B, E), dtype=jnp.float32)
        W_base = jax.random.normal(ks[2], (O, C), dtype=jnp.float32) * 0.02
        b_base = jax.random.normal(ks[3], (O,), dtype=jnp.float32) * 0.02
        As = jax.random.normal(ks[4], (E, R, C), dtype=jnp.float32) * 0.02
        Bs = jax.random.normal(ks[5], (E, O, R), dtype=jnp.float32) * 0.02
        return {'x': x, 'w': w, 'W_base': W_base, 'b_base': b_base, 'As': As, 'Bs': Bs}
    _L1_cond_all = _L1_cond_setup()
    _L1_cond_in = {k: v for k, v in _L1_cond_all.items() if k in ('W_base', 'b_base', 'As', 'Bs')}
    del _L1_cond_all

    def _L1_ffn_setup():
        import jax, jax.numpy as jnp
        import numpy as np
        B, S, D = (4, 1024, 256)
        E, F_EXP = (16, 512)
        F_C = 2.0
        F_SH = 512
        key = jax.random.key(seed)
        ks = jax.random.split(key, 8)
        s = 0.02
        return {'hidden_states': jax.random.normal(ks[0], (B, S, D), jnp.float32), 'gate_w': jax.random.normal(ks[1], (E, D), jnp.float32) * s, 'Wg': jax.random.normal(ks[2], (E, F_EXP, D), jnp.float32) * s, 'Wu': jax.random.normal(ks[3], (E, F_EXP, D), jnp.float32) * s, 'Wd': jax.random.normal(ks[4], (E, D, F_EXP), jnp.float32) * s, 'Ws_g': jax.random.normal(ks[5], (F_SH, D), jnp.float32) * s, 'Ws_u': jax.random.normal(ks[6], (F_SH, D), jnp.float32) * s, 'Ws_d': jax.random.normal(ks[7], (D, F_SH), jnp.float32) * s}
    _L1_ffn_all = _L1_ffn_setup()
    _L1_ffn_in = {k: v for k, v in _L1_ffn_all.items() if k in ('gate_w', 'Wg', 'Wu', 'Wd', 'Ws_g', 'Ws_u', 'Ws_d')}
    del _L1_ffn_all
    return {'x': x, 'cond_8': cond_8, 'L0_cond_W_up': _L0_cond_in['W_up'], 'L0_cond_b_up': _L0_cond_in['b_up'], 'L0_cond_W_gate': _L0_cond_in['W_gate'], 'L0_cond_b_gate': _L0_cond_in['b_gate'], 'L0_cond_W_down': _L0_cond_in['W_down'], 'L0_cond_b_down': _L0_cond_in['b_down'], 'L0_ffn_attn_norm_w': _L0_ffn_in['attn_norm_w'], 'L0_ffn_ffn_norm_w': _L0_ffn_in['ffn_norm_w'], 'L0_ffn_wq': _L0_ffn_in['wq'], 'L0_ffn_wk': _L0_ffn_in['wk'], 'L0_ffn_wv': _L0_ffn_in['wv'], 'L0_ffn_wo': _L0_ffn_in['wo'], 'L0_ffn_gate_w': _L0_ffn_in['gate_w'], 'L0_ffn_expert_w': _L0_ffn_in['expert_w'], 'L1_cond_W_base': _L1_cond_in['W_base'], 'L1_cond_b_base': _L1_cond_in['b_base'], 'L1_cond_As': _L1_cond_in['As'], 'L1_cond_Bs': _L1_cond_in['Bs'], 'L1_ffn_gate_w': _L1_ffn_in['gate_w'], 'L1_ffn_Wg': _L1_ffn_in['Wg'], 'L1_ffn_Wu': _L1_ffn_in['Wu'], 'L1_ffn_Wd': _L1_ffn_in['Wd'], 'L1_ffn_Ws_g': _L1_ffn_in['Ws_g'], 'L1_ffn_Ws_u': _L1_ffn_in['Ws_u'], 'L1_ffn_Ws_d': _L1_ffn_in['Ws_d']}

def reference(x, cond_8, L0_cond_W_up, L0_cond_b_up, L0_cond_W_gate, L0_cond_b_gate, L0_cond_W_down, L0_cond_b_down, L0_ffn_attn_norm_w, L0_ffn_ffn_norm_w, L0_ffn_wq, L0_ffn_wk, L0_ffn_wv, L0_ffn_wo, L0_ffn_gate_w, L0_ffn_expert_w, L1_cond_W_base, L1_cond_b_base, L1_cond_As, L1_cond_Bs, L1_ffn_gate_w, L1_ffn_Wg, L1_ffn_Wu, L1_ffn_Wd, L1_ffn_Ws_g, L1_ffn_Ws_u, L1_ffn_Ws_d):
    import jax
    import jax.numpy as jnp

    def _L0_cond_ref(x, opcode_onehot, W_up, b_up, W_gate, b_gate, W_down, b_down):
        import jax, jax.numpy as jnp
        import numpy as np
        B, S, D = (16, 512, 256)
        E, H = (8, 512)
        expert = jnp.argmax(opcode_onehot, axis=-1)
        wu, bu = (W_up[expert], b_up[expert])
        wg, bg = (W_gate[expert], b_gate[expert])
        wd, bd = (W_down[expert], b_down[expert])
        up = jnp.einsum('bsd,bhd->bsh', x, wu) + bu[:, None, :]
        gate = jnp.einsum('bsd,bhd->bsh', x, wg) + bg[:, None, :]
        hidden = jax.nn.silu(up) * gate
        out = jnp.einsum('bsh,bdh->bsd', hidden, wd) + bd[:, None, :]
        return out

    def _L0_ffn_ref(x, attn_norm_w, ffn_norm_w, wq, wk, wv, wo, gate_w, expert_w):
        import jax, jax.numpy as jnp
        import numpy as np
        N_HEADS = 16
        N_KV_HEADS = 4
        N_EMBD = 256
        HEAD_DIM = N_EMBD // N_HEADS
        N_EXPERTS = 8
        TOP_K = 2
        EPS = 1e-06

        def _rmsnorm(x, w):
            xf = x.astype(jnp.float32)
            n = xf * jax.lax.rsqrt(jnp.mean(xf * xf, axis=-1, keepdims=True) + EPS)
            return n.astype(x.dtype) * w

        def _gqa(x, wq, wk, wv, wo):
            B, S, C = x.shape
            n_rep = N_HEADS // N_KV_HEADS
            q = (x @ wq.T).reshape(B, S, N_HEADS, HEAD_DIM)
            k = (x @ wk.T).reshape(B, S, N_KV_HEADS, HEAD_DIM)
            v = (x @ wv.T).reshape(B, S, N_KV_HEADS, HEAD_DIM)
            k = jnp.repeat(k, n_rep, axis=2)
            v = jnp.repeat(v, n_rep, axis=2)
            scale = 1.0 / np.sqrt(HEAD_DIM).astype(np.float32)
            attn = jnp.einsum('bqhd,bkhd->bhqk', q, k) * scale
            causal = jnp.tril(jnp.ones((S, S), dtype=bool))
            attn = jnp.where(causal, attn, jnp.float32(-jnp.inf))
            attn = jax.nn.softmax(attn, axis=-1)
            out = jnp.einsum('bhqk,bkhd->bqhd', attn, v).reshape(B, S, C)
            return out @ wo.T

        def _moe(x, gate_w, expert_w):
            B, S, C = x.shape
            t = x.reshape(B * S, C)
            logits = t @ gate_w.T
            w, sel = jax.lax.top_k(logits, TOP_K)
            w = jax.nn.softmax(w.astype(jnp.float32), axis=1).astype(t.dtype)
            comb = jnp.sum(w[..., None] * jax.nn.one_hot(sel, N_EXPERTS, dtype=t.dtype), axis=1)
            out = jnp.zeros_like(t)
            for e in range(N_EXPERTS):
                out = out + comb[:, e, None] * (t @ expert_w[e].T)
            return out.reshape(B, S, C)
        h = x + _gqa(_rmsnorm(x, attn_norm_w), wq, wk, wv, wo)
        out = h + _moe(_rmsnorm(h, ffn_norm_w), gate_w, expert_w)
        return out

    def _L1_cond_ref(x, w, W_base, b_base, As, Bs):
        import jax, jax.numpy as jnp
        import numpy as np
        R = 16
        ALPHA = 32.0
        SCALING = ALPHA / R
        out = jnp.einsum('btc,oc->bto', x, W_base) + b_base
        h = jnp.einsum('btc,erc->bter', x, As)
        lora = jnp.einsum('bter,eor,be->bto', h, Bs, w)
        return out + lora * SCALING

    def _L1_ffn_ref(hidden_states, gate_w, Wg, Wu, Wd, Ws_g, Ws_u, Ws_d):
        import jax, jax.numpy as jnp
        import numpy as np
        B, S, D = (4, 1024, 256)
        E, F_EXP = (16, 512)
        F_C = 2.0
        F_SH = 512
        b, s, d = hidden_states.shape
        e = gate_w.shape[0]
        cap = int(s * F_C / e)
        logits = jnp.einsum('bsd,ed->bse', hidden_states, gate_w)
        scores = jax.nn.softmax(logits, axis=-1).transpose(0, 2, 1)
        topk_w, topk_idx = jax.lax.top_k(scores, cap)
        x_tok = jnp.take_along_axis(hidden_states[:, None, :, :], topk_idx[..., None], axis=2)
        g = jnp.einsum('becd,efd->becf', x_tok, Wg)
        u = jnp.einsum('becd,efd->becf', x_tok, Wu)
        h = jax.nn.gelu(g, approximate=False) * u
        eo = jnp.einsum('becf,edf->becd', h, Wd) * topk_w[..., None]
        offs = (jnp.arange(b) * s)[:, None, None]
        flat_idx = (topk_idx + offs).reshape(-1)
        flat = jnp.zeros((b * s, d), hidden_states.dtype)
        flat = flat.at[flat_idx].add(eo.reshape(-1, d))
        out = flat.reshape(b, s, d)
        gs = jnp.einsum('bsd,fd->bsf', hidden_states, Ws_g)
        us = jnp.einsum('bsd,fd->bsf', hidden_states, Ws_u)
        shared = jnp.einsum('bsf,df->bsd', jax.nn.gelu(gs, approximate=False) * us, Ws_d)
        return out + shared
    x = x + _L0_ffn_ref(_L0_cond_ref(x, cond_8, L0_cond_W_up, L0_cond_b_up, L0_cond_W_gate, L0_cond_b_gate, L0_cond_W_down, L0_cond_b_down), L0_ffn_attn_norm_w, L0_ffn_ffn_norm_w, L0_ffn_wq, L0_ffn_wk, L0_ffn_wv, L0_ffn_wo, L0_ffn_gate_w, L0_ffn_expert_w)
    x = x + _L1_ffn_ref(_L1_cond_ref(x, cond_8, L1_cond_W_base, L1_cond_b_base, L1_cond_As, L1_cond_Bs), L1_ffn_gate_w, L1_ffn_Wg, L1_ffn_Wu, L1_ffn_Wd, L1_ffn_Ws_g, L1_ffn_Ws_u, L1_ffn_Ws_d)
    return x

_drawn_inputs = setup_inputs


def setup_inputs(seed=0):
    import zlib

    import numpy as np

    out = dict(_drawn_inputs(seed))
    spreads = {'L0_cond_b_up': (0.0, 0.1),
     'L0_cond_b_gate': (0.0, 0.1),
     'L0_cond_b_down': (0.0, 0.1),
     'L0_ffn_attn_norm_w': (1.0, 0.2),
     'L0_ffn_ffn_norm_w': (1.0, 0.2)}
    factors = {'L0_ffn_wq': 8.0,
     'L0_ffn_wk': 8.0,
     'L1_cond_W_base': 8.0,
     'L1_cond_b_base': 8.0,
     'L1_cond_As': 8.0,
     'L1_cond_Bs': 8.0,
     'L1_ffn_gate_w': 8.0,
     'L1_ffn_Wg': 8.0,
     'L1_ffn_Wu': 8.0,
     'L1_ffn_Wd': 8.0,
     'L1_ffn_Ws_g': 8.0,
     'L1_ffn_Ws_u': 8.0,
     'L1_ffn_Ws_d': 8.0}
    for name, (base, spread) in spreads.items():
        noise = np.random.default_rng([zlib.crc32(name.encode()), seed]).standard_normal(out[name].shape)
        drawn = base * np.exp(spread * noise) if base else spread * noise
        out[name] = jnp.asarray(drawn.astype(out[name].dtype))
    for name, factor in factors.items():
        out[name] = (out[name] * factor).astype(out[name].dtype)
    return out
```

```python
from contextlib import ExitStack

import concourse.bass as bass
from concourse import mybir

F32 = mybir.dt.float32
F32R = mybir.dt.float32r
BF16 = mybir.dt.bfloat16
U32 = mybir.dt.uint32
ALU = mybir.AluOpType
ACT = mybir.ActivationFunctionType
AX_X = mybir.AxisListType.X

P = 128
B, S, D = 32, 256, 256
TT = S // P
KT = D // P
PAIRS = B // 2
E0, H0 = 8, 512
HT0 = H0 // P


def until(engine, semaphore, value):
    if not (isinstance(value, int) and value <= 0):
        engine.wait_ge(semaphore, value)


def after(j, par):
    return (j, 1) if par == 0 else (j + 1, 0)


def before(j, par):
    return (j, 0) if par == 1 else (j - 1, 1)


def rolled(engine, first, body, last):
    first()
    body(0, 0, False, True)
    body(0, 1, True, True)
    with engine.Fori(1, PAIRS - 1) as j:
        body(j, 0, True, True)
        body(j, 1, True, True)
    body(PAIRS - 1, 0, True, True)
    body(PAIRS - 1, 1, True, False)
    last()


def in_pairs(engine, prepare, compute, finish):
    def body(j, par, has_prev, has_next):
        if has_next:
            prepare(*after(j, par))
        compute(j, par)
        if has_prev:
            finish(*before(j, par))

    rolled(engine, lambda: prepare(0, 0), body, lambda: finish(PAIRS - 1, 1))


def alone(engine):
    engine.nop(nofuse=True)


def nothing(j, par):
    pass


def exact_product(nc, out, lhs, rhs, start, stop):
    (lhs_hi, lhs_lo), (rhs_hi, rhs_lo) = lhs, rhs
    nc.tensor.matmul(out, lhs_hi, rhs_lo, start=start, stop=False)
    nc.tensor.matmul(out, lhs_lo, rhs_hi, start=False, stop=False)
    return nc.tensor.matmul(out, lhs_hi, rhs_hi, start=False, stop=stop)


def cond_ffn_phase(nc, sem, x_t, w_ug, w_dn, cond, expert_dram, c0):
    UG = 2 * KT * H0
    DN = HT0 * D
    with ExitStack() as ctx:
        def sb(name, shape, dt=F32):
            return ctx.enter_context(nc.sbuf_tensor(name, shape, dt))

        cond_sb = sb("cond_sb", [B, E0])
        cond_top = sb("cond_top", [B, 8])
        cond_arg = sb("cond_arg", [B, 8], U32)
        expert_row = sb("expert_row", [1, B], U32)
        ug_raw = [sb(f"ug_raw{p}", [P, UG + 2 * HT0]) for p in range(2)]
        dn_raw = [sb(f"dn_raw{p}", [P, DN + D]) for p in range(2)]
        x_raw = [sb(f"x_raw{p}", [P, KT, S]) for p in range(2)]
        ug_bias = [sb(f"ug_bias{p}", [P, 2 * HT0]) for p in range(2)]
        dn_bias = [sb(f"dn_bias{p}", [P, D]) for p in range(2)]
        ug_hi = [sb(f"ug_hi{p}", [P, UG], F32R) for p in range(2)]
        ug_lo = [sb(f"ug_lo{p}", [P, UG], F32R) for p in range(2)]
        dn_hi = [sb(f"dn_hi{p}", [P, DN], F32R) for p in range(2)]
        dn_lo = [sb(f"dn_lo{p}", [P, DN], F32R) for p in range(2)]
        x_hi = [sb(f"x_hi{p}", [P, KT, S], F32R) for p in range(2)]
        x_lo = [sb(f"x_lo{p}", [P, KT, S], F32R) for p in range(2)]
        act_up = [sb(f"act_up{p}", [P, HT0, S]) for p in range(2)]
        hid = [sb(f"hid{p}", [P, HT0, S]) for p in range(2)]
        hid_hi = [sb(f"hid_hi{p}", [P, HT0, S], F32R) for p in range(2)]
        hid_lo = [sb(f"hid_lo{p}", [P, HT0, S], F32R) for p in range(2)]
        c0_sb = [sb(f"c0_sb{p}", [P, TT, D]) for p in range(2)]
        ps_up = [ctx.enter_context(nc.psum_tensor(f"ps_up{q}", [P, 2, S], F32)) for q in range(2)]
        ps_gate = [ctx.enter_context(nc.psum_tensor(f"ps_gate{q}", [P, 2, S], F32)) for q in range(2)]
        ps_down = [ctx.enter_context(nc.psum_tensor(f"ps_down{q}", [P, TT, D], F32)) for q in range(2)]

        cond_in = sem("cond_in")
        cond_max = sem("cond_max")
        expert_out = sem("expert_out")
        expert_in = sem("expert_in")
        ug_in = [sem(f"ug_in{p}") for p in range(2)]
        dn_in = [sem(f"dn_in{p}") for p in range(2)]
        ug_hi_done = sem("ug_hi_done")
        ug_lo_done = sem("ug_lo_done")
        dn_hi_done = sem("dn_hi_done")
        dn_lo_done = sem("dn_lo_done")
        up_gate_done = sem("up_gate_done")
        silu_done = sem("silu_done")
        hid_done = sem("hid_done")
        hid_hi_done = sem("hid_hi_done")
        hid_lo_done = sem("hid_lo_done")
        down_done = sem("down_done")
        c0_done = sem("c0_done")
        c0_out = [sem(f"c0_out{p}") for p in range(2)]

        block = ctx.enter_context(nc.Block())

        @block.sync
        def _(sp):
            sp.dma_start(cond_sb[:], cond).then_inc(cond_in, 16)
            sp.wait_ge(cond_max, 2)
            sp.dma_start(expert_dram, cond_arg[:, 0:1]).then_inc(expert_out, 16)
            sp.wait_ge(expert_out, 16)
            sp.dma_start(expert_row[:], expert_dram.rearrange("b a -> a b")).then_inc(expert_in, 16)
            sp.wait_ge(expert_in, 16)

            def load(j, par):
                i = 2 * j + par
                e = sp.value_load(expert_row[0:1, bass.ds(i, 1)], min_val=0, max_val=E0 - 1)
                until(sp, ug_hi_done, 3 * i - 3)
                until(sp, ug_lo_done, 2 * i - 2)
                sp.dma_start(ug_raw[par][:], w_ug[bass.ds(e, 1)].rearrange("e p n -> (e p) n")).then_inc(ug_in[par], 16)
                sp.dma_start(x_raw[par][:], x_t[bass.ds(i, 1)].rearrange("b p k s -> (b p) k s")).then_inc(ug_in[par], 16)
                until(sp, dn_hi_done, 2 * i - 2)
                alone(sp)
                until(sp, dn_lo_done, i - 1)
                sp.dma_start(dn_raw[par][:], w_dn[bass.ds(e, 1)].rearrange("e p n -> (e p) n")).then_inc(dn_in[par], 16)

            load(0, 0)
            load(0, 1)
            with sp.Fori(1, PAIRS) as j:
                load(j, 0)
                load(j, 1)

        @block.scalar
        def _(act):
            def split(j, par):
                i = 2 * j + par
                act.wait_ge(ug_in[par], 32 * j + 32)
                until(act, up_gate_done, 2 * i - 2)
                nc.scalar.activation(x_hi[par][:], x_raw[par][:], ACT.Copy).then_inc(ug_hi_done, 1)
                nc.scalar.activation(ug_hi[par][:], ug_raw[par][:, 0:UG], ACT.Copy).then_inc(ug_hi_done, 1)
                until(act, silu_done, 4 * i - 4)
                until(act, hid_done, 4 * i - 4)
                nc.scalar.activation(ug_bias[par][:], ug_raw[par][:, UG:UG + 2 * HT0], ACT.Copy).then_inc(ug_hi_done, 1)

            def middle(j, par):
                i = 2 * j + par
                act.wait_ge(ug_hi_done, 3 * i + 3)
                for q in range(2):
                    act.wait_ge(up_gate_done, 2 * i + q + 1)
                    if q == 0:
                        until(act, hid_done, 4 * i - 4)
                    for m in range(2):
                        t = 2 * q + m
                        nc.scalar.activation(act_up[par][:, t, :], ps_up[q][:, m, :], ACT.Silu,
                                             bias=ug_bias[par][:, t:t + 1]).then_inc(silu_done, 1)
                    if q == 0:
                        act.wait_ge(dn_in[par], 16 * j + 16)
                        until(act, down_done, i - 1)
                        until(act, c0_done, i - 1)
                        nc.scalar.activation(dn_hi[par][:], dn_raw[par][:, 0:DN], ACT.Copy).then_inc(dn_hi_done, 1)
                        nc.scalar.activation(dn_bias[par][:], dn_raw[par][:, DN:DN + D], ACT.Copy).then_inc(dn_hi_done, 1)
                    act.wait_ge(hid_done, 4 * i + 2 * q + 2)
                    until(act, down_done, i - 1)
                    nc.scalar.activation(hid_hi[par][:, 2 * q:2 * q + 2, :], hid[par][:, 2 * q:2 * q + 2, :], ACT.Copy).then_inc(hid_hi_done, 1)

            in_pairs(act, split, middle, nothing)

        @block.gpsimd
        def _(pool):
            def store(j, par):
                i = 2 * j + par
                pool.wait_ge(c0_done, i + 1)
                pool.dma_start(c0[bass.ds(i, 1)].rearrange("b p t d -> (b p) t d"), c0_sb[par][:]).then_inc(c0_out[par], 16)

            in_pairs(pool, nothing, nothing, store)
            for p in range(2):
                pool.wait_ge(c0_out[p], 16 * PAIRS)

        @block.vector
        def _(dve):
            dve.wait_ge(cond_in, 16)
            nc.vector.max(cond_top[:], cond_sb[:]).then_inc(cond_max, 1)
            dve.wait_ge(cond_max, 1)
            nc.vector.max_index(cond_arg[:], cond_top[:], cond_sb[:]).then_inc(cond_max, 1)

            def split(j, par):
                i = 2 * j + par
                dve.wait_ge(ug_hi_done, 3 * i + 2)
                until(dve, up_gate_done, 2 * i - 2)
                nc.vector.tensor_tensor(x_lo[par][:], x_raw[par][:], x_hi[par][:].bitcast(F32), ALU.subtract).then_inc(ug_lo_done, 1)
                nc.vector.tensor_tensor(ug_lo[par][:], ug_raw[par][:, 0:UG], ug_hi[par][:].bitcast(F32), ALU.subtract).then_inc(ug_lo_done, 1)

            def middle(j, par):
                i = 2 * j + par
                for q in range(2):
                    until(dve, hid_lo_done, 2 * i - 2 + q)
                    until(dve, hid_hi_done, 2 * i - 2 + q)
                    dve.wait_ge(silu_done, 4 * i + 2 * q + 2)
                    for m in range(2):
                        t = 2 * q + m
                        nc.vector.scalar_tensor_tensor(out=hid[par][:, t, :], in0=ps_gate[q][:, m, :],
                                                       scalar=ug_bias[par][:, HT0 + t:HT0 + t + 1], in1=act_up[par][:, t, :],
                                                       op0=ALU.add, op1=ALU.mult).then_inc(hid_done, 1)
                    if q == 0:
                        dve.wait_ge(dn_hi_done, 2 * i + 1)
                        until(dve, down_done, i - 1)
                        nc.vector.tensor_tensor(dn_lo[par][:], dn_raw[par][:, 0:DN], dn_hi[par][:].bitcast(F32), ALU.subtract).then_inc(dn_lo_done, 1)
                    dve.wait_ge(hid_hi_done, 2 * i + q + 1)
                    until(dve, down_done, i - 1)
                    nc.vector.tensor_tensor(hid_lo[par][:, 2 * q:2 * q + 2, :], hid[par][:, 2 * q:2 * q + 2, :],
                                            hid_hi[par][:, 2 * q:2 * q + 2, :].bitcast(F32), ALU.subtract).then_inc(hid_lo_done, 1)

            def finish(j, par):
                i = 2 * j + par
                dve.wait_ge(down_done, i + 1)
                dve.wait_ge(dn_hi_done, 2 * i + 2)
                until(dve, c0_out[par], 16 * j)
                bias = dn_bias[par][:].unsqueeze(1).broadcast_to([P, TT, D])
                nc.vector.tensor_tensor(c0_sb[par][:], ps_down[par][:], bias, ALU.add).then_inc(c0_done, 1)

            in_pairs(dve, split, middle, finish)

        @block.tensor
        def _(pe):
            def up_gate(j, par):
                i = 2 * j + par
                pe.wait_ge(ug_hi_done, 3 * i + 2)
                pe.wait_ge(ug_lo_done, 2 * i + 2)
                hi = ug_hi[par][:].rearrange("p (g k h) -> p g k h", g=2, k=KT)
                lo = ug_lo[par][:].rearrange("p (g k h) -> p g k h", g=2, k=KT)
                for q in range(2):
                    until(pe, hid_done, 4 * i - 2 + 2 * q)
                    until(pe, silu_done, 4 * i - 2 + 2 * q)
                    for g, ps in ((0, ps_up[q]), (1, ps_gate[q])):
                        for m in range(2):
                            cols = slice((2 * q + m) * P, (2 * q + m + 1) * P)
                            for k in range(KT):
                                last = exact_product(nc, ps[:, m, :], (hi[:, g, k, cols], lo[:, g, k, cols]),
                                                     (x_hi[par][:, k, :], x_lo[par][:, k, :]), k == 0, k == KT - 1)
                    last.then_inc(up_gate_done, 1)

            def down(j, par):
                i = 2 * j + par
                pe.wait_ge(dn_hi_done, 2 * i + 1)
                pe.wait_ge(dn_lo_done, i + 1)
                pe.wait_ge(hid_lo_done, 2 * i + 2)
                until(pe, c0_done, i - 1)
                hi = dn_hi[par][:].rearrange("p (h d) -> p h d", h=HT0)
                lo = dn_lo[par][:].rearrange("p (h d) -> p h d", h=HT0)
                for t in range(TT):
                    for h in range(HT0):
                        toks = slice(t * P, (t + 1) * P)
                        last = exact_product(nc, ps_down[par][:, t, :], (hid_hi[par][:, h, toks], hid_lo[par][:, h, toks]),
                                             (hi[:, h, :], lo[:, h, :]), h == 0, h == HT0 - 1)
                last.then_inc(down_done, 1)

            in_pairs(pe, nothing, up_gate, down)


NH, NKV, HD = 16, 4, 16
G = NH // NKV
QKV = NH * HD + 2 * NKV * HD
UNITS = 2 * NKV
EPS = 1e-6
MASKED = -1e30

PIECES = {"out_q1": (0, 0), "norm_t": (1, 0), "out_q0": (1, 1), "qkv_0": (2, 0), "out_t": (2, 1),
          "qkv_1": (3, 0), "out_proj": (3, 1), "k_0": (4, 0), "k_1": (4, 1),
          "q_1_a": (5, 0), "q_0_a": (5, 1), "q_1_b": (6, 0), "q_0_b": (6, 1)}
OUT_PIECES = [n for n in PIECES if n.startswith("out")]
PROJ_PIECES = [n for n in PIECES if not n.startswith("out")]


def attention_phase(nc, sem, c0, norm_w, w_qkv, w_o, ident_in, mask_in, h):
    with ExitStack() as ctx:
        def sb(name, shape, dt=F32):
            return ctx.enter_context(nc.sbuf_tensor(name, shape, dt))

        def bank(name, shape):
            return ctx.enter_context(nc.psum_tensor(name, shape, F32))

        ident = sb("at_ident", [P, P])
        identb = sb("at_identb", [P, P], BF16)
        mask = sb("at_mask", [P, P])
        maskb = sb("maskb", [P, G, P], BF16)
        nw = sb("at_norm_w", [P, D])
        wqkv_raw = sb("wqkv_raw", [P, KT, QKV])
        wqkv_hi = sb("wqkv_hi", [P, KT, QKV], F32R)
        wqkv_lo = sb("wqkv_lo", [P, KT, QKV], F32R)
        wo_raw = sb("wo_raw", [P, KT, D])
        wo_hi = sb("wo_hi", [P, KT, D], F32R)
        wo_lo = sb("wo_lo", [P, KT, D], F32R)
        minus_half = sb("at_minus_half", [P, TT])

        c0n = [sb(f"c0n{p}", [P, TT, D]) for p in range(2)]
        c0r = [sb(f"c0r{p}", [P, TT, D]) for p in range(2)]
        squares = sb("squares", [P, D])
        ssq = sb("ssq", [P, TT])
        msq = sb("msq", [P, TT])
        rstd = sb("rstd", [P, TT])
        normed = sb("normed", [P, TT, D])
        nt_hi = sb("nt_hi", [P, KT, S], F32R)
        nt_lo = sb("nt_lo", [P, KT, S], F32R)
        q_parts = [sb(f"q_parts{t}", [P, NH, 4, HD], F32R) for t in range(TT)]
        k_parts = [sb(f"k_parts{t}", [P, NKV, 4, 2, HD], F32R) for t in range(TT)]
        q_t = [sb(f"q_t{p}", [P, NH // 2, S], F32R) for p in range(2)]
        k_t = [sb(f"k_t{p}", [P, NKV, S], F32R) for p in range(2)]
        VW = NKV * P
        VSTEP = P + 2 * HD
        v_parts = [sb(f"v_parts{p}", [P, TT, VW + VSTEP], F32R) for p in range(2)]
        neg_max = [sb(f"neg_max{q}", [P, G]) for q in range(2)]
        probs = [sb(f"probs{q}", [P, G, (q + 1) * P]) for q in range(2)]
        pt_hi = [sb(f"pt_hi{q}", [P, q + 1, G * P], F32R) for q in range(2)]
        pt_lo = [sb(f"pt_lo{q}", [P, q + 1, G * P], F32R) for q in range(2)]
        sums = [sb(f"sums{p}", [P, TT, NKV, G]) for p in range(2)]
        rinv = [sb(f"rinv{q}", [P, G, NKV]) for q in range(2)]
        ot_sb = [sb(f"ot_sb{q}", [P, G, P]) for q in range(2)]
        on = [sb(f"on{q}", [P, G, NKV, 2, HD]) for q in range(2)]
        o = sb("o", [P, TT, D])
        o_hi = sb("o_hi", [P, KT, S], F32R)
        o_lo = sb("o_lo", [P, KT, S], F32R)
        h_sb = [sb(f"h_sb{p}", [P, TT, D]) for p in range(2)]

        s_q1 = [bank(f"s_q1_{n}", [P, 2, S]) for n in range(2)]
        s_q0 = bank("s_q0", [P, G, P])
        pt = [bank(f"pt{n}", [P, G * P]) for n in range(2)]
        ot = [bank(f"ot{q}", [P, G * P]) for q in range(2)]
        shared = bank("shared", [P, 512])
        shared_k = shared[:].rearrange("p (k s) -> p k s", k=KT)

        const_in = sem("at_const_in")
        w_hi_done = sem("at_w_hi_done")
        w_lo_done = sem("at_w_lo_done")
        set_done = sem("at_set_done")
        c0n_in = [sem(f"c0n_in{p}") for p in range(2)]
        c0r_in = [sem(f"c0r_in{p}") for p in range(2)]
        ssq_done = sem("ssq_done")
        msq_done = sem("msq_done")
        rstd_done = sem("rstd_done")
        normed_done = sem("normed_done")
        piece_done = sem("piece_done")
        piece_free = sem("piece_free")
        nt_hi_done = sem("nt_hi_done")
        nt_lo_done = sem("nt_lo_done")
        qkv_hi_done = sem("qkv_hi_done")
        o_hi_done = sem("o_hi_done")
        half_done = sem("half_done")
        scores_done = sem("scores_done")
        max_done = sem("max_done")
        exp_done = sem("exp_done")
        pt_done = sem("pt_done")
        pt_hi_done = sem("pt_hi_done")
        pt_lo_done = sem("pt_lo_done")
        pv_done = sem("pv_done")
        ot_out = sem("ot_out")
        rinv_done = sem("rinv_done")
        heads_done = sem("heads_done")
        h_out = [sem(f"h_out{p}") for p in range(2)]

        def tile_of(u):
            return 1 - u % 2

        def banks(u):
            return 2 - u % 2

        def bank0(u):
            return 3 * (u // 2) + 2 * (u % 2)

        def places(j, par, has_prev, has_next):
            base = 26 * j + 13 * par + 5 if has_prev else len(PROJ_PIECES)
            names = [n for n in PIECES if (has_prev if n in OUT_PIECES else has_next)]
            return {n: base + c for c, n in enumerate(names)}

        FIRST = {n: c for c, n in enumerate(PROJ_PIECES)}
        LAST = {n: 13 * B - len(OUT_PIECES) + c for c, n in enumerate(OUT_PIECES)}
        LAST_BATCH = (PAIRS - 1, 1)

        def v_slots(par, t, part):
            return v_parts[par][:, t, part * HD:part * HD + NKV * VSTEP].rearrange("p (g c) -> p g c", c=VSTEP)[:, :, 0:HD]

        def transposed(name, par):
            t = int(name[2])
            if name[0] == "k":
                return k_t[par][:, :, t * P:(t + 1) * P]
            c = 4 * "ab".index(name[4])
            return q_t[par][:, c:c + 4, t * P:(t + 1) * P]

        def step_pieces(piece, n, u, place, j, par):
            for name in n:
                if PIECES[name] == (u, place):
                    piece(name, *(before(j, par) if name in OUT_PIECES else after(j, par)), n[name])

        block = ctx.enter_context(nc.Block())

        @block.sync
        def _(sp):
            for dst, src in ((wqkv_raw, w_qkv), (wo_raw, w_o), (nw, norm_w), (ident, ident_in), (mask, mask_in)):
                sp.dma_start(dst[:], src).then_inc(const_in, 16)

            def load(j, par):
                i = 2 * j + par
                until(sp, normed_done, 2 * i - 2)
                sp.dma_start(c0n[par][:], c0[bass.ds(i, 1)].rearrange("b p t d -> (b p) t d")).then_inc(c0n_in[par], 16)
                until(sp, h_out[par], 16 * j)
                sp.dma_start(c0r[par][:], c0[bass.ds(i, 1)].rearrange("b p t d -> (b p) t d")).then_inc(c0r_in[par], 16)

            load(0, 0)
            load(0, 1)
            with sp.Fori(1, PAIRS) as j:
                load(j, 0)
                load(j, 1)

        @block.gpsimd
        def _(pool):
            def root(j, par):
                i = 2 * j + par
                pool.wait_ge(msq_done, i + 1)
                until(pool, normed_done, 2 * i)
                nc.gpsimd.tensor_tensor(rstd[:], msq[:], minus_half[:], ALU.pow).then_inc(rstd_done, 1)

            def piece(name, j, par, n):
                if name in ("out_q1", "out_q0"):
                    q = int(name[-1])
                    pool.wait_ge(piece_free, n + 1)
                    out = o[:, q, :].rearrange("p (g j d) -> p j g d", g=NKV, j=G)
                    nc.gpsimd.tensor_tensor(out, on[q][:, :, :, 0, :], on[q][:, :, :, 1, :], ALU.add).then_inc(heads_done, 1)
                elif name == "out_proj":
                    i = 2 * j + par
                    pool.wait_ge(piece_free, n + 1)
                    pool.dma_start(h[bass.ds(i, 1)].rearrange("b p t d -> (b p) t d"), h_sb[par][:]).then_inc(h_out[par], 16)

            def first():
                for p in range(2):
                    nc.gpsimd.memset(v_parts[p][:].bitcast(F32), 0.0).then_inc(set_done, 1)
                nc.gpsimd.memset(minus_half[:], -0.5).then_inc(set_done, 1)
                pool.wait_ge(set_done, 3)
                root(0, 0)

            def body(j, par, has_prev, has_next):
                n = places(j, par, has_prev, has_next)
                if has_next:
                    root(*after(j, par))
                for u in range(UNITS):
                    for place in range(2):
                        step_pieces(piece, n, u, place, j, par)

            def last():
                for name in OUT_PIECES:
                    piece(name, *LAST_BATCH, LAST[name])

            rolled(pool, first, body, last)
            for p in range(2):
                pool.wait_ge(h_out[p], 16 * PAIRS)

        @block.scalar
        def _(act):
            def square_sums(j, par):
                i = 2 * j + par
                act.wait_ge(c0n_in[par], 16 * j + 16)
                until(act, msq_done, i)
                for t in range(TT):
                    until(act, ssq_done, 2 * i + t)
                    nc.scalar.activation(squares[:], c0n[par][:, t, :], ACT.Square, accum_out=ssq[:, t:t + 1]).then_inc(ssq_done, 1)

            def piece(name, j, par, n):
                i = 2 * j + par
                if name in ("norm_t", "out_t"):
                    hi, done = (nt_hi, nt_hi_done) if name == "norm_t" else (o_hi, o_hi_done)
                    act.wait_ge(piece_done, n + 1)
                    nc.scalar.activation(hi[:], shared_k, ACT.Copy).then_inc(done, 1)
                elif name in ("qkv_0", "qkv_1"):
                    t = int(name[-1])
                    act.wait_ge(piece_done, n + 1)
                    q = shared[:, 0:D].rearrange("p (h d) -> p h d", h=NH).unsqueeze(2).broadcast_to([P, NH, 2, HD])
                    nc.scalar.activation(q_parts[t][:, :, 0:2, :], q, ACT.Copy).then_inc(qkv_hi_done, 1)
                    k = shared[:, D:D + NKV * HD].rearrange("p (h d) -> p h d", h=NKV).unsqueeze(2).broadcast_to([P, NKV, 4, HD])
                    nc.scalar.activation(k_parts[t][:, :, :, 0, :], k, ACT.Copy).then_inc(qkv_hi_done, 1)
                    act.wait_ge(set_done, 3)
                    until(act, pv_done, 8 * i - 8)
                    v = shared[:, D + NKV * HD:QKV].rearrange("p (h d) -> p h d", h=NKV)
                    nc.scalar.activation(v_slots(par, t, 0), v, ACT.Copy).then_inc(qkv_hi_done, 1)
                elif name in ("k_0", "q_1_a", "q_1_b"):
                    act.wait_ge(piece_done, n + 1)
                    nc.scalar.activation(transposed(name, par), shared[:].rearrange("p (c s) -> p c s", s=P), ACT.Copy).then_inc(piece_free, 1)

            def exps(j, par, u):
                i = 2 * j + par
                q, g = tile_of(u), u // 2
                until(act, pt_done, 12 * i + (bank0(u - 1) if u else -1))
                if u < 2:
                    until(act, rinv_done, 2 * i - 2)
                for m in (0, 2, 1, 3):
                    act.wait_ge(max_done, 12 * i + bank0(u) + (m % 2 + 1 if q else 1))
                    src = s_q1[m % 2][:, m // 2, :] if q else s_q0[:, m, :]
                    nc.scalar.activation(probs[q][:, m, :], src, ACT.Exp, bias=neg_max[q][:, m:m + 1],
                                         accum_out=sums[par][:, q, g, m:m + 1]).then_inc(exp_done, 1)

            def high_parts(j, par, u):
                i = 2 * j + par
                q = tile_of(u)
                until(act, pv_done, 8 * i + u - 1)
                for n in range(banks(u)):
                    act.wait_ge(pt_done, 12 * i + bank0(u) + n + 1)
                    nc.scalar.activation(pt_hi[q][:, n, :], pt[n][:], ACT.Copy).then_inc(pt_hi_done, 1)

            def empty_ot(j, par, q):
                i = 2 * j + par
                act.wait_ge(pv_done, 8 * i + 8 - q)
                nc.scalar.activation(ot_sb[q][:].rearrange("p j s -> p (j s)"), ot[q][:], ACT.Copy).then_inc(ot_out, 1)

            def first():
                act.wait_ge(const_in, 16 * 5)
                nc.scalar.activation(identb[:], ident[:], ACT.Copy).then_inc(w_hi_done, 1)
                nc.scalar.activation(maskb[:], mask[:].unsqueeze(1).broadcast_to([P, G, P]), ACT.Copy).then_inc(w_hi_done, 1)
                for t in range(KT):
                    nc.scalar.activation(wqkv_hi[:, t, 0:D], wqkv_raw[:, t, 0:D], ACT.Copy, scale=HD ** -0.5).then_inc(w_hi_done, 1)
                    nc.scalar.activation(wqkv_hi[:, t, D:QKV], wqkv_raw[:, t, D:QKV], ACT.Copy).then_inc(w_hi_done, 1)
                nc.scalar.activation(wo_hi[:], wo_raw[:], ACT.Copy).then_inc(w_hi_done, 1)
                square_sums(0, 0)
                for name in PROJ_PIECES:
                    piece(name, 0, 0, FIRST[name])
                exps(0, 0, 0)

            def body(j, par, has_prev, has_next):
                n = places(j, par, has_prev, has_next)
                for u in range(UNITS):
                    if has_prev and u < 2:
                        empty_ot(*before(j, par), 1 - u)
                    if has_next and u == 0:
                        square_sums(*after(j, par))
                    step_pieces(piece, n, u, 0, j, par)
                    if u + 1 < UNITS:
                        exps(j, par, u + 1)
                    elif has_next:
                        exps(*after(j, par), 0)
                    high_parts(j, par, u)
                    step_pieces(piece, n, u, 1, j, par)

            def last():
                for q in (1, 0):
                    empty_ot(*LAST_BATCH, q)
                for name in OUT_PIECES:
                    piece(name, *LAST_BATCH, LAST[name])

            rolled(act, first, body, last)

        @block.vector
        def _(dve):
            def mean_squares(j, par):
                i = 2 * j + par
                dve.wait_ge(ssq_done, 2 * i + 2)
                until(dve, rstd_done, i)
                nc.vector.tensor_scalar(msq[:], ssq[:], 1.0 / D, EPS, ALU.mult, ALU.add).then_inc(msq_done, 1)

            def normalise(j, par):
                i = 2 * j + par
                dve.wait_ge(rstd_done, i + 1)
                for t in range(TT):
                    nc.vector.scalar_tensor_tensor(out=normed[:, t, :], in0=c0n[par][:, t, :], scalar=rstd[:, t:t + 1], in1=nw[:],
                                                   op0=ALU.mult, op1=ALU.mult).then_inc(normed_done, 1)

            def piece(name, j, par, n):
                i = 2 * j + par
                if name in ("norm_t", "out_t"):
                    hi, lo, done = (nt_hi, nt_lo, nt_hi_done) if name == "norm_t" else (o_hi, o_lo, o_hi_done)
                    dve.wait_ge(done, i + 1)
                    nc.vector.tensor_tensor(lo[:], shared_k, hi[:].bitcast(F32), ALU.subtract).then_inc(piece_free, 1)
                elif name in ("qkv_0", "qkv_1"):
                    t = int(name[-1])
                    dve.wait_ge(qkv_hi_done, 6 * i + 3 * t + 3)
                    q = shared[:, 0:D].rearrange("p (h d) -> p h d", h=NH).unsqueeze(2).broadcast_to([P, NH, 2, HD])
                    nc.vector.tensor_tensor(q_parts[t][:, :, 2:4, :], q, q_parts[t][:, :, 0:2, :].bitcast(F32), ALU.subtract)
                    k = shared[:, D:D + NKV * HD].rearrange("p (h d) -> p h d", h=NKV).unsqueeze(2).broadcast_to([P, NKV, 4, HD])
                    nc.vector.tensor_tensor(k_parts[t][:, :, :, 1, :], k, k_parts[t][:, :, :, 0, :].bitcast(F32), ALU.subtract)
                    v = shared[:, D + NKV * HD:QKV].rearrange("p (h d) -> p h d", h=NKV)
                    nc.vector.tensor_tensor(v_slots(par, t, 1), v, v_slots(par, t, 0).bitcast(F32), ALU.subtract).then_inc(piece_free, 1)
                elif name in ("k_1", "q_0_a", "q_0_b"):
                    dve.wait_ge(piece_done, n + 1)
                    nc.vector.tensor_copy(transposed(name, par), shared[:].rearrange("p (c s) -> p c s", s=P)).then_inc(piece_free, 1)
                elif name in ("out_q1", "out_q0"):
                    q = int(name[-1])
                    dve.wait_ge(exp_done, 32 * i + 32)
                    nc.vector.reciprocal(rinv[q][:], sums[par][:, q, :, :].rearrange("p g j -> p j g")).then_inc(rinv_done, 1)
                    dve.wait_ge(rinv_done, 2 * i + 2 - q)
                    dve.wait_ge(piece_done, n + 1)
                    until(dve, heads_done, 2 * i - q)
                    scale = rinv[q][:].rearrange("p j g -> p (j g)").unsqueeze(2).broadcast_to([P, NH, 2 * HD])
                    nc.vector.tensor_tensor(on[q][:].rearrange("p j g a d -> p (j g) (a d)"),
                                            shared[:].rearrange("p (h d) -> p h d", h=NH), scale, ALU.mult).then_inc(piece_free, 1)
                elif name == "out_proj":
                    dve.wait_ge(piece_done, n + 1)
                    dve.wait_ge(c0r_in[par], 16 * j + 16)
                    until(dve, h_out[par], 16 * j)
                    nc.vector.tensor_tensor(h_sb[par][:], shared[:].rearrange("p (t d) -> p t d", t=TT), c0r[par][:], ALU.add).then_inc(piece_free, 1)

            def maxima(j, par, u):
                i = 2 * j + par
                q = tile_of(u)
                until(dve, exp_done, 32 * i + 4 * u - 4)
                for n in range(banks(u)):
                    dve.wait_ge(scores_done, 12 * i + bank0(u) + n + 1)
                    out, src = (neg_max[q][:, n::2], s_q1[n][:]) if q else (neg_max[q][:], s_q0[:])
                    nc.vector.tensor_reduce(out, src, AX_X, ALU.max, negate=True).then_inc(max_done, 1)

            def low_parts(j, par, u):
                i = 2 * j + par
                q = tile_of(u)
                for n in range(banks(u)):
                    dve.wait_ge(pt_hi_done, 12 * i + bank0(u) + n + 1)
                    nc.vector.tensor_tensor(pt_lo[q][:, n, :], pt[n][:], pt_hi[q][:, n, :].bitcast(F32), ALU.subtract).then_inc(pt_lo_done, 1)

            def first():
                dve.wait_ge(w_hi_done, 2 * KT + 3)
                for t in range(KT):
                    nc.vector.scalar_tensor_tensor(out=wqkv_lo[:, t, 0:D], in0=wqkv_raw[:, t, 0:D], scalar=HD ** -0.5,
                                                   in1=wqkv_hi[:, t, 0:D].bitcast(F32), op0=ALU.mult, op1=ALU.subtract).then_inc(w_lo_done, 1)
                    nc.vector.tensor_tensor(wqkv_lo[:, t, D:QKV], wqkv_raw[:, t, D:QKV], wqkv_hi[:, t, D:QKV].bitcast(F32),
                                            ALU.subtract).then_inc(w_lo_done, 1)
                nc.vector.tensor_tensor(wo_lo[:], wo_raw[:], wo_hi[:].bitcast(F32), ALU.subtract).then_inc(w_lo_done, 1)
                mean_squares(0, 0)
                normalise(0, 0)
                for name in PROJ_PIECES:
                    piece(name, 0, 0, FIRST[name])
                maxima(0, 0, 0)

            def body(j, par, has_prev, has_next):
                n = places(j, par, has_prev, has_next)
                for u in range(UNITS):
                    if u + 1 < UNITS:
                        maxima(j, par, u + 1)
                    elif has_next:
                        maxima(*after(j, par), 0)
                    if has_next and u == 0:
                        mean_squares(*after(j, par))
                    step_pieces(piece, n, u, 0, j, par)
                    low_parts(j, par, u)
                    if has_next and u == 0:
                        normalise(*after(j, par))
                    step_pieces(piece, n, u, 1, j, par)

            def last():
                for name in OUT_PIECES:
                    piece(name, *LAST_BATCH, LAST[name])

            rolled(dve, first, body, last)

        @block.tensor
        def _(pe):
            def piece(name, j, par, n):
                i = 2 * j + par
                until(pe, piece_free, n)
                if name == "norm_t":
                    pe.wait_ge(normed_done, 2 * i + 2)
                    for t in range(TT):
                        for k in range(KT):
                            last = nc.tensor.transpose(shared[:, k * S + t * P:k * S + (t + 1) * P], normed[:, t, k * P:(k + 1) * P], ident[:])
                elif name in ("qkv_0", "qkv_1"):
                    t = slice(int(name[-1]) * P, (int(name[-1]) + 1) * P)
                    for k in range(KT):
                        last = exact_product(nc, shared[:, 0:QKV], (nt_hi[:, k, t], nt_lo[:, k, t]),
                                             (wqkv_hi[:, k, :], wqkv_lo[:, k, :]), k == 0, k == KT - 1)
                elif name in ("k_0", "k_1"):
                    for g in range(NKV):
                        src = k_parts[int(name[2])][:, g].rearrange("p a b d -> p (a b d)")
                        last = nc.tensor.transpose(shared[:, g * P:(g + 1) * P], src.bitcast(F32), ident[:])
                elif name[0] == "q":
                    for c in range(4):
                        pair = 4 * "ab".index(name[4]) + c
                        src = q_parts[int(name[2])][:, 2 * pair:2 * pair + 2].rearrange("p h a d -> p (h a d)")
                        last = nc.tensor.transpose(shared[:, c * P:(c + 1) * P], src.bitcast(F32), ident[:])
                elif name in ("out_q1", "out_q0"):
                    q = int(name[-1])
                    pe.wait_ge(ot_out, 2 * i + 2 - q)
                    for c in range(G):
                        last = nc.tensor.transpose(shared[:, c * P:(c + 1) * P], ot_sb[q][:, c, :], ident[:])
                elif name == "out_t":
                    pe.wait_ge(heads_done, 2 * i + 2)
                    for t in range(TT):
                        for k in range(KT):
                            last = nc.tensor.transpose(shared[:, k * S + t * P:k * S + (t + 1) * P], o[:, t, k * P:(k + 1) * P], ident[:])
                elif name == "out_proj":
                    for t in range(TT):
                        toks = slice(t * P, (t + 1) * P)
                        for k in range(KT):
                            last = exact_product(nc, shared[:, t * D:(t + 1) * D], (o_hi[:, k, toks], o_lo[:, k, toks]),
                                                 (wo_hi[:, k, :], wo_lo[:, k, :]), k == 0, k == KT - 1)
                last.then_inc(piece_done, 1)

            def scores(j, par, u):
                i = 2 * j + par
                q, g = tile_of(u), u // 2
                until(pe, exp_done, 32 * i + 4 * u - 4)
                for n in range(banks(u)):
                    out = s_q1[n] if q else s_q0
                    for half in ([n] if q else range(2)):
                        rows = slice(64 * half, 64 * half + 64)
                        if half and not q:
                            pe.wait_ge(half_done, 4 * i + g + 1)
                        for c in range(2):
                            last = nc.tensor.matmul(out[:, c if q else 2 * c + half, :], q_t[par][rows, 2 * g + c, q * P:(q + 1) * P],
                                                    k_t[par][rows, g, 0:(q + 1) * P], start=(c == 0 and (q == 1 or half == 0)), stop=False)
                        if not half and not q:
                            last.then_inc(half_done, 1)
                    nc.tensor.matmul(out[:, :, q * P:(q + 1) * P], identb[:], maskb[:, 0:(2 if q else G), :],
                                     start=False, stop=True).then_inc(scores_done, 1)

            def transposes(j, par, u):
                i = 2 * j + par
                q = tile_of(u)
                pe.wait_ge(exp_done, 32 * i + 4 * u + 4)
                until(pe, pt_lo_done, 12 * i + bank0(u) - (u % 2))
                for n in range(banks(u)):
                    for m in range(G):
                        last = nc.tensor.transpose(pt[n][:, m * P:(m + 1) * P], probs[q][:, m, n * P:(n + 1) * P], ident[:])
                    last.then_inc(pt_done, 1)

            def values(j, par, u):
                i = 2 * j + par
                q, g = tile_of(u), u // 2
                if g == 0:
                    until(pe, ot_out, 2 * i - q)
                pe.wait_ge(pt_lo_done, 12 * i + bank0(u) + banks(u))
                for n in range(banks(u)):
                    v = v_parts[par][:, n, g * P:(g + 1) * P]
                    nc.tensor.matmul(ot[q][:], v, pt_lo[q][:, n, :], start=(g == 0 and n == 0), stop=False)
                    last = nc.tensor.matmul(ot[q][:], v, pt_hi[q][:, n, :], start=False, stop=(g == NKV - 1 and n == q))
                last.then_inc(pv_done, 1)

            def first():
                pe.wait_ge(const_in, 16 * 5)
                pe.wait_ge(w_hi_done, 2 * KT + 3)
                pe.wait_ge(w_lo_done, 2 * KT + 1)
                for name in PROJ_PIECES:
                    piece(name, 0, 0, FIRST[name])
                pe.wait_ge(piece_free, FIRST["q_0_a"] + 1)
                scores(0, 0, 0)

            def body(j, par, has_prev, has_next):
                n = places(j, par, has_prev, has_next)
                for u in range(UNITS):
                    if u + 1 < UNITS:
                        scores(j, par, u + 1)
                    elif has_next:
                        pe.wait_ge(piece_free, n["q_0_a"] + 1)
                        scores(*after(j, par), 0)
                    step_pieces(piece, n, u, 0, j, par)
                    transposes(j, par, u)
                    step_pieces(piece, n, u, 1, j, par)
                    if u > 0:
                        values(j, par, u - 1)
                    elif has_prev:
                        values(*before(j, par), UNITS - 1)

            def last():
                values(*LAST_BATCH, UNITS - 1)
                for name in OUT_PIECES:
                    piece(name, *LAST_BATCH, LAST[name])

            rolled(pe, first, body, last)


EM = 8
EBANKS = 4


def moe_phase(nc, sem, h, x, norm_w, gate_w, expert_w, ident_in, iota_in, x1):
    with ExitStack() as ctx:
        def sb(name, shape, dt=F32):
            return ctx.enter_context(nc.sbuf_tensor(name, shape, dt))

        def bank(name, shape):
            return ctx.enter_context(nc.psum_tensor(name, shape, F32))

        ident = sb("mo_ident", [P, P])
        iota = sb("mo_iota", [P, EM])
        nw = sb("mo_norm_w", [P, D])
        gw_raw = sb("gw_raw", [P, KT, EM])
        gw_hi = sb("gw_hi", [P, KT, EM], F32R)
        gw_lo = sb("gw_lo", [P, KT, EM], F32R)
        we_raw = sb("we_raw", [P, KT, EM * D])
        we_hi = sb("we_hi", [P, KT, EM * D], F32R)
        we_lo = sb("we_lo", [P, KT, EM * D], F32R)
        minus_half = sb("mo_minus_half", [P, TT])
        h_in = [sb(f"h_in{p}", [P, TT, D]) for p in range(2)]
        x_in = [sb(f"x_in{p}", [P, TT, D]) for p in range(2)]
        acc = [sb(f"acc{p}", [P, TT, D]) for p in range(2)]
        squares = sb("mo_squares", [P, D])
        ssq = sb("mo_ssq", [P, TT])
        msq = sb("mo_msq", [P, TT])
        rstd = sb("mo_rstd", [P, TT])
        normed = sb("mo_normed", [P, TT, D])
        n_hi = [sb(f"n_hi{p}", [P, KT, S], F32R) for p in range(2)]
        n_lo = [sb(f"n_lo{p}", [P, KT, S], F32R) for p in range(2)]
        logits = sb("logits", [P, TT, EM])
        top = sb("top", [P, TT, 8])
        top_at = sb("top_at", [P, TT, 8], U32)
        picked = sb("picked", [P, TT, 2])
        gap = sb("gap", [P, TT])
        odds = sb("odds", [P, TT])
        odds1 = sb("odds1", [P, TT])
        share = sb("share", [P, TT, 2])
        one_hot = sb("one_hot", [P, TT, 2, EM])
        comb = [sb(f"comb{p}", [P, TT, EM]) for p in range(2)]
        norm_t = bank("norm_t", [P, KT, S])
        gate_ps = bank("gate_ps", [P, TT, EM])
        expert_ps = [bank(f"expert_ps{n}", [P, 2, D]) for n in range(EBANKS)]

        const_in = sem("mo_const_in")
        w_hi_done = sem("mo_w_hi_done")
        w_lo_done = sem("mo_w_lo_done")
        set_done = sem("mo_set_done")
        hx_in = [sem(f"hx_in{p}") for p in range(2)]
        ssq_done = sem("mo_ssq_done")
        msq_done = sem("mo_msq_done")
        rstd_done = sem("mo_rstd_done")
        normed_done = sem("mo_normed_done")
        norm_t_done = sem("norm_t_done")
        n_hi_done = sem("n_hi_done")
        n_lo_done = sem("n_lo_done")
        gate_done = sem("gate_done")
        logits_done = sem("logits_done")
        top_done = sem("top_done")
        odds_done = sem("odds_done")
        comb_done = sem("comb_done")
        expert_done = sem("expert_done")
        acc_set = sem("acc_set")
        acc_done = sem("acc_done")
        x1_out = [sem(f"x1_out{p}") for p in range(2)]
        NPAIR = EM // 2
        NB = TT * NPAIR

        block = ctx.enter_context(nc.Block())

        @block.sync
        def _(sp):
            for dst, src in ((we_raw, expert_w), (gw_raw, gate_w), (nw, norm_w), (ident, ident_in), (iota, iota_in)):
                sp.dma_start(dst[:], src).then_inc(const_in, 16)

            def load(j, par):
                i = 2 * j + par
                until(sp, normed_done, 2 * i - 2)
                alone(sp)
                until(sp, acc_set, i - 1)
                sp.dma_start(h_in[par][:], h[bass.ds(i, 1)].rearrange("b p t d -> (b p) t d")).then_inc(hx_in[par], 16)
                sp.dma_start(x_in[par][:], x[bass.ds(i, 1)].rearrange("b p t d -> (b p) t d")).then_inc(hx_in[par], 16)

            load(0, 0)
            load(0, 1)
            with sp.Fori(1, PAIRS) as j:
                load(j, 0)
                load(j, 1)

        @block.gpsimd
        def _(pool):
            def prepare(j, par):
                i = 2 * j + par
                pool.wait_ge(msq_done, i + 1)
                until(pool, normed_done, 2 * i)
                nc.gpsimd.tensor_tensor(rstd[:], msq[:], minus_half[:], ALU.pow).then_inc(rstd_done, 1)
                pool.wait_ge(hx_in[par], 32 * j + 32)
                until(pool, x1_out[par], 16 * j)
                nc.gpsimd.tensor_tensor(acc[par][:], h_in[par][:], x_in[par][:], ALU.add).then_inc(acc_set, 1)

            def first():
                nc.gpsimd.memset(minus_half[:], -0.5).then_inc(set_done, 1)
                pool.wait_ge(set_done, 1)
                prepare(0, 0)

            def store(j, par):
                i = 2 * j + par
                pool.wait_ge(acc_done, EM * TT * (i + 1))
                pool.dma_start(x1[bass.ds(i, 1)].rearrange("b p t d -> (b p) t d"), acc[par][:]).then_inc(x1_out[par], 16)

            def body(j, par, has_prev, has_next):
                if has_prev:
                    store(*before(j, par))
                if has_next:
                    prepare(*after(j, par))

            rolled(pool, first, body, lambda: store(PAIRS - 1, 1))
            for p in range(2):
                pool.wait_ge(x1_out[p], 16 * PAIRS)

        @block.scalar
        def _(act):
            def square_sums(j, par):
                i = 2 * j + par
                act.wait_ge(hx_in[par], 32 * j + 32)
                until(act, msq_done, i)
                for t in range(TT):
                    until(act, ssq_done, 2 * i + t)
                    nc.scalar.activation(squares[:], h_in[par][:, t, :], ACT.Square, accum_out=ssq[:, t:t + 1]).then_inc(ssq_done, 1)

            def high_parts(j, par):
                i = 2 * j + par
                act.wait_ge(norm_t_done, i + 1)
                until(act, expert_done, NB * (i - 1))
                nc.scalar.activation(n_hi[par][:], norm_t[:], ACT.Copy).then_inc(n_hi_done, 1)

            def second_odds(j, par):
                i = 2 * j + par
                act.wait_ge(top_done, 7 * i + 6)
                nc.scalar.activation(odds[:], gap[:], ACT.Exp).then_inc(odds_done, 1)

            def first():
                act.wait_ge(const_in, 16 * 5)
                nc.scalar.activation(we_hi[:], we_raw[:], ACT.Copy).then_inc(w_hi_done, 1)
                nc.scalar.activation(gw_hi[:], gw_raw[:], ACT.Copy).then_inc(w_hi_done, 1)
                square_sums(0, 0)
                high_parts(0, 0)
                second_odds(0, 0)

            def body(j, par, has_prev, has_next):
                if has_next:
                    square_sums(*after(j, par))
                    high_parts(*after(j, par))
                    second_odds(*after(j, par))

            rolled(act, first, body, lambda: None)

        @block.vector
        def _(dve):
            def normalise(j, par):
                i = 2 * j + par
                dve.wait_ge(ssq_done, 2 * i + 2)
                until(dve, rstd_done, i)
                nc.vector.tensor_scalar(msq[:], ssq[:], 1.0 / D, EPS, ALU.mult, ALU.add).then_inc(msq_done, 1)
                dve.wait_ge(rstd_done, i + 1)
                until(dve, norm_t_done, i)
                for t in range(TT):
                    nc.vector.scalar_tensor_tensor(out=normed[:, t, :], in0=h_in[par][:, t, :], scalar=rstd[:, t:t + 1], in1=nw[:],
                                                   op0=ALU.mult, op1=ALU.mult).then_inc(normed_done, 1)

            def low_parts(j, par):
                i = 2 * j + par
                dve.wait_ge(n_hi_done, i + 1)
                nc.vector.tensor_tensor(n_lo[par][:], norm_t[:], n_hi[par][:].bitcast(F32), ALU.subtract).then_inc(n_lo_done, 1)

            def top_two(j, par):
                i = 2 * j + par
                dve.wait_ge(gate_done, i + 1)
                until(dve, comb_done, 7 * i)
                nc.vector.tensor_copy(logits[:], gate_ps[:]).then_inc(logits_done, 1)
                dve.wait_ge(logits_done, i + 1)
                alone(dve)
                for t in range(TT):
                    nc.vector.max(top[:, t, :], logits[:, t, :]).then_inc(top_done, 1)
                for t in range(TT):
                    dve.wait_ge(top_done, 7 * i + t + 1)
                    alone(dve)
                    nc.vector.max_index(top_at[:, t, :], top[:, t, :], logits[:, t, :]).then_inc(top_done, 1)
                dve.wait_ge(top_done, 7 * i + 4)
                nc.vector.tensor_copy(picked[:], top_at[:, :, 0:2]).then_inc(top_done, 1)
                until(dve, odds_done, i)
                nc.vector.tensor_tensor(gap[:], top[:, :, 1], top[:, :, 0], ALU.subtract).then_inc(top_done, 1)
                dve.wait_ge(odds_done, i + 1)
                nc.vector.tensor_scalar(odds1[:], odds[:], 1.0, None, ALU.add).then_inc(top_done, 1)
                dve.wait_ge(top_done, 7 * i + 7)
                nc.vector.reciprocal(share[:, :, 0], odds1[:]).then_inc(comb_done, 1)
                dve.wait_ge(comb_done, 7 * i + 1)
                nc.vector.tensor_tensor(share[:, :, 1], odds[:], share[:, :, 0], ALU.mult).then_inc(comb_done, 1)
                dve.wait_ge(comb_done, 7 * i + 2)
                for t in range(TT):
                    for n in range(2):
                        nc.vector.tensor_scalar(one_hot[:, t, n, :], iota[:], picked[:, t, n:n + 1], share[:, t, n:n + 1],
                                                ALU.is_equal, ALU.mult).then_inc(comb_done, 1)
                dve.wait_ge(comb_done, 7 * i + 6)
                until(dve, acc_done, EM * TT * (i - 1))
                nc.vector.tensor_tensor(comb[par][:], one_hot[:, :, 0, :], one_hot[:, :, 1, :], ALU.add).then_inc(comb_done, 1)

            def add_experts(j, par, t, pairs):
                i = 2 * j + par
                for m in pairs:
                    n = NPAIR * t + m
                    if n == 0:
                        dve.wait_ge(comb_done, 7 * i + 7)
                        dve.wait_ge(acc_set, i + 1)
                    dve.wait_ge(expert_done, NB * i + n + 1)
                    for c in range(2):
                        until(dve, acc_done, EM * TT * i + 2 * n + c)
                        nc.vector.scalar_tensor_tensor(out=acc[par][:, t, :], in0=expert_ps[n % EBANKS][:, c, :],
                                                       scalar=comb[par][:, t, 2 * m + c:2 * m + c + 1], in1=acc[par][:, t, :],
                                                       op0=ALU.mult, op1=ALU.add).then_inc(acc_done, 1)

            def first():
                dve.wait_ge(w_hi_done, 2)
                nc.vector.tensor_tensor(we_lo[:], we_raw[:], we_hi[:].bitcast(F32), ALU.subtract).then_inc(w_lo_done, 1)
                nc.vector.tensor_tensor(gw_lo[:], gw_raw[:], gw_hi[:].bitcast(F32), ALU.subtract).then_inc(w_lo_done, 1)
                normalise(0, 0)
                low_parts(0, 0)
                top_two(0, 0)

            def body(j, par, has_prev, has_next):
                if has_next:
                    normalise(*after(j, par))
                add_experts(j, par, 0, range(0, 2))
                if has_next:
                    low_parts(*after(j, par))
                add_experts(j, par, 0, range(2, 4))
                add_experts(j, par, 1, range(0, 2))
                if has_next:
                    top_two(*after(j, par))
                add_experts(j, par, 1, range(2, 4))

            rolled(dve, first, body, lambda: None)

        @block.tensor
        def _(pe):
            def transposes(j, par):
                i = 2 * j + par
                pe.wait_ge(normed_done, 2 * i + 2)
                until(pe, n_lo_done, i)
                for t in range(TT):
                    for k in range(KT):
                        last = nc.tensor.transpose(norm_t[:, k, t * P:(t + 1) * P], normed[:, t, k * P:(k + 1) * P], ident[:])
                last.then_inc(norm_t_done, 1)

            def gate(j, par):
                i = 2 * j + par
                pe.wait_ge(n_lo_done, i + 1)
                until(pe, logits_done, i)
                for t in range(TT):
                    toks = slice(t * P, (t + 1) * P)
                    for k in range(KT):
                        last = exact_product(nc, gate_ps[:, t, :], (n_hi[par][:, k, toks], n_lo[par][:, k, toks]),
                                             (gw_hi[:, k, :], gw_lo[:, k, :]), k == 0, k == KT - 1)
                last.then_inc(gate_done, 1)

            def experts(j, par, t, pairs):
                i = 2 * j + par
                toks = slice(t * P, (t + 1) * P)
                for m in pairs:
                    n = NPAIR * t + m
                    cols = slice(2 * m * D, (2 * m + 2) * D)
                    until(pe, acc_done, EM * TT * i + 2 * (n - EBANKS) + 2)
                    out = expert_ps[n % EBANKS][:].rearrange("p e d -> p (e d)")
                    for k in range(KT):
                        last = exact_product(nc, out, (n_hi[par][:, k, toks], n_lo[par][:, k, toks]),
                                             (we_hi[:, k, cols], we_lo[:, k, cols]), k == 0, k == KT - 1)
                    last.then_inc(expert_done, 1)

            def first():
                pe.wait_ge(const_in, 16 * 5)
                pe.wait_ge(w_lo_done, 2)
                transposes(0, 0)
                gate(0, 0)

            def body(j, par, has_prev, has_next):
                experts(j, par, 0, range(0, 2))
                if has_next:
                    transposes(*after(j, par))
                experts(j, par, 0, range(2, 4))
                if has_next:
                    gate(*after(j, par))
                experts(j, par, 1, range(0, 4))

            rolled(pe, first, body, lambda: None)


ER = P
LORA_SCALE = 2.0
E1, H1 = 16, 512
HT1 = H1 // P


def lora_shared_phase(nc, sem, x1, cond_er, w_base, b_base, a_er, b_er, gate_w, ws_gu, ws_d, ident_in, hs, scores, out):
    GU = 2 * KT * H1
    DN = HT1 * D
    with ExitStack() as ctx:
        def sb(name, shape, dt=F32):
            return ctx.enter_context(nc.sbuf_tensor(name, shape, dt))

        def bank(name, shape):
            return ctx.enter_context(nc.psum_tensor(name, shape, F32))

        ident = sb("lo_ident", [P, P])
        cond_sb = sb("lo_cond", [ER, B])
        wb_sb = sb("wb_sb", [P, KT, D])
        bb_sb = sb("bb_sb", [P, D])
        a_raw = sb("a_raw", [ER, D])
        a_hi = sb("a_hi", [ER, D], F32R)
        a_lo = sb("a_lo", [ER, D], F32R)
        b_raw = sb("b_raw", [ER, D])
        rw_raw = sb("rw_raw", [P, KT, E1])
        rw_hi = sb("rw_hi", [P, KT, E1], F32R)
        rw_lo = sb("rw_lo", [P, KT, E1], F32R)
        gu_raw = sb("sh_gu_raw", [P, GU])
        gu_hi = sb("sh_gu_hi", [P, GU], F32R)
        gu_lo = sb("sh_gu_lo", [P, GU], F32R)
        dn_raw = sb("sh_dn_raw", [P, DN])
        dn_hi = sb("sh_dn_hi", [P, DN], F32R)
        dn_lo = sb("sh_dn_lo", [P, DN], F32R)
        x1_sb = [sb(f"x1_sb{p}", [P, TT, D]) for p in range(2)]
        x1_add = [sb(f"x1_add{p}", [P, TT, D]) for p in range(2)]
        b_scaled = sb("b_scaled", [ER, D])
        b_hi = sb("b_hi", [ER, D], F32R)
        b_lo = sb("b_lo", [ER, D], F32R)
        weff = sb("weff", [P, KT, D])
        weff_hi = sb("weff_hi", [P, KT, D], F32R)
        weff_lo = sb("weff_lo", [P, KT, D], F32R)
        xt_hi = sb("xt_hi", [P, KT, S], F32R)
        xt_lo = sb("xt_lo", [P, KT, S], F32R)
        hs_sb = [sb(f"hs_sb{p}", [P, TT, D]) for p in range(2)]
        ht_hi = [sb(f"ht_hi{p}", [P, KT, S], F32R) for p in range(2)]
        ht_lo = [sb(f"ht_lo{p}", [P, KT, S], F32R) for p in range(2)]
        neg_top = sb("neg_top", [P, TT])
        expd = sb("expd", [P, TT, E1])
        exp_sum = sb("exp_sum", [P, TT])
        exp_inv = sb("exp_inv", [P, TT])
        gelu = [sb(f"sh_gelu{q}", [P, 2, S]) for q in range(2)]
        hid = [sb(f"sh_hid{q}", [P, 2, S]) for q in range(2)]
        hid_hi = [sb(f"sh_hid_hi{q}", [P, 2, S], F32R) for q in range(2)]
        hid_lo = [sb(f"sh_hid_lo{q}", [P, 2, S], F32R) for q in range(2)]
        out_sb = [sb(f"out_sb{p}", [P, TT, D]) for p in range(2)]
        turned = bank("turned", [P, KT, S])
        cond_ps = bank("cond_ps", [P, TT, D])
        side = bank("side", [P, KT, D])
        gate_ps = [bank(f"sh_gate_ps{q}", [P, 2, S]) for q in range(2)]
        up_ps = [bank(f"sh_up_ps{q}", [P, 2, S]) for q in range(2)]
        down_ps = bank("sh_down_ps", [P, TT, D])

        const_in = sem("lo_const_in")
        w_hi_done = sem("lo_w_hi_done")
        w_lo_done = sem("lo_w_lo_done")
        x1_in = [sem(f"x1_in{p}") for p in range(2)]
        x1_add_in = [sem(f"x1_add_in{p}") for p in range(2)]
        b_scaled_done = sem("b_scaled_done")
        b_hi_done = sem("b_hi_done")
        b_lo_done = sem("b_lo_done")
        lora_done = sem("lora_done")
        weff_done = sem("weff_done")
        weff_hi_done = sem("weff_hi_done")
        weff_lo_done = sem("weff_lo_done")
        xt_done = sem("xt_done")
        xt_hi_done = sem("xt_hi_done")
        xt_lo_done = sem("xt_lo_done")
        cond_done = sem("cond_done")
        hs_done = sem("hs_done")
        hs_out = [sem(f"hs_out{p}") for p in range(2)]
        ht_done = sem("ht_done")
        ht_hi_done = sem("ht_hi_done")
        ht_lo_done = sem("ht_lo_done")
        route_done = sem("route_done")
        neg_top_done = sem("neg_top_done")
        expd_done = sem("expd_done")
        exp_inv_done = sem("exp_inv_done")
        scores_set = sem("scores_set")
        gate_up_done = sem("sh_gate_up_done")
        gelu_done = sem("sh_gelu_done")
        hid_done = sem("sh_hid_done")
        hid_hi_done = sem("sh_hid_hi_done")
        hid_lo_done = sem("sh_hid_lo_done")
        down_done = sem("sh_down_done")
        out_done = sem("sh_out_done")
        out_out = [sem(f"sh_out_out{p}") for p in range(2)]
        CONSTS = ((gu_raw, ws_gu), (dn_raw, ws_d), (a_raw, a_er), (b_raw, b_er), (rw_raw, gate_w),
                  (wb_sb, w_base), (bb_sb, b_base), (cond_sb, cond_er), (ident, ident_in))

        block = ctx.enter_context(nc.Block())

        @block.sync
        def _(sp):
            for dst, src in CONSTS:
                sp.dma_start(dst[:], src).then_inc(const_in, 16)

            def load(j, par):
                i = 2 * j + par
                until(sp, xt_done, i - 1)
                sp.dma_start(x1_sb[par][:], x1[bass.ds(i, 1)].rearrange("b p t d -> (b p) t d")).then_inc(x1_in[par], 16)
                until(sp, out_done, i - 1)
                sp.dma_start(x1_add[par][:], x1[bass.ds(i, 1)].rearrange("b p t d -> (b p) t d")).then_inc(x1_add_in[par], 16)

            load(0, 0)
            load(0, 1)
            with sp.Fori(1, PAIRS) as j:
                load(j, 0)
                load(j, 1)

        @block.gpsimd
        def _(pool):
            def body(j, par, has_prev, has_next):
                if has_next:
                    weff_low(*after(j, par))
                    store_hs(*after(j, par))
                if has_prev:
                    store_out(*before(j, par))

            def weff_low(j, par):
                i = 2 * j + par
                pool.wait_ge(weff_hi_done, i + 1)
                until(pool, cond_done, i)
                nc.gpsimd.tensor_tensor(weff_lo[:], weff[:], weff_hi[:].bitcast(F32), ALU.subtract).then_inc(weff_lo_done, 1)

            def store_hs(j, par):
                i = 2 * j + par
                pool.wait_ge(hs_done, i + 1)
                pool.dma_start(hs[bass.ds(i, 1)].rearrange("b (t p) d -> p (b t) d", p=P), hs_sb[par][:]).then_inc(hs_out[par], 16)

            def store_out(j, par):
                i = 2 * j + par
                pool.wait_ge(out_done, i + 1)
                pool.dma_start(out[bass.ds(i, 1)].rearrange("b (t p) d -> p (b t) d", p=P), out_sb[par][:]).then_inc(out_out[par], 16)

            def first():
                weff_low(0, 0)
                store_hs(0, 0)

            rolled(pool, first, body, lambda: store_out(PAIRS - 1, 1))
            for p in range(2):
                pool.wait_ge(hs_out[p], 16 * PAIRS)
                pool.wait_ge(out_out[p], 16 * PAIRS)

        @block.scalar
        def _(act):
            def b_high(j, par):
                i = 2 * j + par
                act.wait_ge(b_scaled_done, i + 1)
                until(act, lora_done, i)
                nc.scalar.activation(b_hi[:], b_scaled[:], ACT.Copy).then_inc(b_hi_done, 1)

            def weff_high(j, par):
                i = 2 * j + par
                act.wait_ge(weff_done, i + 1)
                until(act, cond_done, i)
                nc.scalar.activation(weff_hi[:], weff[:], ACT.Copy).then_inc(weff_hi_done, 1)

            def x1_high(j, par):
                i = 2 * j + par
                act.wait_ge(xt_done, i + 1)
                until(act, cond_done, i)
                nc.scalar.activation(xt_hi[:], turned[:], ACT.Copy).then_inc(xt_hi_done, 1)

            def hs_high(j, par):
                i = 2 * j + par
                act.wait_ge(ht_done, i + 1)
                until(act, gate_up_done, 2 * i - 2)
                until(act, route_done, i - 1)
                nc.scalar.activation(ht_hi[par][:], turned[:], ACT.Copy).then_inc(ht_hi_done, 1)

            def exps(j, par):
                i = 2 * j + par
                act.wait_ge(neg_top_done, i + 1)
                until(act, scores_set, TT * i)
                for t in range(TT):
                    nc.scalar.activation(expd[:, t, :], side[:, 0, t * E1:(t + 1) * E1], ACT.Exp, bias=neg_top[:, t:t + 1],
                                         accum_out=exp_sum[:, t:t + 1]).then_inc(expd_done, 1)

            def gelus(j, par, q):
                i = 2 * j + par
                act.wait_ge(gate_up_done, 2 * i + q + 1)
                until(act, hid_done, 2 * i - 1 + q)
                nc.scalar.activation(gelu[q][:], gate_ps[q][:], ACT.Gelu).then_inc(gelu_done, 1)

            def hidden_high(j, par, q):
                i = 2 * j + par
                act.wait_ge(hid_done, 2 * i + q + 1)
                until(act, down_done, i)
                nc.scalar.activation(hid_hi[q][:], hid[q][:], ACT.Copy).then_inc(hid_hi_done, 1)

            def first():
                act.wait_ge(const_in, 16 * len(CONSTS))
                for dst, src in ((gu_hi, gu_raw), (dn_hi, dn_raw), (a_hi, a_raw), (rw_hi, rw_raw)):
                    nc.scalar.activation(dst[:], src[:], ACT.Copy).then_inc(w_hi_done, 1)
                b_high(0, 0)
                x1_high(0, 0)
                weff_high(0, 0)
                hs_high(0, 0)

            def body(j, par, has_prev, has_next):
                exps(j, par)
                if has_next:
                    b_high(*after(j, par))
                    x1_high(*after(j, par))
                gelus(j, par, 0)
                if has_next:
                    weff_high(*after(j, par))
                hidden_high(j, par, 0)
                if has_next:
                    hs_high(*after(j, par))
                gelus(j, par, 1)
                hidden_high(j, par, 1)

            rolled(act, first, body, lambda: None)

        @block.vector
        def _(dve):
            def scale_b(j, par):
                i = 2 * j + par
                until(dve, b_hi_done, i)
                until(dve, b_lo_done, i)
                nc.vector.tensor_scalar(b_scaled[:], b_raw[:], cond_sb[:, bass.ds(i, 1)], LORA_SCALE, ALU.mult, ALU.mult).then_inc(b_scaled_done, 1)

            def b_low(j, par):
                i = 2 * j + par
                dve.wait_ge(b_hi_done, i + 1)
                until(dve, lora_done, i)
                nc.vector.tensor_tensor(b_lo[:], b_scaled[:], b_hi[:].bitcast(F32), ALU.subtract).then_inc(b_lo_done, 1)

            def x1_low(j, par):
                i = 2 * j + par
                dve.wait_ge(xt_hi_done, i + 1)
                until(dve, cond_done, i)
                nc.vector.tensor_tensor(xt_lo[:], turned[:], xt_hi[:].bitcast(F32), ALU.subtract).then_inc(xt_lo_done, 1)

            def add_base(j, par):
                i = 2 * j + par
                dve.wait_ge(lora_done, i + 1)
                until(dve, weff_lo_done, i)
                nc.vector.tensor_tensor(weff[:], side[:], wb_sb[:], ALU.add).then_inc(weff_done, 1)

            def add_bias(j, par):
                i = 2 * j + par
                dve.wait_ge(cond_done, i + 1)
                until(dve, hs_out[par], 16 * j)
                until(dve, ht_done, i - 1)
                bias = bb_sb[:].unsqueeze(1).broadcast_to([P, TT, D])
                nc.vector.tensor_tensor(hs_sb[par][:], cond_ps[:], bias, ALU.add).then_inc(hs_done, 1)

            def hs_low(j, par):
                i = 2 * j + par
                dve.wait_ge(ht_hi_done, i + 1)
                nc.vector.tensor_tensor(ht_lo[par][:], turned[:], ht_hi[par][:].bitcast(F32), ALU.subtract).then_inc(ht_lo_done, 1)

            def tops(j, par):
                i = 2 * j + par
                dve.wait_ge(route_done, i + 1)
                until(dve, expd_done, TT * i)
                nc.vector.tensor_reduce(neg_top[:], side[:, 0, 0:TT * E1].rearrange("p (t e) -> p t e", t=TT),
                                        AX_X, ALU.max, negate=True).then_inc(neg_top_done, 1)

            def softmax(j, par):
                i = 2 * j + par
                dve.wait_ge(expd_done, TT * i + TT)
                nc.vector.reciprocal(exp_inv[:], exp_sum[:]).then_inc(exp_inv_done, 1)
                dve.wait_ge(exp_inv_done, i + 1)
                for t in range(TT):
                    nc.vector.tensor_scalar(scores[:, t, bass.ds(i * E1, E1)], expd[:, t, :], exp_inv[:, t:t + 1], None,
                                            ALU.mult).then_inc(scores_set, 1)

            def hidden(j, par, q):
                i = 2 * j + par
                dve.wait_ge(gelu_done, 2 * i + q + 1)
                until(dve, hid_lo_done, 2 * i - 1 + q)
                nc.vector.tensor_tensor(hid[q][:], up_ps[q][:], gelu[q][:], ALU.mult).then_inc(hid_done, 1)

            def hidden_low(j, par, q):
                i = 2 * j + par
                dve.wait_ge(hid_hi_done, 2 * i + q + 1)
                until(dve, down_done, i)
                nc.vector.tensor_tensor(hid_lo[q][:], hid[q][:], hid_hi[q][:].bitcast(F32), ALU.subtract).then_inc(hid_lo_done, 1)

            def add_x1(j, par):
                i = 2 * j + par
                dve.wait_ge(down_done, i + 1)
                dve.wait_ge(x1_add_in[par], 16 * j + 16)
                until(dve, out_out[par], 16 * j)
                nc.vector.tensor_tensor(out_sb[par][:], down_ps[:], x1_add[par][:], ALU.add).then_inc(out_done, 1)

            def first():
                dve.wait_ge(w_hi_done, 4)
                for dst, src, hi in ((gu_lo, gu_raw, gu_hi), (dn_lo, dn_raw, dn_hi), (a_lo, a_raw, a_hi), (rw_lo, rw_raw, rw_hi)):
                    nc.vector.tensor_tensor(dst[:], src[:], hi[:].bitcast(F32), ALU.subtract).then_inc(w_lo_done, 1)
                scale_b(0, 0)
                b_low(0, 0)
                x1_low(0, 0)
                add_base(0, 0)
                add_bias(0, 0)
                hs_low(0, 0)

            def body(j, par, has_prev, has_next):
                tops(j, par)
                if has_next:
                    scale_b(*after(j, par))
                    b_low(*after(j, par))
                    x1_low(*after(j, par))
                softmax(j, par)
                hidden(j, par, 0)
                if has_next:
                    add_base(*after(j, par))
                hidden_low(j, par, 0)
                if has_next:
                    add_bias(*after(j, par))
                if has_prev:
                    add_x1(*before(j, par))
                if has_next:
                    hs_low(*after(j, par))
                hidden(j, par, 1)
                hidden_low(j, par, 1)

            rolled(dve, first, body, lambda: add_x1(PAIRS - 1, 1))

        @block.tensor
        def _(pe):
            gu_h = gu_hi[:].rearrange("p (g k h) -> p g k h", g=2, k=KT)
            gu_l = gu_lo[:].rearrange("p (g k h) -> p g k h", g=2, k=KT)
            dn_h = dn_hi[:].rearrange("p (h d) -> p h d", h=HT1)
            dn_l = dn_lo[:].rearrange("p (h d) -> p h d", h=HT1)

            def turn_x1(j, par):
                i = 2 * j + par
                pe.wait_ge(x1_in[par], 16 * j + 16)
                until(pe, ht_lo_done, i)
                for t in range(TT):
                    for k in range(KT):
                        last = nc.tensor.transpose(turned[:, k, t * P:(t + 1) * P], x1_sb[par][:, t, k * P:(k + 1) * P], ident[:])
                last.then_inc(xt_done, 1)

            def lora(j, par):
                i = 2 * j + par
                pe.wait_ge(b_lo_done, i + 1)
                until(pe, expd_done, TT * i)
                for k in range(KT):
                    c = slice(k * P, (k + 1) * P)
                    last = exact_product(nc, side[:, k, :], (a_hi[:, c], a_lo[:, c]), (b_hi[:], b_lo[:]), True, True)
                last.then_inc(lora_done, 1)

            def cond(j, par):
                i = 2 * j + par
                pe.wait_ge(xt_lo_done, i + 1)
                pe.wait_ge(weff_lo_done, i + 1)
                until(pe, hs_done, i)
                for t in range(TT):
                    toks = slice(t * P, (t + 1) * P)
                    for k in range(KT):
                        last = exact_product(nc, cond_ps[:, t, :], (xt_hi[:, k, toks], xt_lo[:, k, toks]),
                                             (weff_hi[:, k, :], weff_lo[:, k, :]), k == 0, k == KT - 1)
                last.then_inc(cond_done, 1)

            def turn_hs(j, par):
                i = 2 * j + par
                pe.wait_ge(hs_done, i + 1)
                for t in range(TT):
                    for k in range(KT):
                        last = nc.tensor.transpose(turned[:, k, t * P:(t + 1) * P], hs_sb[par][:, t, k * P:(k + 1) * P], ident[:])
                last.then_inc(ht_done, 1)

            def route(j, par):
                i = 2 * j + par
                pe.wait_ge(ht_lo_done, i + 1)
                pe.wait_ge(weff_done, i + 1)
                for t in range(TT):
                    toks = slice(t * P, (t + 1) * P)
                    for k in range(KT):
                        last = exact_product(nc, side[:, 0, t * E1:(t + 1) * E1], (ht_hi[par][:, k, toks], ht_lo[par][:, k, toks]),
                                             (rw_hi[:, k, :], rw_lo[:, k, :]), k == 0, k == KT - 1)
                last.then_inc(route_done, 1)

            def gate_up(j, par, q):
                i = 2 * j + par
                until(pe, hid_done, 2 * i - 1 + q)
                for g, ps in ((0, gate_ps[q]), (1, up_ps[q])):
                    for m in range(2):
                        cols = slice((2 * q + m) * P, (2 * q + m + 1) * P)
                        for k in range(KT):
                            last = exact_product(nc, ps[:, m, :], (gu_h[:, g, k, cols], gu_l[:, g, k, cols]),
                                                 (ht_hi[par][:, k, :], ht_lo[par][:, k, :]), k == 0, k == KT - 1)
                last.then_inc(gate_up_done, 1)

            def down(j, par, t):
                i = 2 * j + par
                if t == 0:
                    pe.wait_ge(hid_lo_done, 2 * i + 2)
                    until(pe, out_done, i)
                toks = slice(t * P, (t + 1) * P)
                for m in range(HT1):
                    last = exact_product(nc, down_ps[:, t, :], (hid_hi[m // 2][:, m % 2, toks], hid_lo[m // 2][:, m % 2, toks]),
                                         (dn_h[:, m, :], dn_l[:, m, :]), m == 0, m == HT1 - 1)
                if t == TT - 1:
                    last.then_inc(down_done, 1)

            def first():
                pe.wait_ge(const_in, 16 * len(CONSTS))
                pe.wait_ge(w_lo_done, 4)
                turn_x1(0, 0)
                lora(0, 0)
                cond(0, 0)
                turn_hs(0, 0)

            def body(j, par, has_prev, has_next):
                route(j, par)
                if has_next:
                    turn_x1(*after(j, par))
                gate_up(j, par, 0)
                if has_next:
                    lora(*after(j, par))
                if has_prev:
                    down(*before(j, par), 0)
                if has_next:
                    cond(*after(j, par))
                if has_prev:
                    down(*before(j, par), 1)
                if has_next:
                    turn_hs(*after(j, par))
                gate_up(j, par, 1)

            def last():
                for t in range(TT):
                    down(PAIRS - 1, 1, t)

            rolled(pe, first, body, last)


CAP = 2 * S // E1
GROUPS = B * E1 // P
GB = B // GROUPS
GQ = P // CAP
SLOT_COLS = GROUPS * CAP
TILES = GROUPS * GB // GQ


def topk_phase(nc, sem, scores, first_row, ident_in, slot_row, slot_weight):
    with ExitStack() as ctx:
        def sb(name, shape, dt=F32):
            return ctx.enter_context(nc.sbuf_tensor(name, shape, dt))

        ident = sb("tk_ident", [P, P])
        row0 = sb("row0", [P, GROUPS])
        work = sb("work", [P, GROUPS, S])
        vals = sb("vals", [P, GROUPS, CAP])
        at = sb("at", [P, GROUPS, CAP], U32)
        rows = sb("rows", [P, GROUPS, CAP])
        rows_t = sb("rows_t", [P, GROUPS, CAP])
        by_expert = [ctx.enter_context(nc.psum_tensor(f"by_expert{n}", [P, 2, S], F32)) for n in range(GROUPS // 2)]

        const_in = sem("tk_const_in")
        turned_done = sem("tk_turned_done")
        work_set = sem("work_set")
        best_done = sem("best_done")
        at_done = sem("at_done")
        replaced = sem("replaced")
        rows_done = sem("rows_done")
        slots_set = sem("slots_set")
        ROUNDS = CAP // 8

        block = ctx.enter_context(nc.Block())

        @block.sync
        def _(sp):
            sp.dma_start(ident[:], ident_in).then_inc(const_in, 16)
            sp.dma_start(row0[:], first_row).then_inc(const_in, 16)

        @block.tensor
        def _(pe):
            pe.wait_ge(const_in, 32)
            for g in range(GROUPS):
                for t in range(TT):
                    last = nc.tensor.transpose(by_expert[g // 2][:, g % 2, t * P:(t + 1) * P], scores[:, t, g * P:(g + 1) * P], ident[:])
                last.then_inc(turned_done, 1)

        @block.scalar
        def _(act):
            act.wait_ge(turned_done, GROUPS)
            for n in range(GROUPS // 2):
                nc.scalar.activation(work[:, 2 * n:2 * n + 2, :], by_expert[n][:], ACT.Copy).then_inc(work_set, 1)

        @block.vector
        def _(dve):
            dve.wait_ge(const_in, 32)
            dve.wait_ge(work_set, GROUPS // 2)
            for r in range(ROUNDS):
                eight = slice(8 * r, 8 * r + 8)
                for g in range(GROUPS):
                    until(dve, replaced, GROUPS * (r - 1) + g + 1)
                    nc.vector.max(vals[:, g, eight], work[:, g, :]).then_inc(best_done, 1)
                for g in range(GROUPS):
                    dve.wait_ge(best_done, GROUPS * r + g + 1)
                    nc.vector.max_index(at[:, g, eight], vals[:, g, eight], work[:, g, :]).then_inc(at_done, 1)
                if r < ROUNDS - 1:
                    for g in range(GROUPS):
                        dve.wait_ge(at_done, GROUPS * r + g + 1)
                        nc.vector.match_replace(work[:, g, :], vals[:, g, eight], work[:, g, :], -1.0).then_inc(replaced, 1)
            dve.wait_ge(at_done, GROUPS * ROUNDS)
            nc.vector.tensor_tensor(rows[:], at[:], row0[:].unsqueeze(2).broadcast_to([P, GROUPS, CAP]), ALU.add).then_inc(rows_done, 1)
            dve.wait_ge(rows_done, 1)
            for g in range(GROUPS):
                nc.vector.transpose(rows_t[:, g, :], rows[:, g, :]).then_inc(rows_done, 1)
            for g in range(GROUPS):
                nc.vector.transpose(slot_weight[:, g, :], vals[:, g, :]).then_inc(slots_set, 1)
            dve.wait_ge(rows_done, GROUPS + 1)
            nc.vector.tensor_copy(slot_row[:], rows_t[:]).then_inc(slots_set, 1)
            dve.wait_ge(slots_set, GROUPS + 1)


def experts_phase(nc, sem, hs_rows, slot_row, slot_weight, w_gu, w_dn, ident_in, out_rows):
    GU = 2 * KT * H1
    DN = HT1 * D
    CT = TILES // 2
    CN = CT * P
    with ExitStack() as ctx:
        def sb(name, shape, dt=F32):
            return ctx.enter_context(nc.sbuf_tensor(name, shape, dt))

        def bank(name, shape):
            return ctx.enter_context(nc.psum_tensor(name, shape, F32))

        ident = sb("ex_ident", [P, P])
        gu_raw = sb("gu_raw", [P, GU])
        dn_raw = sb("ex_dn_raw", [P, DN])
        gu_hi = [sb(f"gu_hi{p}", [P, GU], F32R) for p in range(2)]
        gu_lo = [sb(f"gu_lo{p}", [P, GU], F32R) for p in range(2)]
        dn_hi = [sb(f"ex_dn_hi{p}", [P, DN], F32R) for p in range(2)]
        dn_lo = [sb(f"ex_dn_lo{p}", [P, DN], F32R) for p in range(2)]
        row_now = [sb(f"row_now{p}", [P, TILES], U32) for p in range(2)]
        weight_now = [sb(f"weight_now{p}", [P, TILES]) for p in range(2)]
        toks = [sb(f"toks{c}", [P, CT, D]) for c in range(2)]
        xt_hi = [sb(f"ex_xt_hi{c}", [P, KT, CN], F32R) for c in range(2)]
        xt_lo = [sb(f"ex_xt_lo{c}", [P, KT, CN], F32R) for c in range(2)]
        gelu = [sb(f"gelu{q}", [P, CN]) for q in range(2)]
        hid = [sb(f"ex_hid{q}", [P, CN]) for q in range(2)]
        hid_hi = sb("ex_hid_hi", [P, HT1, CN], F32R)
        hid_lo = sb("ex_hid_lo", [P, HT1, CN], F32R)
        eo = [sb(f"eo{c}", [P, CT, D]) for c in range(2)]
        turned = [bank(f"ex_turned{k}", [P, CN]) for k in range(KT)]
        gate_ps = [bank(f"ex_gate_ps{q}", [P, CN]) for q in range(2)]
        up_ps = [bank(f"ex_up_ps{q}", [P, CN]) for q in range(2)]
        down_ps = [bank(f"ex_down_ps{n}", [P, 2, D]) for n in range(2)]

        const_in = sem("ex_const_in")
        gu_in = sem("ex_gu_in")
        dn_in = sem("ex_dn_in")
        gu_hi_done = sem("ex_gu_hi_done")
        gu_lo_done = sem("ex_gu_lo_done")
        dn_hi_done = sem("ex_dn_hi_done")
        dn_lo_done = sem("ex_dn_lo_done")
        rows_set = sem("ex_rows_set")
        weights_set = sem("ex_weights_set")
        toks_in = [sem(f"ex_toks_in{c}") for c in range(2)]
        xt_done = sem("ex_xt_done")
        xt_hi_done = sem("ex_xt_hi_done")
        xt_lo_done = sem("ex_xt_lo_done")
        gate_up_done = sem("ex_gate_up_done")
        gelu_done = sem("ex_gelu_done")
        hid_done = sem("ex_hid_done")
        hid_hi_done = sem("ex_hid_hi_done")
        hid_lo_done = sem("ex_hid_lo_done")
        down_done = sem("ex_down_done")
        eo_done = sem("ex_eo_done")
        added = [sem(f"ex_added{c}") for c in range(2)]

        EPAIRS = E1 // 2

        def chunk_after(j, par, c):
            return (j, par, 1) if c == 0 else (j, 1, 0) if par == 0 else (j + 1, 0, 0)

        def expert_after(j, par):
            return (j, 1) if par == 0 else (j + 1, 0)

        def by_expert(engine, first, body, last):
            first()
            body(0, 0, False, True)
            body(0, 1, True, True)
            with engine.Fori(1, EPAIRS - 1) as j:
                body(j, 0, True, True)
                body(j, 1, True, True)
            body(EPAIRS - 1, 0, True, True)
            body(EPAIRS - 1, 1, True, False)
            last()

        block = ctx.enter_context(nc.Block())

        @block.sync
        def _(sp):
            sp.dma_start(ident[:], ident_in).then_inc(const_in, 16)

            def load(e):
                until(sp, gu_hi_done, e)
                until(sp, gu_lo_done, e)
                sp.dma_start(gu_raw[:], w_gu[bass.ds(e, 1)].rearrange("e p n -> (e p) n")).then_inc(gu_in, 16)
                until(sp, dn_hi_done, e)
                until(sp, dn_lo_done, e)
                sp.dma_start(dn_raw[:], w_dn[bass.ds(e, 1)].rearrange("e p n -> (e p) n")).then_inc(dn_in, 16)

            load(0)
            with sp.Fori(1, E1) as e:
                load(e)

        @block.gpsimd
        def _(pool):
            def gather(j, par, c):
                e = 2 * j + par
                pool.wait_ge(rows_set, e + 1)
                until(pool, xt_done, 2 * (2 * e + c) - 2)
                alone(pool)
                for n in range(CT):
                    at = row_now[par][:, CT * c + n:CT * c + n + 1]
                    nc.gpsimd.indirect_dma_start(out=toks[c][:, n, :], out_offset=None, in_=hs_rows,
                                                 in_offset=bass.IndirectOffsetOnAxis(ap=at, axis=0)).then_inc(toks_in[c], 16)

            def add(j, par, c):
                e = 2 * j + par
                pool.wait_ge(eo_done, CT * (2 * e + c) + CT)
                until(pool, added[c], 16 * CT * e)
                alone(pool)
                for n in range(CT):
                    at = row_now[par][:, CT * c + n:CT * c + n + 1]
                    nc.gpsimd.indirect_dma_start(out=out_rows, out_offset=bass.IndirectOffsetOnAxis(ap=at, axis=0),
                                                 in_=eo[c][:, n, :], in_offset=None, compute_op=ALU.add).then_inc(added[c], 16)

            def first():
                gather(0, 0, 0)
                gather(0, 0, 1)

            def body(j, par, has_prev, has_next):
                if has_prev:
                    add(*before(j, par), 1)
                if has_next:
                    gather(*expert_after(j, par), 0)
                add(j, par, 0)
                if has_next:
                    gather(*expert_after(j, par), 1)

            by_expert(pool, first, body, lambda: add(EPAIRS - 1, 1, 1))
            for c in range(2):
                pool.wait_ge(added[c], 16 * CT * E1)

        @block.scalar
        def _(act):
            def gu_high(j, par):
                e = 2 * j + par
                act.wait_ge(gu_in, 16 * e + 16)
                until(act, gate_up_done, 8 * e - 8)
                nc.scalar.activation(gu_hi[par][:], gu_raw[:], ACT.Copy).then_inc(gu_hi_done, 1)

            def dn_high(j, par):
                e = 2 * j + par
                act.wait_ge(dn_in, 16 * e + 16)
                until(act, down_done, 4 * e - 4)
                nc.scalar.activation(dn_hi[par][:], dn_raw[:], ACT.Copy).then_inc(dn_hi_done, 1)

            def xt_high(j, par, c):
                n = 2 * (2 * j + par) + c
                until(act, gate_up_done, 4 * n - 4)
                for k in range(KT):
                    act.wait_ge(xt_done, 2 * n + k + 1)
                    nc.scalar.activation(xt_hi[c][:, k, :], turned[k][:], ACT.Copy).then_inc(xt_hi_done, 1)

            def gelus(j, par, c, f):
                n = 2 * (2 * j + par) + c
                act.wait_ge(gate_up_done, 4 * n + f + 1)
                until(act, hid_done, 4 * n + f - 1)
                nc.scalar.activation(gelu[f % 2][:], gate_ps[f % 2][:], ACT.Gelu).then_inc(gelu_done, 1)

            def hid_high(j, par, c, f):
                n = 2 * (2 * j + par) + c
                act.wait_ge(hid_done, 4 * n + f + 1)
                until(act, down_done, 2 * n)
                nc.scalar.activation(hid_hi[:, f, :], hid[f % 2][:], ACT.Copy).then_inc(hid_hi_done, 1)

            def weigh(j, par, c):
                e = 2 * j + par
                n = 2 * e + c
                act.wait_ge(weights_set, e + 1)
                until(act, added[c], 16 * CT * e)
                for m in range(CT):
                    act.wait_ge(down_done, 2 * n + m // 2 + 1)
                    nc.scalar.activation(eo[c][:, m, :], down_ps[m // 2][:, m % 2, :], ACT.Copy,
                                         scale=weight_now[par][:, CT * c + m:CT * c + m + 1]).then_inc(eo_done, 1)

            def first():
                gu_high(0, 0)
                xt_high(0, 0, 0)
                dn_high(0, 0)

            def body(j, par, has_prev, has_next):
                for c in range(2):
                    gelus(j, par, c, 0)
                    gelus(j, par, c, 1)
                    if c == 1:
                        weigh(j, par, 0)
                    elif has_prev:
                        weigh(*before(j, par), 1)
                    hid_high(j, par, c, 0)
                    gelus(j, par, c, 2)
                    if c == 0 and has_next:
                        gu_high(*expert_after(j, par))
                    hid_high(j, par, c, 1)
                    gelus(j, par, c, 3)
                    if c == 0 or has_next:
                        xt_high(*chunk_after(j, par, c))
                    hid_high(j, par, c, 2)
                    hid_high(j, par, c, 3)
                    if c == 0 and has_next:
                        dn_high(*expert_after(j, par))

            by_expert(act, first, body, lambda: weigh(EPAIRS - 1, 1, 1))

        @block.vector
        def _(dve):
            def slots(j, par):
                e = 2 * j + par
                for c in range(2):
                    until(dve, added[c], 16 * CT * (e - 1))
                rows = slot_row.rearrange("p g (b e) -> p (g b) e", b=GB // GQ)[:, :, bass.ds(e, 1)]
                nc.vector.tensor_copy(row_now[par][:].unsqueeze(2), rows).then_inc(rows_set, 1)
                until(dve, eo_done, 2 * CT * (e - 1))
                weights = slot_weight.rearrange("p g (b e) -> p (g b) e", b=GB // GQ)[:, :, bass.ds(e, 1)]
                nc.vector.tensor_copy(weight_now[par][:].unsqueeze(2), weights).then_inc(weights_set, 1)

            def gu_low(j, par):
                e = 2 * j + par
                dve.wait_ge(gu_hi_done, e + 1)
                nc.vector.tensor_tensor(gu_lo[par][:], gu_raw[:], gu_hi[par][:].bitcast(F32), ALU.subtract).then_inc(gu_lo_done, 1)

            def dn_low(j, par):
                e = 2 * j + par
                dve.wait_ge(dn_hi_done, e + 1)
                nc.vector.tensor_tensor(dn_lo[par][:], dn_raw[:], dn_hi[par][:].bitcast(F32), ALU.subtract).then_inc(dn_lo_done, 1)

            def xt_low(j, par, c):
                n = 2 * (2 * j + par) + c
                for k in range(KT):
                    dve.wait_ge(xt_hi_done, 2 * n + k + 1)
                    nc.vector.tensor_tensor(xt_lo[c][:, k, :], turned[k][:], xt_hi[c][:, k, :].bitcast(F32), ALU.subtract).then_inc(xt_lo_done, 1)

            def hidden(j, par, c, f):
                n = 2 * (2 * j + par) + c
                dve.wait_ge(gelu_done, 4 * n + f + 1)
                until(dve, hid_lo_done, 4 * n + f - 1)
                nc.vector.tensor_tensor(hid[f % 2][:], up_ps[f % 2][:], gelu[f % 2][:], ALU.mult).then_inc(hid_done, 1)

            def hid_low(j, par, c, f):
                n = 2 * (2 * j + par) + c
                dve.wait_ge(hid_hi_done, 4 * n + f + 1)
                nc.vector.tensor_tensor(hid_lo[:, f, :], hid[f % 2][:], hid_hi[:, f, :].bitcast(F32), ALU.subtract).then_inc(hid_lo_done, 1)

            def first():
                slots(0, 0)
                gu_low(0, 0)
                xt_low(0, 0, 0)
                dn_low(0, 0)

            def body(j, par, has_prev, has_next):
                for c in range(2):
                    hidden(j, par, c, 0)
                    hidden(j, par, c, 1)
                    hid_low(j, par, c, 0)
                    hidden(j, par, c, 2)
                    if c == 0 and has_next:
                        slots(*expert_after(j, par))
                        gu_low(*expert_after(j, par))
                    hid_low(j, par, c, 1)
                    hidden(j, par, c, 3)
                    if c == 0 or has_next:
                        xt_low(*chunk_after(j, par, c))
                    hid_low(j, par, c, 2)
                    hid_low(j, par, c, 3)
                    if c == 0 and has_next:
                        dn_low(*expert_after(j, par))

            by_expert(dve, first, body, lambda: None)

        @block.tensor
        def _(pe):
            def turn(j, par, c):
                e = 2 * j + par
                n = 2 * e + c
                pe.wait_ge(toks_in[c], 16 * CT * e + 16 * CT)
                until(pe, xt_lo_done, 2 * n)
                for k in range(KT):
                    for m in range(CT):
                        last = nc.tensor.transpose(turned[k][:, m * P:(m + 1) * P], toks[c][:, m, k * P:(k + 1) * P], ident[:])
                    last.then_inc(xt_done, 1)

            def gate_up(j, par, c, f):
                e = 2 * j + par
                n = 2 * e + c
                if f == 0:
                    pe.wait_ge(gu_lo_done, e + 1)
                    pe.wait_ge(xt_lo_done, 2 * n + 2)
                until(pe, hid_done, 4 * n + f - 1)
                hi = gu_hi[par][:].rearrange("p (g k h) -> p g k h", g=2, k=KT)
                lo = gu_lo[par][:].rearrange("p (g k h) -> p g k h", g=2, k=KT)
                cols = slice(f * P, (f + 1) * P)
                for g, ps in ((0, gate_ps[f % 2]), (1, up_ps[f % 2])):
                    for k in range(KT):
                        last = exact_product(nc, ps[:], (hi[:, g, k, cols], lo[:, g, k, cols]),
                                             (xt_hi[c][:, k, :], xt_lo[c][:, k, :]), k == 0, k == KT - 1)
                last.then_inc(gate_up_done, 1)

            def down(j, par, c):
                e = 2 * j + par
                n = 2 * e + c
                pe.wait_ge(dn_lo_done, e + 1)
                pe.wait_ge(hid_lo_done, 4 * n + 4)
                hi = dn_hi[par][:].rearrange("p (h d) -> p h d", h=HT1)
                lo = dn_lo[par][:].rearrange("p (h d) -> p h d", h=HT1)
                for m in range(CT):
                    if m % 2 == 0:
                        until(pe, eo_done, CT * (n - 1) + m + 2)
                    cols = slice(m * P, (m + 1) * P)
                    for f in range(HT1):
                        last = exact_product(nc, down_ps[m // 2][:, m % 2, :], (hid_hi[:, f, cols], hid_lo[:, f, cols]),
                                             (hi[:, f, :], lo[:, f, :]), f == 0, f == HT1 - 1)
                    if m % 2:
                        last.then_inc(down_done, 1)

            def first():
                pe.wait_ge(const_in, 16)
                turn(0, 0, 0)

            def body(j, par, has_prev, has_next):
                for c in range(2):
                    gate_up(j, par, c, 0)
                    gate_up(j, par, c, 1)
                    if c == 1:
                        down(j, par, 0)
                    elif has_prev:
                        down(*before(j, par), 1)
                    gate_up(j, par, c, 2)
                    if c == 0 or has_next:
                        turn(*chunk_after(j, par, c))
                    gate_up(j, par, c, 3)

            by_expert(pe, first, body, lambda: down(EPAIRS - 1, 1, 1))


def block_program(nc, t):
    with ExitStack() as ctx:
        def sem(name):
            return ctx.enter_context(nc.semaphore(name))

        def scratch(name, shape, dt=F32):
            return nc.dram_tensor(name, shape, dt).ap()

        expert_dram = scratch("expert_dram", [B, 1], U32)
        c0 = scratch("c0", [B, P, TT, D])
        h = scratch("h", [B, P, TT, D])
        x1 = scratch("x1", [B, P, TT, D])
        hs = scratch("hs", [B, S, D])
        rows = "b s d -> (b s) d"

        cond_ffn_phase(nc, sem, t["x_t"], t["w_ug"], t["w_dn"], t["cond"], expert_dram, c0)
        attention_phase(nc, sem, c0, t["attn_norm_w"], t["w_qkv"], t["w_o"], t["ident"], t["causal"], h)
        moe_phase(nc, sem, h, t["x"], t["ffn_norm_w"], t["moe_gate_w"], t["moe_w"], t["ident"], t["expert_iota"], x1)
        scores = ctx.enter_context(nc.sbuf_tensor("route_scores", [P, TT, B * E1], F32))
        slot_row = ctx.enter_context(nc.sbuf_tensor("slot_row", [P, GROUPS, CAP], U32))
        slot_weight = ctx.enter_context(nc.sbuf_tensor("slot_weight", [P, GROUPS, CAP], F32))
        lora_shared_phase(nc, sem, x1, t["cond_er"], t["w_base"], t["b_base"], t["lora_a"], t["lora_b"], t["route_w"],
                          t["shared_gu"], t["shared_d"], t["ident"], hs, scores, t["out"])
        topk_phase(nc, sem, scores, t["first_row"], t["ident"], slot_row, slot_weight)
        experts_phase(nc, sem, hs.rearrange(rows), slot_row, slot_weight, t["expert_gu"], t["expert_d"], t["ident"],
                      t["out"].rearrange(rows))


def lay_out(inputs):
    import numpy as np
    a = {n: np.asarray(v) for n, v in inputs.items()}

    def by_rows(w):
        w = np.swapaxes(w, -1, -2)
        w = w.reshape(w.shape[:-2] + (w.shape[-2] // P, P, w.shape[-1]))
        return np.swapaxes(w, -3, -2).reshape(w.shape[:-3] + (P, -1))

    def to_all(v):
        return np.broadcast_to(v, (P,) + v.shape)

    def by_slice(b):
        return b.reshape(E0, HT0, P).transpose(0, 2, 1)

    x = a["x"]
    L0, F0, C1, F1 = "L0_cond_", "L0_ffn_", "L1_cond_", "L1_ffn_"
    eye = np.eye(P, dtype=np.float32)
    later = np.arange(P)[None, :] > np.arange(P)[:, None]
    d = {
        "x_t": x.reshape(B, S, KT, P).transpose(0, 3, 2, 1),
        "x": x.reshape(B, TT, P, D).transpose(0, 2, 1, 3),
        "w_ug": np.concatenate([by_rows(a[L0 + "W_up"]), by_rows(a[L0 + "W_gate"]),
                                by_slice(a[L0 + "b_up"]), by_slice(a[L0 + "b_gate"])], 2),
        "w_dn": np.concatenate([by_rows(a[L0 + "W_down"]), np.broadcast_to(a[L0 + "b_down"][:, None], (E0, P, D))], 2),
        "cond": a["cond_8"],
        "attn_norm_w": to_all(a[F0 + "attn_norm_w"]),
        "ffn_norm_w": to_all(a[F0 + "ffn_norm_w"]),
        "w_qkv": by_rows(np.concatenate([a[F0 + "wq"], a[F0 + "wk"], a[F0 + "wv"]], 0)).reshape(P, KT, QKV),
        "w_o": by_rows(a[F0 + "wo"]).reshape(P, KT, D),
        "moe_gate_w": by_rows(a[F0 + "gate_w"]).reshape(P, KT, EM),
        "moe_w": by_rows(a[F0 + "expert_w"].reshape(EM * D, D)).reshape(P, KT, EM * D),
        "cond_er": np.repeat(a["cond_8"].T, ER // E0, axis=0),
        "w_base": by_rows(a[C1 + "W_base"]).reshape(P, KT, D),
        "b_base": to_all(a[C1 + "b_base"]),
        "lora_a": a[C1 + "As"].reshape(ER, D),
        "lora_b": a[C1 + "Bs"].transpose(0, 2, 1).reshape(ER, D),
        "route_w": by_rows(a[F1 + "gate_w"]).reshape(P, KT, E1),
        "shared_gu": np.concatenate([by_rows(a[F1 + "Ws_g"]), by_rows(a[F1 + "Ws_u"])], 1),
        "shared_d": by_rows(a[F1 + "Ws_d"]),
        "expert_gu": np.concatenate([by_rows(a[F1 + "Wg"]), by_rows(a[F1 + "Wu"])], 2),
        "expert_d": by_rows(a[F1 + "Wd"]),
        "ident": eye,
        "causal": np.where(later, MASKED, 0.0).astype(np.float32),
        "expert_iota": to_all(np.arange(EM, dtype=np.float32)),
        "first_row": np.repeat(S * np.arange(B, dtype=np.float32).reshape(GROUPS, GB).T, E1, axis=0),
    }
    return {n: np.ascontiguousarray(v) for n, v in d.items()}


def kernel(**inputs):
    import concourse.bacc as _bacc
    from concourse import mybir as _mybir
    from concourse.bass_utils import run_bass_kernel_spmd as _run

    nc = _bacc.Bacc("TRN2", target_bir_lowering=False, num_devices=1)
    arrays, t = {}, {}
    for name, a in lay_out(inputs).items():
        arrays[f"in_{name}"] = a
        t[name] = nc.dram_tensor(f"in_{name}", a.shape, _mybir.dt.from_np(a.dtype), kind="ExternalInput").ap()
    t["out"] = nc.dram_tensor("out", [B, S, D], F32, kind="ExternalOutput").ap()
    block_program(nc, t)
    r = _run(nc, [arrays], core_ids=[0])
    return r.results[0]["out"]
```

```python
from contextlib import ExitStack

import concourse.bass as bass
from concourse import mybir

F32 = mybir.dt.float32
F32R = mybir.dt.float32r
BF16 = mybir.dt.bfloat16
U32 = mybir.dt.uint32
ALU = mybir.AluOpType
ACT = mybir.ActivationFunctionType
AX_X = mybir.AxisListType.X

P = 128
B, S, D = 32, 256, 256
TT = S // P
KT = D // P
PAIRS = B // 2
E0, H0 = 8, 512
HT0 = H0 // P


def until(engine, semaphore, value):
    if not (isinstance(value, int) and value <= 0):
        engine.wait_ge(semaphore, value)


def after(j, par):
    return (j, 1) if par == 0 else (j + 1, 0)


def before(j, par):
    return (j, 0) if par == 1 else (j - 1, 1)


def rolled(engine, first, body, last):
    first()
    body(0, 0, False, True)
    body(0, 1, True, True)
    with engine.Fori(1, PAIRS - 1) as j:
        body(j, 0, True, True)
        body(j, 1, True, True)
    body(PAIRS - 1, 0, True, True)
    body(PAIRS - 1, 1, True, False)
    last()


def alone(engine):
    engine.nop(nofuse=True)


def exact_product(nc, out, lhs, rhs, start, stop):
    (lhs_hi, lhs_lo), (rhs_hi, rhs_lo) = lhs, rhs
    nc.tensor.matmul(out, lhs_hi, rhs_lo, start=start, stop=False)
    nc.tensor.matmul(out, lhs_lo, rhs_hi, start=False, stop=False)
    return nc.tensor.matmul(out, lhs_hi, rhs_hi, start=False, stop=stop)


def cond_ffn_phase(nc, sem, x_t, w_ug, w_dn, cond, expert_dram, c0):
    UG = 2 * KT * H0
    DN = HT0 * D
    with ExitStack() as ctx:
        def sb(name, shape, dt=F32):
            return ctx.enter_context(nc.sbuf_tensor(name, shape, dt))

        cond_sb = sb("cond_sb", [B, E0])
        cond_top = sb("cond_top", [B, 8])
        cond_arg = sb("cond_arg", [B, 8], U32)
        expert_row = sb("expert_row", [1, B], U32)
        ug_raw = [sb(f"ug_raw{p}", [P, UG + 2 * HT0]) for p in range(2)]
        dn_raw = [sb(f"dn_raw{p}", [P, DN + D]) for p in range(2)]
        x_raw = [sb(f"x_raw{p}", [P, KT, S]) for p in range(2)]
        ug_bias = [sb(f"ug_bias{p}", [P, 2 * HT0]) for p in range(2)]
        dn_bias = [sb(f"dn_bias{p}", [P, D]) for p in range(2)]
        ug_hi = [sb(f"ug_hi{p}", [P, UG], F32R) for p in range(2)]
        ug_lo = [sb(f"ug_lo{p}", [P, UG], F32R) for p in range(2)]
        dn_hi = [sb(f"dn_hi{p}", [P, DN], F32R) for p in range(2)]
        dn_lo = [sb(f"dn_lo{p}", [P, DN], F32R) for p in range(2)]
        x_hi = [sb(f"x_hi{p}", [P, KT, S], F32R) for p in range(2)]
        x_lo = [sb(f"x_lo{p}", [P, KT, S], F32R) for p in range(2)]
        act_up = [sb(f"act_up{p}", [P, HT0, S]) for p in range(2)]
        hid = [sb(f"hid{p}", [P, HT0, S]) for p in range(2)]
        hid_hi = [sb(f"hid_hi{p}", [P, HT0, S], F32R) for p in range(2)]
        hid_lo = [sb(f"hid_lo{p}", [P, HT0, S], F32R) for p in range(2)]
        c0_sb = [sb(f"c0_sb{p}", [P, TT, D]) for p in range(2)]
        ps_up = [ctx.enter_context(nc.psum_tensor(f"ps_up{q}", [P, 2, S], F32)) for q in range(2)]
        ps_gate = [ctx.enter_context(nc.psum_tensor(f"ps_gate{q}", [P, 2, S], F32)) for q in range(2)]
        ps_down = [ctx.enter_context(nc.psum_tensor(f"ps_down{q}", [P, TT, D], F32)) for q in range(2)]

        cond_in = sem("cond_in")
        cond_max = sem("cond_max")
        expert_out = sem("expert_out")
        expert_in = sem("expert_in")
        ug_in = [sem(f"ug_in{p}") for p in range(2)]
        dn_in = [sem(f"dn_in{p}") for p in range(2)]
        ug_hi_done = sem("ug_hi_done")
        ug_lo_done = sem("ug_lo_done")
        x_lo_done = sem("x_lo_done")
        dn_hi_done = sem("dn_hi_done")
        dn_lo_done = sem("dn_lo_done")
        up_gate_done = sem("up_gate_done")
        silu_done = sem("silu_done")
        hid_done = sem("hid_done")
        hid_hi_done = sem("hid_hi_done")
        hid_lo_done = sem("hid_lo_done")
        down_done = sem("down_done")
        c0_done = sem("c0_done")
        c0_out = [sem(f"c0_out{p}") for p in range(2)]

        block = ctx.enter_context(nc.Block())

        @block.sync
        def _(sp):
            sp.dma_start(cond_sb[:], cond).then_inc(cond_in, 16)
            sp.wait_ge(cond_max, 2)
            sp.dma_start(expert_dram, cond_arg[:, 0:1]).then_inc(expert_out, 16)
            sp.wait_ge(expert_out, 16)
            sp.dma_start(expert_row[:], expert_dram.rearrange("b a -> a b")).then_inc(expert_in, 16)
            sp.wait_ge(expert_in, 16)

            def picked(i):
                return sp.value_load(expert_row[0:1, bass.ds(i, 1)], min_val=0, max_val=E0 - 1)

            def load_up_gate(j, par):
                i = 2 * j + par
                e = picked(i)
                until(sp, ug_hi_done, 3 * i - 3)
                alone(sp)
                until(sp, ug_lo_done, i - 1)
                alone(sp)
                sp.dma_start(ug_raw[par][:], w_ug[bass.ds(e, 1)].rearrange("e p n -> (e p) n")).then_inc(ug_in[par], 16)
                until(sp, x_lo_done, i - 1)
                sp.dma_start(x_raw[par][:], x_t[bass.ds(i, 1)].rearrange("b p k s -> (b p) k s")).then_inc(ug_in[par], 16)

            def load_down(j, par):
                i = 2 * j + par
                e = picked(i)
                until(sp, dn_hi_done, 2 * i - 2)
                alone(sp)
                until(sp, dn_lo_done, i - 1)
                sp.dma_start(dn_raw[par][:], w_dn[bass.ds(e, 1)].rearrange("e p n -> (e p) n")).then_inc(dn_in[par], 16)

            load_up_gate(0, 0)
            load_up_gate(0, 1)
            load_down(0, 0)
            load_up_gate(1, 0)
            load_down(0, 1)
            load_up_gate(1, 1)
            load_down(1, 0)
            with sp.Fori(2, PAIRS) as j:
                load_up_gate(j, 0)
                load_down(j - 1, 1)
                load_up_gate(j, 1)
                load_down(j, 0)
            load_down(PAIRS - 1, 1)

        @block.scalar
        def _(act):
            def split(j, par):
                i = 2 * j + par
                act.wait_ge(ug_in[par], 32 * j + 32)
                until(act, up_gate_done, 2 * i - 2)
                nc.scalar.activation(x_hi[par][:], x_raw[par][:], ACT.Copy).then_inc(ug_hi_done, 1)
                nc.scalar.activation(ug_hi[par][:], ug_raw[par][:, 0:UG], ACT.Copy).then_inc(ug_hi_done, 1)
                until(act, silu_done, 4 * i - 4)
                until(act, hid_done, 4 * i - 4)
                nc.scalar.activation(ug_bias[par][:], ug_raw[par][:, UG:UG + 2 * HT0], ACT.Copy).then_inc(ug_hi_done, 1)

            def silu(j, par, q):
                i = 2 * j + par
                act.wait_ge(ug_hi_done, 3 * i + 3)
                act.wait_ge(up_gate_done, 2 * i + q + 1)
                until(act, hid_done, 4 * i - 4)
                for m in range(2):
                    t = 2 * q + m
                    nc.scalar.activation(act_up[par][:, t, :], ps_up[q][:, m, :], ACT.Silu,
                                         bias=ug_bias[par][:, t:t + 1]).then_inc(silu_done, 1)

            def hid_high(j, par, q):
                i = 2 * j + par
                act.wait_ge(hid_done, 4 * i + 2 * q + 2)
                until(act, down_done, i - 1)
                nc.scalar.activation(hid_hi[par][:, 2 * q:2 * q + 2, :], hid[par][:, 2 * q:2 * q + 2, :], ACT.Copy).then_inc(hid_hi_done, 1)

            def dn_high(j, par):
                i = 2 * j + par
                act.wait_ge(dn_in[par], 16 * j + 16)
                until(act, down_done, i - 1)
                until(act, c0_done, i - 1)
                nc.scalar.activation(dn_hi[par][:], dn_raw[par][:, 0:DN], ACT.Copy).then_inc(dn_hi_done, 1)
                nc.scalar.activation(dn_bias[par][:], dn_raw[par][:, DN:DN + D], ACT.Copy).then_inc(dn_hi_done, 1)

            def body(j, par, has_prev, has_next):
                if has_next:
                    split(*after(j, par))
                silu(j, par, 0)
                hid_high(j, par, 0)
                dn_high(j, par)
                silu(j, par, 1)
                hid_high(j, par, 1)

            rolled(act, lambda: split(0, 0), body, lambda: None)

        @block.gpsimd
        def _(pool):
            def store(j, par):
                i = 2 * j + par
                pool.wait_ge(c0_done, i + 1)
                pool.dma_start(c0[bass.ds(i, 1)].rearrange("b p t d -> (b p) t d"), c0_sb[par][:]).then_inc(c0_out[par], 16)

            def x_low(j, par):
                i = 2 * j + par
                pool.wait_ge(ug_hi_done, 3 * i + 1)
                until(pool, up_gate_done, 2 * i - 2)
                nc.gpsimd.tensor_tensor(x_lo[par][:], x_raw[par][:], x_hi[par][:].bitcast(F32), ALU.subtract).then_inc(x_lo_done, 1)

            def dn_low(j, par):
                i = 2 * j + par
                pool.wait_ge(dn_hi_done, 2 * i + 1)
                until(pool, down_done, i - 1)
                nc.gpsimd.tensor_tensor(dn_lo[par][:], dn_raw[par][:, 0:DN], dn_hi[par][:].bitcast(F32), ALU.subtract).then_inc(dn_lo_done, 1)

            def body(j, par, has_prev, has_next):
                if has_next:
                    x_low(*after(j, par))
                dn_low(j, par)
                if has_prev:
                    store(*before(j, par))

            rolled(pool, lambda: x_low(0, 0), body, lambda: store(PAIRS - 1, 1))
            for p in range(2):
                pool.wait_ge(c0_out[p], 16 * PAIRS)

        @block.vector
        def _(dve):
            dve.wait_ge(cond_in, 16)
            nc.vector.max(cond_top[:], cond_sb[:]).then_inc(cond_max, 1)
            dve.wait_ge(cond_max, 1)
            nc.vector.max_index(cond_arg[:], cond_top[:], cond_sb[:]).then_inc(cond_max, 1)

            def split(j, par):
                i = 2 * j + par
                dve.wait_ge(ug_hi_done, 3 * i + 2)
                until(dve, up_gate_done, 2 * i - 2)
                nc.vector.tensor_tensor(ug_lo[par][:], ug_raw[par][:, 0:UG], ug_hi[par][:].bitcast(F32), ALU.subtract).then_inc(ug_lo_done, 1)

            def hidden(j, par, q):
                i = 2 * j + par
                until(dve, hid_lo_done, 2 * i - 2 + q)
                until(dve, hid_hi_done, 2 * i - 2 + q)
                dve.wait_ge(silu_done, 4 * i + 2 * q + 2)
                for m in range(2):
                    t = 2 * q + m
                    nc.vector.scalar_tensor_tensor(out=hid[par][:, t, :], in0=ps_gate[q][:, m, :],
                                                   scalar=ug_bias[par][:, HT0 + t:HT0 + t + 1], in1=act_up[par][:, t, :],
                                                   op0=ALU.add, op1=ALU.mult).then_inc(hid_done, 1)

            def hid_low(j, par, q):
                i = 2 * j + par
                dve.wait_ge(hid_hi_done, 2 * i + q + 1)
                until(dve, down_done, i - 1)
                nc.vector.tensor_tensor(hid_lo[par][:, 2 * q:2 * q + 2, :], hid[par][:, 2 * q:2 * q + 2, :],
                                        hid_hi[par][:, 2 * q:2 * q + 2, :].bitcast(F32), ALU.subtract).then_inc(hid_lo_done, 1)

            def finish(j, par):
                i = 2 * j + par
                dve.wait_ge(down_done, i + 1)
                dve.wait_ge(dn_hi_done, 2 * i + 2)
                until(dve, c0_out[par], 16 * j)
                bias = dn_bias[par][:].unsqueeze(1).broadcast_to([P, TT, D])
                nc.vector.tensor_tensor(c0_sb[par][:], ps_down[par][:], bias, ALU.add).then_inc(c0_done, 1)

            def body(j, par, has_prev, has_next):
                hidden(j, par, 0)
                if has_next:
                    split(*after(j, par))
                hid_low(j, par, 0)
                hidden(j, par, 1)
                hid_low(j, par, 1)
                if has_prev:
                    finish(*before(j, par))

            rolled(dve, lambda: split(0, 0), body, lambda: finish(PAIRS - 1, 1))

        @block.tensor
        def _(pe):
            def up_gate(j, par):
                i = 2 * j + par
                pe.wait_ge(ug_hi_done, 3 * i + 2)
                pe.wait_ge(ug_lo_done, i + 1)
                pe.wait_ge(x_lo_done, i + 1)
                hi = ug_hi[par][:].rearrange("p (g k h) -> p g k h", g=2, k=KT)
                lo = ug_lo[par][:].rearrange("p (g k h) -> p g k h", g=2, k=KT)
                for q in range(2):
                    until(pe, hid_done, 4 * i - 2 + 2 * q)
                    until(pe, silu_done, 4 * i - 2 + 2 * q)
                    for g, ps in ((0, ps_up[q]), (1, ps_gate[q])):
                        for m in range(2):
                            cols = slice((2 * q + m) * P, (2 * q + m + 1) * P)
                            for k in range(KT):
                                last = exact_product(nc, ps[:, m, :], (hi[:, g, k, cols], lo[:, g, k, cols]),
                                                     (x_hi[par][:, k, :], x_lo[par][:, k, :]), k == 0, k == KT - 1)
                    last.then_inc(up_gate_done, 1)

            def down(j, par):
                i = 2 * j + par
                pe.wait_ge(dn_hi_done, 2 * i + 1)
                pe.wait_ge(dn_lo_done, i + 1)
                pe.wait_ge(hid_lo_done, 2 * i + 2)
                until(pe, c0_done, i - 1)
                hi = dn_hi[par][:].rearrange("p (h d) -> p h d", h=HT0)
                lo = dn_lo[par][:].rearrange("p (h d) -> p h d", h=HT0)
                for t in range(TT):
                    for h in range(HT0):
                        toks = slice(t * P, (t + 1) * P)
                        last = exact_product(nc, ps_down[par][:, t, :], (hid_hi[par][:, h, toks], hid_lo[par][:, h, toks]),
                                             (hi[:, h, :], lo[:, h, :]), h == 0, h == HT0 - 1)
                last.then_inc(down_done, 1)

            def body(j, par, has_prev, has_next):
                up_gate(j, par)
                if has_prev:
                    down(*before(j, par))

            rolled(pe, lambda: None, body, lambda: down(PAIRS - 1, 1))


NH, NKV, HD = 16, 4, 16
G = NH // NKV
QKV = NH * HD + 2 * NKV * HD
UNITS = 2 * NKV
EPS = 1e-6
MASKED = -1e30

PIECES = {"norm_t": (0, 0), "qkv_0": (0, 1), "out_q1": (1, 0), "qkv_1": (1, 1), "out_q0": (2, 0),
          "k_0": (2, 1), "out_t": (3, 0), "k_1": (3, 1), "q_1_a": (4, 0), "q_0_a": (4, 1),
          "q_1_b": (5, 0), "out_proj": (5, 1), "q_0_b": (6, 0)}
OUT_PIECES = [n for n in PIECES if n.startswith("out")]
PROJ_PIECES = [n for n in PIECES if not n.startswith("out")]


def attention_phase(nc, sem, c0, norm_w, w_qkv, w_o, ident_in, mask_in, h, later_weights):
    with ExitStack() as ctx:
        def sb(name, shape, dt=F32):
            return ctx.enter_context(nc.sbuf_tensor(name, shape, dt))

        def bank(name, shape):
            return ctx.enter_context(nc.psum_tensor(name, shape, F32))

        ident = sb("at_ident", [P, P])
        identb = sb("at_identb", [P, P], BF16)
        mask = sb("at_mask", [P, P])
        maskb = sb("maskb", [P, G, P], BF16)
        nw = sb("at_norm_w", [P, D])
        wqkv_raw = sb("wqkv_raw", [P, KT, QKV])
        wqkv_hi = sb("wqkv_hi", [P, KT, QKV], F32R)
        wqkv_lo = sb("wqkv_lo", [P, KT, QKV], F32R)
        wo_raw = sb("wo_raw", [P, KT, D])
        wo_hi = sb("wo_hi", [P, KT, D], F32R)
        wo_lo = sb("wo_lo", [P, KT, D], F32R)
        minus_half = sb("at_minus_half", [P, TT])

        c0n = [sb(f"c0n{p}", [P, TT, D]) for p in range(2)]
        c0r = [sb(f"c0r{p}", [P, TT, D]) for p in range(2)]
        squares = sb("squares", [P, D])
        ssq = sb("ssq", [P, TT])
        msq = sb("msq", [P, TT])
        rstd = sb("rstd", [P, TT])
        normed = sb("normed", [P, TT, D])
        nt_hi = sb("nt_hi", [P, KT, S], F32R)
        nt_lo = sb("nt_lo", [P, KT, S], F32R)
        q_parts = [sb(f"q_parts{t}", [P, NH, 4, HD], F32R) for t in range(TT)]
        k_parts = [sb(f"k_parts{t}", [P, NKV, 4, 2, HD], F32R) for t in range(TT)]
        q_t = [sb(f"q_t{p}", [P, NH // 2, S], F32R) for p in range(2)]
        k_t = [sb(f"k_t{p}", [P, NKV, S], F32R) for p in range(2)]
        VW = NKV * P
        VSTEP = P + 2 * HD
        v_parts = [sb(f"v_parts{p}", [P, TT, VW + VSTEP], F32R) for p in range(2)]
        neg_max = [sb(f"neg_max{q}", [P, G]) for q in range(2)]
        probs = [sb(f"probs{q}", [P, G, (q + 1) * P]) for q in range(2)]
        pt_hi = [sb(f"pt_hi{q}", [P, q + 1, G * P], F32R) for q in range(2)]
        pt_lo = [sb(f"pt_lo{q}", [P, q + 1, G * P], F32R) for q in range(2)]
        sums = [sb(f"sums{p}", [P, TT, NKV, G]) for p in range(2)]
        rinv = [sb(f"rinv{q}", [P, G, NKV]) for q in range(2)]
        ot_sb = [sb(f"ot_sb{q}", [P, G, P]) for q in range(2)]
        on = [sb(f"on{q}", [P, G, NKV, 2, HD]) for q in range(2)]
        o = sb("o", [P, TT, D])
        o_hi = sb("o_hi", [P, KT, S], F32R)
        o_lo = sb("o_lo", [P, KT, S], F32R)
        h_sb = [sb(f"h_sb{p}", [P, TT, D]) for p in range(2)]

        s_q1 = [bank(f"s_q1_{n}", [P, 2, S]) for n in range(2)]
        s_q0 = bank("s_q0", [P, G, P])
        pt = [bank(f"pt{n}", [P, G * P]) for n in range(2)]
        ot = [bank(f"ot{q}", [P, G * P]) for q in range(2)]
        shared = bank("shared", [P, 512])
        shared_k = shared[:].rearrange("p (k s) -> p k s", k=KT)

        const_in = sem("at_const_in")
        w_hi_done = sem("at_w_hi_done")
        w_lo_done = sem("at_w_lo_done")
        set_done = sem("at_set_done")
        c0n_in = [sem(f"c0n_in{p}") for p in range(2)]
        c0r_in = [sem(f"c0r_in{p}") for p in range(2)]
        ssq_done = sem("ssq_done")
        msq_done = sem("msq_done")
        rstd_done = sem("rstd_done")
        normed_done = sem("normed_done")
        piece_done = sem("piece_done")
        piece_free = sem("piece_free")
        nt_hi_done = sem("nt_hi_done")
        nt_lo_done = sem("nt_lo_done")
        qkv_hi_done = sem("qkv_hi_done")
        o_hi_done = sem("o_hi_done")
        half_done = sem("half_done")
        scores_done = sem("scores_done")
        max_done = sem("max_done")
        exp_done = sem("exp_done")
        pt_done = sem("pt_done")
        pt_hi_done = sem("pt_hi_done")
        pt_lo_done = sem("pt_lo_done")
        pv_done = sem("pv_done")
        ot_out = sem("ot_out")
        rinv_done = sem("rinv_done")
        heads_done = sem("heads_done")
        h_out = [sem(f"h_out{p}") for p in range(2)]

        def tile_of(u):
            return 1 - u % 2

        def banks(u):
            return 2 - u % 2

        def bank0(u):
            return 3 * (u // 2) + 2 * (u % 2)

        def places(j, par, has_prev, has_next):
            base = 26 * j + 13 * par + 5 if has_prev else len(PROJ_PIECES)
            names = [n for n in PIECES if (has_prev if n in OUT_PIECES else has_next)]
            return {n: base + c for c, n in enumerate(names)}

        FIRST = {n: c for c, n in enumerate(PROJ_PIECES)}
        LAST = {n: 13 * B - len(OUT_PIECES) + c for c, n in enumerate(OUT_PIECES)}
        LAST_BATCH = (PAIRS - 1, 1)

        def v_slots(par, t, part):
            return v_parts[par][:, t, part * HD:part * HD + NKV * VSTEP].rearrange("p (g c) -> p g c", c=VSTEP)[:, :, 0:HD]

        def transposed(name, par):
            t = int(name[2])
            if name[0] == "k":
                return k_t[par][:, :, t * P:(t + 1) * P]
            c = 4 * "ab".index(name[4])
            return q_t[par][:, c:c + 4, t * P:(t + 1) * P]

        def has_second(j):
            return not (isinstance(j, int) and j == PAIRS - 1)

        def step_pieces(piece, n, u, place, j, par):
            for name in n:
                if PIECES[name] == (u, place):
                    piece(name, *(before(j, par) if name in OUT_PIECES else after(j, par)), n[name])

        block = ctx.enter_context(nc.Block())

        @block.sync
        def _(sp):
            for dst, src in ((wqkv_raw, w_qkv), (wo_raw, w_o), (nw, norm_w), (ident, ident_in), (mask, mask_in)):
                sp.dma_start(dst[:], src).then_inc(const_in, 16)

            def load_to_normalise(j, par):
                i = 2 * j + par
                until(sp, normed_done, 2 * i - 2)
                sp.dma_start(c0n[par][:], c0[bass.ds(i, 1)].rearrange("b p t d -> (b p) t d")).then_inc(c0n_in[par], 16)

            def load_to_add(j, par):
                i = 2 * j + par
                until(sp, h_out[par], 16 * j)
                sp.dma_start(c0r[par][:], c0[bass.ds(i, 1)].rearrange("b p t d -> (b p) t d")).then_inc(c0r_in[par], 16)

            load_to_normalise(0, 0)
            load_to_normalise(0, 1)
            load_to_add(0, 0)
            load_to_normalise(1, 0)
            load_to_add(0, 1)
            load_to_normalise(1, 1)
            load_to_add(1, 0)
            with sp.Fori(2, PAIRS) as j:
                load_to_normalise(j, 0)
                load_to_add(j - 1, 1)
                load_to_normalise(j, 1)
                load_to_add(j, 0)
            load_to_add(PAIRS - 1, 1)
            for dst, src, arrived in later_weights:
                sp.dma_start(dst[:], src).then_inc(arrived, 16)

        @block.gpsimd
        def _(pool):
            def root(j, par):
                i = 2 * j + par
                pool.wait_ge(msq_done, i + 1)
                until(pool, normed_done, 2 * i)
                nc.gpsimd.tensor_tensor(rstd[:], msq[:], minus_half[:], ALU.pow).then_inc(rstd_done, 1)

            def piece(name, j, par, n):
                if name in ("out_q1", "out_q0"):
                    q = int(name[-1])
                    pool.wait_ge(piece_free, n + 1)
                    out = o[:, q, :].rearrange("p (g j d) -> p j g d", g=NKV, j=G)
                    nc.gpsimd.tensor_tensor(out, on[q][:, :, :, 0, :], on[q][:, :, :, 1, :], ALU.add).then_inc(heads_done, 1)
                elif name == "out_proj":
                    i = 2 * j + par
                    pool.wait_ge(piece_free, n + 1)
                    pool.dma_start(h[bass.ds(i, 1)].rearrange("b p t d -> (b p) t d"), h_sb[par][:]).then_inc(h_out[par], 16)

            def first():
                for p in range(2):
                    nc.gpsimd.memset(v_parts[p][:].bitcast(F32), 0.0).then_inc(set_done, 1)
                nc.gpsimd.memset(minus_half[:], -0.5).then_inc(set_done, 1)
                pool.wait_ge(set_done, 3)
                root(0, 0)
                root(0, 1)

            def body(j, par, has_prev, has_next):
                n = places(j, par, has_prev, has_next)
                for u in range(UNITS):
                    for place in range(2):
                        step_pieces(piece, n, u, place, j, par)
                if has_second(j):
                    root(j + 1, par)

            def last():
                for name in OUT_PIECES:
                    piece(name, *LAST_BATCH, LAST[name])

            rolled(pool, first, body, last)
            for p in range(2):
                pool.wait_ge(h_out[p], 16 * PAIRS)

        @block.scalar
        def _(act):
            def square_sums(j, par):
                i = 2 * j + par
                act.wait_ge(c0n_in[par], 16 * j + 16)
                until(act, msq_done, i)
                for t in range(TT):
                    until(act, ssq_done, 2 * i + t)
                    nc.scalar.activation(squares[:], c0n[par][:, t, :], ACT.Square, accum_out=ssq[:, t:t + 1]).then_inc(ssq_done, 1)

            def piece(name, j, par, n):
                i = 2 * j + par
                if name in ("norm_t", "out_t"):
                    hi, done = (nt_hi, nt_hi_done) if name == "norm_t" else (o_hi, o_hi_done)
                    act.wait_ge(piece_done, n + 1)
                    nc.scalar.activation(hi[:], shared_k, ACT.Copy).then_inc(done, 1)
                elif name in ("qkv_0", "qkv_1"):
                    t = int(name[-1])
                    act.wait_ge(piece_done, n + 1)
                    q = shared[:, 0:D].rearrange("p (h d) -> p h d", h=NH).unsqueeze(2).broadcast_to([P, NH, 2, HD])
                    nc.scalar.activation(q_parts[t][:, :, 0:2, :], q, ACT.Copy).then_inc(qkv_hi_done, 1)
                    k = shared[:, D:D + NKV * HD].rearrange("p (h d) -> p h d", h=NKV).unsqueeze(2).broadcast_to([P, NKV, 4, HD])
                    nc.scalar.activation(k_parts[t][:, :, :, 0, :], k, ACT.Copy).then_inc(qkv_hi_done, 1)
                    act.wait_ge(set_done, 3)
                    until(act, pv_done, 8 * i - 8)
                    v = shared[:, D + NKV * HD:QKV].rearrange("p (h d) -> p h d", h=NKV)
                    nc.scalar.activation(v_slots(par, t, 0), v, ACT.Copy).then_inc(qkv_hi_done, 1)
                elif name in ("k_0", "k_1", "q_1_a", "q_1_b"):
                    act.wait_ge(piece_done, n + 1)
                    nc.scalar.activation(transposed(name, par), shared[:].rearrange("p (c s) -> p c s", s=P), ACT.Copy).then_inc(piece_free, 1)

            def exps(j, par, u):
                i = 2 * j + par
                q, g = tile_of(u), u // 2
                until(act, pt_done, 12 * i + (bank0(u - 1) if u else -1))
                if u < 2:
                    until(act, rinv_done, 2 * i - 2)
                for m in (0, 2, 1, 3):
                    act.wait_ge(max_done, 12 * i + bank0(u) + (m % 2 + 1 if q else 1))
                    src = s_q1[m % 2][:, m // 2, :] if q else s_q0[:, m, :]
                    nc.scalar.activation(probs[q][:, m, :], src, ACT.Exp, bias=neg_max[q][:, m:m + 1],
                                         accum_out=sums[par][:, q, g, m:m + 1]).then_inc(exp_done, 1)

            def high_parts(j, par, u):
                i = 2 * j + par
                q = tile_of(u)
                until(act, pv_done, 8 * i + u - 1)
                for n in range(banks(u)):
                    act.wait_ge(pt_done, 12 * i + bank0(u) + n + 1)
                    nc.scalar.activation(pt_hi[q][:, n, :], pt[(bank0(u) + n) % 2][:], ACT.Copy).then_inc(pt_hi_done, 1)

            def empty_ot(j, par, q):
                i = 2 * j + par
                act.wait_ge(pv_done, 8 * i + 8 - q)
                nc.scalar.activation(ot_sb[q][:].rearrange("p j s -> p (j s)"), ot[q][:], ACT.Copy).then_inc(ot_out, 1)

            def first():
                act.wait_ge(const_in, 16 * 5)
                nc.scalar.activation(identb[:], ident[:], ACT.Copy).then_inc(w_hi_done, 1)
                nc.scalar.activation(maskb[:], mask[:].unsqueeze(1).broadcast_to([P, G, P]), ACT.Copy).then_inc(w_hi_done, 1)
                for t in range(KT):
                    nc.scalar.activation(wqkv_hi[:, t, 0:D], wqkv_raw[:, t, 0:D], ACT.Copy, scale=HD ** -0.5).then_inc(w_hi_done, 1)
                    nc.scalar.activation(wqkv_hi[:, t, D:QKV], wqkv_raw[:, t, D:QKV], ACT.Copy).then_inc(w_hi_done, 1)
                nc.scalar.activation(wo_hi[:], wo_raw[:], ACT.Copy).then_inc(w_hi_done, 1)
                square_sums(0, 0)
                for name in PROJ_PIECES:
                    piece(name, 0, 0, FIRST[name])
                exps(0, 0, 0)
                square_sums(0, 1)

            def body(j, par, has_prev, has_next):
                n = places(j, par, has_prev, has_next)
                for u in range(UNITS):
                    if has_prev and u < 2:
                        empty_ot(*before(j, par), 1 - u)
                    if u + 1 < UNITS:
                        exps(j, par, u + 1)
                    elif has_next:
                        exps(*after(j, par), 0)
                    step_pieces(piece, n, u - 1, 1, j, par)
                    high_parts(j, par, u)
                    step_pieces(piece, n, u, 0, j, par)
                    if u == 6 and has_second(j):
                        square_sums(j + 1, par)

            def last():
                for q in (1, 0):
                    empty_ot(*LAST_BATCH, q)
                for name in OUT_PIECES:
                    piece(name, *LAST_BATCH, LAST[name])

            rolled(act, first, body, last)

        @block.vector
        def _(dve):
            def mean_squares(j, par):
                i = 2 * j + par
                dve.wait_ge(ssq_done, 2 * i + 2)
                until(dve, rstd_done, i)
                nc.vector.tensor_scalar(msq[:], ssq[:], 1.0 / D, EPS, ALU.mult, ALU.add).then_inc(msq_done, 1)

            def normalise(j, par):
                i = 2 * j + par
                dve.wait_ge(rstd_done, i + 1)
                for t in range(TT):
                    nc.vector.scalar_tensor_tensor(out=normed[:, t, :], in0=c0n[par][:, t, :], scalar=rstd[:, t:t + 1], in1=nw[:],
                                                   op0=ALU.mult, op1=ALU.mult).then_inc(normed_done, 1)

            def piece(name, j, par, n):
                i = 2 * j + par
                if name in ("norm_t", "out_t"):
                    hi, lo, done = (nt_hi, nt_lo, nt_hi_done) if name == "norm_t" else (o_hi, o_lo, o_hi_done)
                    dve.wait_ge(done, i + 1)
                    nc.vector.tensor_tensor(lo[:], shared_k, hi[:].bitcast(F32), ALU.subtract).then_inc(piece_free, 1)
                elif name in ("qkv_0", "qkv_1"):
                    t = int(name[-1])
                    dve.wait_ge(qkv_hi_done, 6 * i + 3 * t + 3)
                    q = shared[:, 0:D].rearrange("p (h d) -> p h d", h=NH).unsqueeze(2).broadcast_to([P, NH, 2, HD])
                    nc.vector.tensor_tensor(q_parts[t][:, :, 2:4, :], q, q_parts[t][:, :, 0:2, :].bitcast(F32), ALU.subtract)
                    k = shared[:, D:D + NKV * HD].rearrange("p (h d) -> p h d", h=NKV).unsqueeze(2).broadcast_to([P, NKV, 4, HD])
                    nc.vector.tensor_tensor(k_parts[t][:, :, :, 1, :], k, k_parts[t][:, :, :, 0, :].bitcast(F32), ALU.subtract)
                    v = shared[:, D + NKV * HD:QKV].rearrange("p (h d) -> p h d", h=NKV)
                    nc.vector.tensor_tensor(v_slots(par, t, 1), v, v_slots(par, t, 0).bitcast(F32), ALU.subtract).then_inc(piece_free, 1)
                elif name in ("q_0_a", "q_0_b"):
                    dve.wait_ge(piece_done, n + 1)
                    nc.vector.tensor_copy(transposed(name, par), shared[:].rearrange("p (c s) -> p c s", s=P)).then_inc(piece_free, 1)
                elif name in ("out_q1", "out_q0"):
                    q = int(name[-1])
                    dve.wait_ge(rinv_done, 2 * i + 2 - q)
                    dve.wait_ge(piece_done, n + 1)
                    until(dve, heads_done, 2 * i - q)
                    scale = rinv[q][:].rearrange("p j g -> p (j g)").unsqueeze(2).broadcast_to([P, NH, 2 * HD])
                    nc.vector.tensor_tensor(on[q][:].rearrange("p j g a d -> p (j g) (a d)"),
                                            shared[:].rearrange("p (h d) -> p h d", h=NH), scale, ALU.mult).then_inc(piece_free, 1)
                elif name == "out_proj":
                    dve.wait_ge(piece_done, n + 1)
                    dve.wait_ge(c0r_in[par], 16 * j + 16)
                    until(dve, h_out[par], 16 * j)
                    nc.vector.tensor_tensor(h_sb[par][:], shared[:].rearrange("p (t d) -> p t d", t=TT), c0r[par][:], ALU.add).then_inc(piece_free, 1)

            def inverse_sums(j, par):
                i = 2 * j + par
                dve.wait_ge(exp_done, 32 * i + 32)
                for q in (1, 0):
                    nc.vector.reciprocal(rinv[q][:], sums[par][:, q, :, :].rearrange("p g j -> p j g")).then_inc(rinv_done, 1)

            def maxima(j, par, u):
                i = 2 * j + par
                q = tile_of(u)
                until(dve, exp_done, 32 * i + 4 * u - 4)
                for n in range(banks(u)):
                    dve.wait_ge(scores_done, 12 * i + bank0(u) + n + 1)
                    out, src = (neg_max[q][:, n::2], s_q1[n][:]) if q else (neg_max[q][:], s_q0[:])
                    nc.vector.tensor_reduce(out, src, AX_X, ALU.max, negate=True).then_inc(max_done, 1)

            def low_parts(j, par, u):
                i = 2 * j + par
                q = tile_of(u)
                for n in range(banks(u)):
                    dve.wait_ge(pt_hi_done, 12 * i + bank0(u) + n + 1)
                    nc.vector.tensor_tensor(pt_lo[q][:, n, :], pt[(bank0(u) + n) % 2][:], pt_hi[q][:, n, :].bitcast(F32), ALU.subtract).then_inc(pt_lo_done, 1)

            def first():
                dve.wait_ge(w_hi_done, 2 * KT + 3)
                for t in range(KT):
                    nc.vector.scalar_tensor_tensor(out=wqkv_lo[:, t, 0:D], in0=wqkv_raw[:, t, 0:D], scalar=HD ** -0.5,
                                                   in1=wqkv_hi[:, t, 0:D].bitcast(F32), op0=ALU.mult, op1=ALU.subtract).then_inc(w_lo_done, 1)
                    nc.vector.tensor_tensor(wqkv_lo[:, t, D:QKV], wqkv_raw[:, t, D:QKV], wqkv_hi[:, t, D:QKV].bitcast(F32),
                                            ALU.subtract).then_inc(w_lo_done, 1)
                nc.vector.tensor_tensor(wo_lo[:], wo_raw[:], wo_hi[:].bitcast(F32), ALU.subtract).then_inc(w_lo_done, 1)
                mean_squares(0, 0)
                normalise(0, 0)
                for name in PROJ_PIECES:
                    piece(name, 0, 0, FIRST[name])
                maxima(0, 0, 0)
                maxima(0, 0, 1)
                mean_squares(0, 1)
                normalise(0, 1)

            def body(j, par, has_prev, has_next):
                n = places(j, par, has_prev, has_next)
                for u in range(UNITS):
                    if u + 2 < UNITS:
                        maxima(j, par, u + 2)
                    elif has_next:
                        maxima(*after(j, par), u + 2 - UNITS)
                    step_pieces(piece, n, u - 1, 1, j, par)
                    low_parts(j, par, u)
                    step_pieces(piece, n, u, 0, j, par)
                    if u == 7:
                        inverse_sums(j, par)
                    if u == 6 and has_second(j):
                        mean_squares(j + 1, par)
                    if u == 7 and has_second(j):
                        normalise(j + 1, par)

            def last():
                for name in OUT_PIECES:
                    piece(name, *LAST_BATCH, LAST[name])

            rolled(dve, first, body, last)

        @block.tensor
        def _(pe):
            def piece(name, j, par, n):
                i = 2 * j + par
                until(pe, piece_free, n)
                if name == "norm_t":
                    pe.wait_ge(normed_done, 2 * i + 2)
                    for t in range(TT):
                        for k in range(KT):
                            last = nc.tensor.transpose(shared[:, k * S + t * P:k * S + (t + 1) * P], normed[:, t, k * P:(k + 1) * P], ident[:])
                elif name in ("qkv_0", "qkv_1"):
                    t = slice(int(name[-1]) * P, (int(name[-1]) + 1) * P)
                    for k in range(KT):
                        last = exact_product(nc, shared[:, 0:QKV], (nt_hi[:, k, t], nt_lo[:, k, t]),
                                             (wqkv_hi[:, k, :], wqkv_lo[:, k, :]), k == 0, k == KT - 1)
                elif name in ("k_0", "k_1"):
                    for g in range(NKV):
                        src = k_parts[int(name[2])][:, g].rearrange("p a b d -> p (a b d)")
                        last = nc.tensor.transpose(shared[:, g * P:(g + 1) * P], src.bitcast(F32), ident[:])
                elif name[0] == "q":
                    for c in range(4):
                        pair = 4 * "ab".index(name[4]) + c
                        src = q_parts[int(name[2])][:, 2 * pair:2 * pair + 2].rearrange("p h a d -> p (h a d)")
                        last = nc.tensor.transpose(shared[:, c * P:(c + 1) * P], src.bitcast(F32), ident[:])
                elif name in ("out_q1", "out_q0"):
                    q = int(name[-1])
                    pe.wait_ge(ot_out, 2 * i + 2 - q)
                    for c in range(G):
                        last = nc.tensor.transpose(shared[:, c * P:(c + 1) * P], ot_sb[q][:, c, :], ident[:])
                elif name == "out_t":
                    pe.wait_ge(heads_done, 2 * i + 2)
                    for t in range(TT):
                        for k in range(KT):
                            last = nc.tensor.transpose(shared[:, k * S + t * P:k * S + (t + 1) * P], o[:, t, k * P:(k + 1) * P], ident[:])
                elif name == "out_proj":
                    for t in range(TT):
                        toks = slice(t * P, (t + 1) * P)
                        for k in range(KT):
                            last = exact_product(nc, shared[:, t * D:(t + 1) * D], (o_hi[:, k, toks], o_lo[:, k, toks]),
                                                 (wo_hi[:, k, :], wo_lo[:, k, :]), k == 0, k == KT - 1)
                last.then_inc(piece_done, 1)

            def scores(j, par, u):
                i = 2 * j + par
                q, g = tile_of(u), u // 2
                until(pe, exp_done, 32 * i + 4 * u - 4)
                for n in range(banks(u)):
                    out = s_q1[n] if q else s_q0
                    for half in ([n] if q else range(2)):
                        rows = slice(64 * half, 64 * half + 64)
                        if half and not q:
                            pe.wait_ge(half_done, 4 * i + g + 1)
                        for c in range(2):
                            last = nc.tensor.matmul(out[:, c if q else 2 * c + half, :], q_t[par][rows, 2 * g + c, q * P:(q + 1) * P],
                                                    k_t[par][rows, g, 0:(q + 1) * P], start=(c == 0 and (q == 1 or half == 0)), stop=False)
                        if not half and not q:
                            last.then_inc(half_done, 1)
                    nc.tensor.matmul(out[:, :, q * P:(q + 1) * P], identb[:], maskb[:, 0:(2 if q else G), :],
                                     start=False, stop=True).then_inc(scores_done, 1)

            def transposes(j, par, u):
                i = 2 * j + par
                q = tile_of(u)
                pe.wait_ge(exp_done, 32 * i + 4 * u + 4)
                for n in range(banks(u)):
                    until(pe, pt_lo_done, 12 * i + bank0(u) + n - 1)
                    for m in range(G):
                        last = nc.tensor.transpose(pt[(bank0(u) + n) % 2][:, m * P:(m + 1) * P], probs[q][:, m, n * P:(n + 1) * P], ident[:])
                    last.then_inc(pt_done, 1)

            def values(j, par, u):
                i = 2 * j + par
                q, g = tile_of(u), u // 2
                if g == 0:
                    until(pe, ot_out, 2 * i - q)
                pe.wait_ge(pt_lo_done, 12 * i + bank0(u) + banks(u))
                for n in range(banks(u)):
                    v = v_parts[par][:, n, g * P:(g + 1) * P]
                    nc.tensor.matmul(ot[q][:], v, pt_lo[q][:, n, :], start=(g == 0 and n == 0), stop=False)
                    last = nc.tensor.matmul(ot[q][:], v, pt_hi[q][:, n, :], start=False, stop=(g == NKV - 1 and n == q))
                last.then_inc(pv_done, 1)

            def first():
                pe.wait_ge(const_in, 16 * 5)
                pe.wait_ge(w_hi_done, 2 * KT + 3)
                pe.wait_ge(w_lo_done, 2 * KT + 1)
                for name in PROJ_PIECES:
                    piece(name, 0, 0, FIRST[name])
                pe.wait_ge(piece_free, FIRST["q_0_a"] + 1)
                scores(0, 0, 0)
                scores(0, 0, 1)

            def body(j, par, has_prev, has_next):
                n = places(j, par, has_prev, has_next)
                for u in range(UNITS):
                    if u + 2 < UNITS:
                        scores(j, par, u + 2)
                    elif has_next:
                        unit = u + 2 - UNITS
                        pe.wait_ge(piece_free, n["q_0_a" if unit else "q_1_a"] + 1)
                        scores(*after(j, par), unit)
                    transposes(j, par, u)
                    step_pieces(piece, n, u - 1, 1, j, par)
                    if u > 0:
                        values(j, par, u - 1)
                    elif has_prev:
                        values(*before(j, par), UNITS - 1)
                    step_pieces(piece, n, u, 0, j, par)

            def last():
                values(*LAST_BATCH, UNITS - 1)
                for name in OUT_PIECES:
                    piece(name, *LAST_BATCH, LAST[name])

            rolled(pe, first, body, last)


EM = 8
EBANKS = 4


def moe_phase(nc, sem, h, x, norm_w, gate_w, we_raw, we_in, ident_in, iota_in, x1):
    with ExitStack() as ctx:
        def sb(name, shape, dt=F32):
            return ctx.enter_context(nc.sbuf_tensor(name, shape, dt))

        def bank(name, shape):
            return ctx.enter_context(nc.psum_tensor(name, shape, F32))

        ident = sb("mo_ident", [P, P])
        iota = sb("mo_iota", [P, EM])
        nw = sb("mo_norm_w", [P, D])
        gw_raw = sb("gw_raw", [P, KT, EM])
        gw_hi = sb("gw_hi", [P, KT, EM], F32R)
        gw_lo = sb("gw_lo", [P, KT, EM], F32R)
        we_hi = sb("we_hi", [P, KT, EM * D], F32R)
        we_lo = sb("we_lo", [P, KT, EM * D], F32R)
        minus_half = sb("mo_minus_half", [P, TT])
        h_in = [sb(f"h_in{p}", [P, TT, D]) for p in range(2)]
        x_in = [sb(f"x_in{p}", [P, TT, D]) for p in range(2)]
        acc = [sb(f"acc{p}", [P, TT, D]) for p in range(2)]
        squares = sb("mo_squares", [P, D])
        ssq = sb("mo_ssq", [P, TT])
        msq = sb("mo_msq", [P, TT])
        rstd = sb("mo_rstd", [P, TT])
        normed = sb("mo_normed", [P, TT, D])
        n_hi = [sb(f"n_hi{p}", [P, KT, S], F32R) for p in range(2)]
        n_lo = [sb(f"n_lo{p}", [P, KT, S], F32R) for p in range(2)]
        logits = sb("logits", [P, TT, EM])
        top = sb("top", [P, TT, 8])
        top_at = sb("top_at", [P, TT, 8], U32)
        picked = sb("picked", [P, TT, 2])
        gap = sb("gap", [P, TT])
        odds = sb("odds", [P, TT])
        odds1 = sb("odds1", [P, TT])
        share = sb("share", [P, TT, 2])
        one_hot = sb("one_hot", [P, TT, 2, EM])
        comb = [sb(f"comb{p}", [P, TT, EM]) for p in range(2)]
        norm_t = bank("norm_t", [P, KT, S])
        gate_ps = bank("gate_ps", [P, TT, EM])
        expert_ps = [bank(f"expert_ps{n}", [P, 2, D]) for n in range(EBANKS)]

        const_in = sem("mo_const_in")
        w_hi_done = sem("mo_w_hi_done")
        w_lo_done = sem("mo_w_lo_done")
        set_done = sem("mo_set_done")
        hx_in = [sem(f"hx_in{p}") for p in range(2)]
        ssq_done = sem("mo_ssq_done")
        msq_done = sem("mo_msq_done")
        rstd_done = sem("mo_rstd_done")
        normed_done = sem("mo_normed_done")
        norm_t_done = sem("norm_t_done")
        n_hi_done = sem("n_hi_done")
        n_lo_done = sem("n_lo_done")
        gate_done = sem("gate_done")
        logits_done = sem("logits_done")
        top_done = sem("top_done")
        odds_done = sem("odds_done")
        comb_done = sem("comb_done")
        expert_done = sem("expert_done")
        acc_set = sem("acc_set")
        acc_done = sem("acc_done")
        x1_out = [sem(f"x1_out{p}") for p in range(2)]
        NPAIR = EM // 2
        NB = TT * NPAIR

        block = ctx.enter_context(nc.Block())

        @block.sync
        def _(sp):
            for dst, src in ((gw_raw, gate_w), (nw, norm_w), (ident, ident_in), (iota, iota_in)):
                sp.dma_start(dst[:], src).then_inc(const_in, 16)

            def load(j, par):
                i = 2 * j + par
                until(sp, normed_done, 2 * i - 2)
                alone(sp)
                until(sp, acc_set, i - 1)
                sp.dma_start(h_in[par][:], h[bass.ds(i, 1)].rearrange("b p t d -> (b p) t d")).then_inc(hx_in[par], 16)
                sp.dma_start(x_in[par][:], x[bass.ds(i, 1)].rearrange("b p t d -> (b p) t d")).then_inc(hx_in[par], 16)

            load(0, 0)
            load(0, 1)
            with sp.Fori(1, PAIRS) as j:
                load(j, 0)
                load(j, 1)

        @block.gpsimd
        def _(pool):
            def root(j, par):
                i = 2 * j + par
                pool.wait_ge(msq_done, i + 1)
                until(pool, normed_done, 2 * i)
                nc.gpsimd.tensor_tensor(rstd[:], msq[:], minus_half[:], ALU.pow).then_inc(rstd_done, 1)

            def begin_sum(j, par):
                i = 2 * j + par
                pool.wait_ge(hx_in[par], 32 * j + 32)
                until(pool, x1_out[par], 16 * j)
                nc.gpsimd.tensor_tensor(acc[par][:], h_in[par][:], x_in[par][:], ALU.add).then_inc(acc_set, 1)

            def first():
                nc.gpsimd.memset(minus_half[:], -0.5).then_inc(set_done, 1)
                pool.wait_ge(set_done, 1)
                root(0, 0)
                begin_sum(0, 0)

            def store(j, par):
                i = 2 * j + par
                pool.wait_ge(acc_done, EM * TT * (i + 1))
                pool.dma_start(x1[bass.ds(i, 1)].rearrange("b p t d -> (b p) t d"), acc[par][:]).then_inc(x1_out[par], 16)

            def body(j, par, has_prev, has_next):
                if has_next:
                    root(*after(j, par))
                if has_prev:
                    store(*before(j, par))
                if has_next:
                    begin_sum(*after(j, par))

            rolled(pool, first, body, lambda: store(PAIRS - 1, 1))
            for p in range(2):
                pool.wait_ge(x1_out[p], 16 * PAIRS)

        @block.scalar
        def _(act):
            def square_sums(j, par):
                i = 2 * j + par
                act.wait_ge(hx_in[par], 32 * j + 32)
                until(act, msq_done, i)
                for t in range(TT):
                    until(act, ssq_done, 2 * i + t)
                    nc.scalar.activation(squares[:], h_in[par][:, t, :], ACT.Square, accum_out=ssq[:, t:t + 1]).then_inc(ssq_done, 1)

            def high_parts(j, par):
                i = 2 * j + par
                act.wait_ge(norm_t_done, i + 1)
                until(act, expert_done, NB * (i - 1))
                nc.scalar.activation(n_hi[par][:], norm_t[:], ACT.Copy).then_inc(n_hi_done, 1)

            def second_odds(j, par):
                i = 2 * j + par
                act.wait_ge(top_done, 7 * i + 6)
                nc.scalar.activation(odds[:], gap[:], ACT.Exp).then_inc(odds_done, 1)

            def first():
                act.wait_ge(we_in, 16)
                act.wait_ge(const_in, 16 * 4)
                nc.scalar.activation(we_hi[:], we_raw[:], ACT.Copy).then_inc(w_hi_done, 1)
                nc.scalar.activation(gw_hi[:], gw_raw[:], ACT.Copy).then_inc(w_hi_done, 1)
                square_sums(0, 0)
                high_parts(0, 0)
                second_odds(0, 0)

            def body(j, par, has_prev, has_next):
                if has_next:
                    square_sums(*after(j, par))
                    high_parts(*after(j, par))
                    second_odds(*after(j, par))

            rolled(act, first, body, lambda: None)

        @block.vector
        def _(dve):
            def normalise(j, par):
                i = 2 * j + par
                dve.wait_ge(ssq_done, 2 * i + 2)
                until(dve, rstd_done, i)
                nc.vector.tensor_scalar(msq[:], ssq[:], 1.0 / D, EPS, ALU.mult, ALU.add).then_inc(msq_done, 1)
                dve.wait_ge(rstd_done, i + 1)
                until(dve, norm_t_done, i)
                for t in range(TT):
                    nc.vector.scalar_tensor_tensor(out=normed[:, t, :], in0=h_in[par][:, t, :], scalar=rstd[:, t:t + 1], in1=nw[:],
                                                   op0=ALU.mult, op1=ALU.mult).then_inc(normed_done, 1)

            def low_parts(j, par):
                i = 2 * j + par
                dve.wait_ge(n_hi_done, i + 1)
                nc.vector.tensor_tensor(n_lo[par][:], norm_t[:], n_hi[par][:].bitcast(F32), ALU.subtract).then_inc(n_lo_done, 1)

            def top_two(j, par):
                i = 2 * j + par
                dve.wait_ge(gate_done, i + 1)
                until(dve, comb_done, 7 * i)
                nc.vector.tensor_copy(logits[:], gate_ps[:]).then_inc(logits_done, 1)
                dve.wait_ge(logits_done, i + 1)
                alone(dve)
                for t in range(TT):
                    nc.vector.max(top[:, t, :], logits[:, t, :]).then_inc(top_done, 1)
                for t in range(TT):
                    dve.wait_ge(top_done, 7 * i + t + 1)
                    alone(dve)
                    nc.vector.max_index(top_at[:, t, :], top[:, t, :], logits[:, t, :]).then_inc(top_done, 1)
                dve.wait_ge(top_done, 7 * i + 4)
                nc.vector.tensor_copy(picked[:], top_at[:, :, 0:2]).then_inc(top_done, 1)
                until(dve, odds_done, i)
                nc.vector.tensor_tensor(gap[:], top[:, :, 1], top[:, :, 0], ALU.subtract).then_inc(top_done, 1)
                dve.wait_ge(odds_done, i + 1)
                nc.vector.tensor_scalar(odds1[:], odds[:], 1.0, None, ALU.add).then_inc(top_done, 1)
                dve.wait_ge(top_done, 7 * i + 7)
                nc.vector.reciprocal(share[:, :, 0], odds1[:]).then_inc(comb_done, 1)
                dve.wait_ge(comb_done, 7 * i + 1)
                nc.vector.tensor_tensor(share[:, :, 1], odds[:], share[:, :, 0], ALU.mult).then_inc(comb_done, 1)
                dve.wait_ge(comb_done, 7 * i + 2)
                for t in range(TT):
                    for n in range(2):
                        nc.vector.tensor_scalar(one_hot[:, t, n, :], iota[:], picked[:, t, n:n + 1], share[:, t, n:n + 1],
                                                ALU.is_equal, ALU.mult).then_inc(comb_done, 1)
                dve.wait_ge(comb_done, 7 * i + 6)
                until(dve, acc_done, EM * TT * (i - 1))
                nc.vector.tensor_tensor(comb[par][:], one_hot[:, :, 0, :], one_hot[:, :, 1, :], ALU.add).then_inc(comb_done, 1)

            def add_pair(j, par, m):
                i = 2 * j + par
                if m == 0:
                    dve.wait_ge(comb_done, 7 * i + 7)
                    dve.wait_ge(acc_set, i + 1)
                dve.wait_ge(expert_done, NB * i + TT * m + TT)
                for c in range(2):
                    for t in range(TT):
                        until(dve, acc_done, EM * TT * i + TT * (2 * m + c) + t - 1)
                        nc.vector.scalar_tensor_tensor(out=acc[par][:, t, :], in0=expert_ps[(TT * m + t) % EBANKS][:, c, :],
                                                       scalar=comb[par][:, t, 2 * m + c:2 * m + c + 1], in1=acc[par][:, t, :],
                                                       op0=ALU.mult, op1=ALU.add).then_inc(acc_done, 1)

            def first():
                dve.wait_ge(w_hi_done, 2)
                nc.vector.tensor_tensor(we_lo[:], we_raw[:], we_hi[:].bitcast(F32), ALU.subtract).then_inc(w_lo_done, 1)
                nc.vector.tensor_tensor(gw_lo[:], gw_raw[:], gw_hi[:].bitcast(F32), ALU.subtract).then_inc(w_lo_done, 1)
                normalise(0, 0)
                low_parts(0, 0)
                top_two(0, 0)

            def body(j, par, has_prev, has_next):
                if has_next:
                    normalise(*after(j, par))
                add_pair(j, par, 0)
                add_pair(j, par, 1)
                if has_next:
                    low_parts(*after(j, par))
                add_pair(j, par, 2)
                if has_next:
                    top_two(*after(j, par))
                add_pair(j, par, 3)

            rolled(dve, first, body, lambda: None)

        @block.tensor
        def _(pe):
            def transposes(j, par):
                i = 2 * j + par
                pe.wait_ge(normed_done, 2 * i + 2)
                until(pe, n_lo_done, i)
                for t in range(TT):
                    for k in range(KT):
                        last = nc.tensor.transpose(norm_t[:, k, t * P:(t + 1) * P], normed[:, t, k * P:(k + 1) * P], ident[:])
                last.then_inc(norm_t_done, 1)

            def gate(j, par):
                i = 2 * j + par
                pe.wait_ge(n_lo_done, i + 1)
                until(pe, logits_done, i)
                for t in range(TT):
                    toks = slice(t * P, (t + 1) * P)
                    for k in range(KT):
                        last = exact_product(nc, gate_ps[:, t, :], (n_hi[par][:, k, toks], n_lo[par][:, k, toks]),
                                             (gw_hi[:, k, :], gw_lo[:, k, :]), k == 0, k == KT - 1)
                last.then_inc(gate_done, 1)

            def experts(j, par, m):
                i = 2 * j + par
                cols = slice(2 * m * D, (2 * m + 2) * D)
                for t in range(TT):
                    toks = slice(t * P, (t + 1) * P)
                    until(pe, acc_done, EM * TT * i + 2 * TT * (m - EBANKS // TT) + 2 * TT)
                    out = expert_ps[(TT * m + t) % EBANKS][:].rearrange("p e d -> p (e d)")
                    for k in range(KT):
                        last = exact_product(nc, out, (n_hi[par][:, k, toks], n_lo[par][:, k, toks]),
                                             (we_hi[:, k, cols], we_lo[:, k, cols]), k == 0, k == KT - 1)
                    last.then_inc(expert_done, 1)

            def first():
                pe.wait_ge(const_in, 16 * 4)
                pe.wait_ge(w_lo_done, 2)
                transposes(0, 0)
                gate(0, 0)

            def body(j, par, has_prev, has_next):
                experts(j, par, 0)
                experts(j, par, 1)
                if has_next:
                    transposes(*after(j, par))
                experts(j, par, 2)
                if has_next:
                    gate(*after(j, par))
                experts(j, par, 3)

            rolled(pe, first, body, lambda: None)


ER = P
LORA_SCALE = 2.0
E1, H1 = 16, 512
HT1 = H1 // P


def lora_shared_phase(nc, sem, x1, cond_er, w_base, b_base, a_er, b_er, gate_w, gu_raw, dn_raw, shared_in, ident_in, hs, logits, out):
    GU = 2 * KT * H1
    DN = HT1 * D
    with ExitStack() as ctx:
        def sb(name, shape, dt=F32):
            return ctx.enter_context(nc.sbuf_tensor(name, shape, dt))

        def bank(name, shape):
            return ctx.enter_context(nc.psum_tensor(name, shape, F32))

        ident = sb("lo_ident", [P, P])
        cond_sb = sb("lo_cond", [ER, B])
        wb_sb = sb("wb_sb", [P, KT, D])
        bb_sb = sb("bb_sb", [P, D])
        a_raw = sb("a_raw", [ER, D])
        a_hi = sb("a_hi", [ER, D], F32R)
        a_lo = sb("a_lo", [ER, D], F32R)
        b_raw = sb("b_raw", [ER, D])
        rw_raw = sb("rw_raw", [P, KT, E1])
        rw_hi = sb("rw_hi", [P, KT, E1], F32R)
        rw_lo = sb("rw_lo", [P, KT, E1], F32R)
        gu_hi = sb("sh_gu_hi", [P, GU], F32R)
        gu_lo = sb("sh_gu_lo", [P, GU], F32R)
        dn_hi = sb("sh_dn_hi", [P, DN], F32R)
        dn_lo = sb("sh_dn_lo", [P, DN], F32R)
        x1_sb = [sb(f"x1_sb{p}", [P, TT, D]) for p in range(2)]
        x1_add = [sb(f"x1_add{p}", [P, TT, D]) for p in range(2)]
        b_scaled = sb("b_scaled", [ER, D])
        b_hi = sb("b_hi", [ER, D], F32R)
        b_lo = sb("b_lo", [ER, D], F32R)
        weff = sb("weff", [P, KT, D])
        weff_hi = sb("weff_hi", [P, KT, D], F32R)
        weff_lo = sb("weff_lo", [P, KT, D], F32R)
        xt_hi = sb("xt_hi", [P, KT, S], F32R)
        xt_lo = sb("xt_lo", [P, KT, S], F32R)
        hs_sb = [sb(f"hs_sb{p}", [P, TT, D]) for p in range(2)]
        ht_hi = [sb(f"ht_hi{p}", [P, KT, S], F32R) for p in range(2)]
        ht_lo = [sb(f"ht_lo{p}", [P, KT, S], F32R) for p in range(2)]
        gelu = [sb(f"sh_gelu{q}", [P, 2, S]) for q in range(2)]
        hid = [sb(f"sh_hid{q}", [P, 2, S]) for q in range(2)]
        hid_hi = [[sb(f"sh_hid_hi{p}{q}", [P, 2, S], F32R) for q in range(2)] for p in range(2)]
        hid_lo = [[sb(f"sh_hid_lo{p}{q}", [P, 2, S], F32R) for q in range(2)] for p in range(2)]
        out_sb = [sb(f"out_sb{p}", [P, TT, D]) for p in range(2)]
        turned = bank("turned", [P, KT, S])
        cond_ps = bank("cond_ps", [P, TT, D])
        side = bank("side", [P, KT, D])
        gate_ps = [bank(f"sh_gate_ps{q}", [P, 2, S]) for q in range(2)]
        up_ps = [bank(f"sh_up_ps{q}", [P, 2, S]) for q in range(2)]
        down_ps = bank("sh_down_ps", [P, TT, D])

        const_in = sem("lo_const_in")
        w_hi_done = sem("lo_w_hi_done")
        w_lo_done = sem("lo_w_lo_done")
        x1_in = [sem(f"x1_in{p}") for p in range(2)]
        x1_add_in = [sem(f"x1_add_in{p}") for p in range(2)]
        b_scaled_done = sem("b_scaled_done")
        b_hi_done = sem("b_hi_done")
        b_lo_done = sem("b_lo_done")
        lora_done = sem("lora_done")
        weff_done = sem("weff_done")
        weff_hi_done = sem("weff_hi_done")
        weff_lo_done = sem("weff_lo_done")
        xt_done = sem("xt_done")
        xt_hi_done = sem("xt_hi_done")
        xt_lo_done = sem("xt_lo_done")
        cond_done = sem("cond_done")
        hs_done = sem("hs_done")
        hs_out = [sem(f"hs_out{p}") for p in range(2)]
        ht_done = sem("ht_done")
        ht_hi_done = sem("ht_hi_done")
        ht_lo_done = sem("ht_lo_done")
        route_done = sem("route_done")
        logits_set = sem("logits_set")
        gate_done = sem("sh_gate_done")
        up_done = sem("sh_up_done")
        gelu_done = sem("sh_gelu_done")
        hid_done = sem("sh_hid_done")
        hid_hi_done = sem("sh_hid_hi_done")
        hid_lo_done = sem("sh_hid_lo_done")
        down_done = sem("sh_down_done")
        out_done = sem("sh_out_done")
        out_out = [sem(f"sh_out_out{p}") for p in range(2)]
        CONSTS = ((a_raw, a_er), (b_raw, b_er), (rw_raw, gate_w),
                  (wb_sb, w_base), (bb_sb, b_base), (cond_sb, cond_er), (ident, ident_in))

        block = ctx.enter_context(nc.Block())

        @block.sync
        def _(sp):
            for dst, src in CONSTS:
                sp.dma_start(dst[:], src).then_inc(const_in, 16)

            def load(j, par):
                i = 2 * j + par
                until(sp, xt_done, i - 1)
                sp.dma_start(x1_sb[par][:], x1[bass.ds(i, 1)].rearrange("b p t d -> (b p) t d")).then_inc(x1_in[par], 16)
                until(sp, out_done, i - 1)
                sp.dma_start(x1_add[par][:], x1[bass.ds(i, 1)].rearrange("b p t d -> (b p) t d")).then_inc(x1_add_in[par], 16)

            load(0, 0)
            load(0, 1)
            with sp.Fori(1, PAIRS) as j:
                load(j, 0)
                load(j, 1)

        @block.gpsimd
        def _(pool):
            def body(j, par, has_prev, has_next):
                if has_next:
                    weff_low(*after(j, par))
                    store_hs(*after(j, par))
                if has_prev:
                    store_out(*before(j, par))

            def weff_low(j, par):
                i = 2 * j + par
                pool.wait_ge(weff_hi_done, i + 1)
                until(pool, cond_done, i)
                nc.gpsimd.tensor_tensor(weff_lo[:], weff[:], weff_hi[:].bitcast(F32), ALU.subtract).then_inc(weff_lo_done, 1)

            def store_hs(j, par):
                i = 2 * j + par
                pool.wait_ge(hs_done, i + 1)
                pool.dma_start(hs[bass.ds(i, 1)].rearrange("b (t p) d -> p (b t) d", p=P), hs_sb[par][:]).then_inc(hs_out[par], 16)

            def store_out(j, par):
                i = 2 * j + par
                pool.wait_ge(out_done, i + 1)
                pool.dma_start(out[bass.ds(i, 1)].rearrange("b (t p) d -> p (b t) d", p=P), out_sb[par][:]).then_inc(out_out[par], 16)

            def first():
                weff_low(0, 0)
                store_hs(0, 0)

            rolled(pool, first, body, lambda: store_out(PAIRS - 1, 1))
            for p in range(2):
                pool.wait_ge(hs_out[p], 16 * PAIRS)
                pool.wait_ge(out_out[p], 16 * PAIRS)

        @block.scalar
        def _(act):
            def b_high(j, par):
                i = 2 * j + par
                act.wait_ge(b_scaled_done, i + 1)
                until(act, lora_done, i)
                nc.scalar.activation(b_hi[:], b_scaled[:], ACT.Copy).then_inc(b_hi_done, 1)

            def weff_high(j, par):
                i = 2 * j + par
                act.wait_ge(weff_done, i + 1)
                until(act, cond_done, i)
                nc.scalar.activation(weff_hi[:], weff[:], ACT.Copy).then_inc(weff_hi_done, 1)

            def x1_high(j, par):
                i = 2 * j + par
                act.wait_ge(xt_done, i + 1)
                until(act, cond_done, i)
                nc.scalar.activation(xt_hi[:], turned[:], ACT.Copy).then_inc(xt_hi_done, 1)

            def hs_high(j, par):
                i = 2 * j + par
                act.wait_ge(ht_done, i + 1)
                until(act, up_done, 2 * i - 2)
                until(act, route_done, i - 1)
                nc.scalar.activation(ht_hi[par][:], turned[:], ACT.Copy).then_inc(ht_hi_done, 1)

            def gelus(j, par, q):
                i = 2 * j + par
                act.wait_ge(gate_done, 2 * i + q + 1)
                until(act, hid_done, 2 * i - 1 + q)
                nc.scalar.activation(gelu[q][:], gate_ps[q][:], ACT.Gelu).then_inc(gelu_done, 1)

            def hidden_high(j, par, q):
                i = 2 * j + par
                act.wait_ge(hid_done, 2 * i + q + 1)
                until(act, down_done, i - 1)
                nc.scalar.activation(hid_hi[par][q][:], hid[q][:], ACT.Copy).then_inc(hid_hi_done, 1)

            def first():
                act.wait_ge(shared_in, 32)
                act.wait_ge(const_in, 16 * len(CONSTS))
                for dst, src in ((gu_hi, gu_raw), (dn_hi, dn_raw), (a_hi, a_raw), (rw_hi, rw_raw)):
                    nc.scalar.activation(dst[:], src[:], ACT.Copy).then_inc(w_hi_done, 1)
                b_high(0, 0)
                x1_high(0, 0)
                weff_high(0, 0)
                hs_high(0, 0)

            def body(j, par, has_prev, has_next):
                if has_next:
                    b_high(*after(j, par))
                    x1_high(*after(j, par))
                gelus(j, par, 0)
                if has_next:
                    weff_high(*after(j, par))
                hidden_high(j, par, 0)
                gelus(j, par, 1)
                if has_next:
                    hs_high(*after(j, par))
                hidden_high(j, par, 1)

            rolled(act, first, body, lambda: None)

        @block.vector
        def _(dve):
            def scale_b(j, par):
                i = 2 * j + par
                until(dve, b_hi_done, i)
                until(dve, b_lo_done, i)
                nc.vector.tensor_scalar(b_scaled[:], b_raw[:], cond_sb[:, bass.ds(i, 1)], LORA_SCALE, ALU.mult, ALU.mult).then_inc(b_scaled_done, 1)

            def b_low(j, par):
                i = 2 * j + par
                dve.wait_ge(b_hi_done, i + 1)
                until(dve, lora_done, i)
                nc.vector.tensor_tensor(b_lo[:], b_scaled[:], b_hi[:].bitcast(F32), ALU.subtract).then_inc(b_lo_done, 1)

            def x1_low(j, par):
                i = 2 * j + par
                dve.wait_ge(xt_hi_done, i + 1)
                until(dve, cond_done, i)
                nc.vector.tensor_tensor(xt_lo[:], turned[:], xt_hi[:].bitcast(F32), ALU.subtract).then_inc(xt_lo_done, 1)

            def add_base(j, par):
                i = 2 * j + par
                dve.wait_ge(lora_done, i + 1)
                until(dve, weff_lo_done, i)
                nc.vector.tensor_tensor(weff[:], side[:], wb_sb[:], ALU.add).then_inc(weff_done, 1)

            def add_bias(j, par):
                i = 2 * j + par
                dve.wait_ge(cond_done, i + 1)
                until(dve, hs_out[par], 16 * j)
                until(dve, ht_done, i - 1)
                bias = bb_sb[:].unsqueeze(1).broadcast_to([P, TT, D])
                nc.vector.tensor_tensor(hs_sb[par][:], cond_ps[:], bias, ALU.add).then_inc(hs_done, 1)

            def hs_low(j, par):
                i = 2 * j + par
                dve.wait_ge(ht_hi_done, i + 1)
                nc.vector.tensor_tensor(ht_lo[par][:], turned[:], ht_hi[par][:].bitcast(F32), ALU.subtract).then_inc(ht_lo_done, 1)

            def keep_logits(j, par):
                i = 2 * j + par
                dve.wait_ge(route_done, i + 1)
                alone(dve)
                nc.vector.tensor_copy(logits[:, :, bass.ds(i * E1, E1)],
                                      side[:, 0, 0:TT * E1].rearrange("p (t e) -> p t e", t=TT)).then_inc(logits_set, 1)

            def hidden(j, par, q):
                i = 2 * j + par
                dve.wait_ge(gelu_done, 2 * i + q + 1)
                dve.wait_ge(up_done, 2 * i + q + 1)
                until(dve, hid_lo_done, 2 * i - 1 + q)
                nc.vector.tensor_tensor(hid[q][:], up_ps[q][:], gelu[q][:], ALU.mult).then_inc(hid_done, 1)

            def hidden_low(j, par, q):
                i = 2 * j + par
                dve.wait_ge(hid_hi_done, 2 * i + q + 1)
                until(dve, down_done, i - 1)
                nc.vector.tensor_tensor(hid_lo[par][q][:], hid[q][:], hid_hi[par][q][:].bitcast(F32), ALU.subtract).then_inc(hid_lo_done, 1)

            def add_x1(j, par):
                i = 2 * j + par
                dve.wait_ge(down_done, i + 1)
                dve.wait_ge(x1_add_in[par], 16 * j + 16)
                until(dve, out_out[par], 16 * j)
                nc.vector.tensor_tensor(out_sb[par][:], down_ps[:], x1_add[par][:], ALU.add).then_inc(out_done, 1)

            def first():
                dve.wait_ge(w_hi_done, 4)
                for dst, src, hi in ((gu_lo, gu_raw, gu_hi), (dn_lo, dn_raw, dn_hi), (a_lo, a_raw, a_hi), (rw_lo, rw_raw, rw_hi)):
                    nc.vector.tensor_tensor(dst[:], src[:], hi[:].bitcast(F32), ALU.subtract).then_inc(w_lo_done, 1)
                scale_b(0, 0)
                b_low(0, 0)
                x1_low(0, 0)
                add_base(0, 0)
                add_bias(0, 0)
                hs_low(0, 0)

            def body(j, par, has_prev, has_next):
                if has_next:
                    scale_b(*after(j, par))
                    b_low(*after(j, par))
                keep_logits(j, par)
                if has_next:
                    x1_low(*after(j, par))
                hidden(j, par, 0)
                if has_next:
                    add_base(*after(j, par))
                hidden_low(j, par, 0)
                if has_prev:
                    add_x1(*before(j, par))
                if has_next:
                    add_bias(*after(j, par))
                    hs_low(*after(j, par))
                hidden(j, par, 1)
                hidden_low(j, par, 1)

            rolled(dve, first, body, lambda: add_x1(PAIRS - 1, 1))

        @block.tensor
        def _(pe):
            gu_h = gu_hi[:].rearrange("p (g k h) -> p g k h", g=2, k=KT)
            gu_l = gu_lo[:].rearrange("p (g k h) -> p g k h", g=2, k=KT)
            dn_h = dn_hi[:].rearrange("p (h d) -> p h d", h=HT1)
            dn_l = dn_lo[:].rearrange("p (h d) -> p h d", h=HT1)

            def turn_x1(j, par):
                i = 2 * j + par
                pe.wait_ge(x1_in[par], 16 * j + 16)
                until(pe, ht_lo_done, i)
                for t in range(TT):
                    for k in range(KT):
                        last = nc.tensor.transpose(turned[:, k, t * P:(t + 1) * P], x1_sb[par][:, t, k * P:(k + 1) * P], ident[:])
                last.then_inc(xt_done, 1)

            def lora(j, par):
                i = 2 * j + par
                pe.wait_ge(b_lo_done, i + 1)
                until(pe, logits_set, i)
                for k in range(KT):
                    c = slice(k * P, (k + 1) * P)
                    last = exact_product(nc, side[:, k, :], (a_hi[:, c], a_lo[:, c]), (b_hi[:], b_lo[:]), True, True)
                last.then_inc(lora_done, 1)

            def cond(j, par):
                i = 2 * j + par
                pe.wait_ge(xt_lo_done, i + 1)
                pe.wait_ge(weff_lo_done, i + 1)
                until(pe, hs_done, i)
                for t in range(TT):
                    toks = slice(t * P, (t + 1) * P)
                    for k in range(KT):
                        last = exact_product(nc, cond_ps[:, t, :], (xt_hi[:, k, toks], xt_lo[:, k, toks]),
                                             (weff_hi[:, k, :], weff_lo[:, k, :]), k == 0, k == KT - 1)
                last.then_inc(cond_done, 1)

            def turn_hs(j, par):
                i = 2 * j + par
                pe.wait_ge(hs_done, i + 1)
                for t in range(TT):
                    for k in range(KT):
                        last = nc.tensor.transpose(turned[:, k, t * P:(t + 1) * P], hs_sb[par][:, t, k * P:(k + 1) * P], ident[:])
                last.then_inc(ht_done, 1)

            def route(j, par):
                i = 2 * j + par
                pe.wait_ge(ht_lo_done, i + 1)
                pe.wait_ge(weff_done, i + 1)
                for t in range(TT):
                    toks = slice(t * P, (t + 1) * P)
                    for k in range(KT):
                        last = exact_product(nc, side[:, 0, t * E1:(t + 1) * E1], (ht_hi[par][:, k, toks], ht_lo[par][:, k, toks]),
                                             (rw_hi[:, k, :], rw_lo[:, k, :]), k == 0, k == KT - 1)
                last.then_inc(route_done, 1)

            def gate(j, par, q):
                until(pe, gelu_done, 2 * (2 * j + par) - 1 + q)
                slices(gate_ps[q], 0, par, q).then_inc(gate_done, 1)

            def up(j, par, q):
                until(pe, hid_done, 2 * (2 * j + par) - 1 + q)
                slices(up_ps[q], 1, par, q).then_inc(up_done, 1)

            def slices(ps, g, par, q):
                for m in range(2):
                    cols = slice((2 * q + m) * P, (2 * q + m + 1) * P)
                    for k in range(KT):
                        last = exact_product(nc, ps[:, m, :], (gu_h[:, g, k, cols], gu_l[:, g, k, cols]),
                                             (ht_hi[par][:, k, :], ht_lo[par][:, k, :]), k == 0, k == KT - 1)
                return last

            def down(j, par, t):
                i = 2 * j + par
                if t == 0:
                    pe.wait_ge(hid_lo_done, 2 * i + 2)
                    until(pe, out_done, i)
                toks = slice(t * P, (t + 1) * P)
                for m in range(HT1):
                    last = exact_product(nc, down_ps[:, t, :], (hid_hi[par][m // 2][:, m % 2, toks], hid_lo[par][m // 2][:, m % 2, toks]),
                                         (dn_h[:, m, :], dn_l[:, m, :]), m == 0, m == HT1 - 1)
                if t == TT - 1:
                    last.then_inc(down_done, 1)

            def first():
                pe.wait_ge(const_in, 16 * len(CONSTS))
                pe.wait_ge(w_lo_done, 4)
                turn_x1(0, 0)
                lora(0, 0)
                cond(0, 0)
                turn_hs(0, 0)

            def body(j, par, has_prev, has_next):
                route(j, par)
                if has_next:
                    turn_x1(*after(j, par))
                gate(j, par, 0)
                up(j, par, 0)
                if has_next:
                    lora(*after(j, par))
                if has_prev:
                    down(*before(j, par), 0)
                    down(*before(j, par), 1)
                if has_next:
                    cond(*after(j, par))
                gate(j, par, 1)
                if has_next:
                    turn_hs(*after(j, par))
                up(j, par, 1)

            def last():
                for t in range(TT):
                    down(PAIRS - 1, 1, t)

            rolled(pe, first, body, last)


CAP = 2 * S // E1
GROUPS = B * E1 // P
GB = B // GROUPS
GQ = P // CAP
SLOT_COLS = GROUPS * CAP
TILES = GROUPS * GB // GQ


def topk_phase(nc, sem, logits, first_row, ident_in, slot_row, slot_weight):
    ROWS = TT * B
    with ExitStack() as ctx:
        def sb(name, shape, dt=F32):
            return ctx.enter_context(nc.sbuf_tensor(name, shape, dt))

        ident = sb("tk_ident", [P, P])
        row0 = sb("row0", [P, GROUPS])
        top = sb("tk_top", [P, ROWS])
        shifted = sb("shifted", [P, ROWS, E1])
        expd = sb("expd", [P, ROWS, E1])
        exp_sum = sb("exp_sum", [P, ROWS])
        exp_inv = sb("exp_inv", [P, ROWS])
        scores = sb("scores", [P, TT, B * E1])
        work = sb("work", [P, GROUPS, S])
        vals = sb("vals", [P, GROUPS, CAP])
        at = sb("at", [P, GROUPS, CAP], U32)
        rows = sb("rows", [P, GROUPS, CAP])
        rows_t = sb("rows_t", [P, GROUPS, CAP])
        by_expert = [ctx.enter_context(nc.psum_tensor(f"by_expert{n}", [P, 2, S], F32)) for n in range(GROUPS // 2)]

        const_in = sem("tk_const_in")
        softmax_step = sem("softmax_step")
        expd_done = sem("expd_done")
        turned_done = sem("tk_turned_done")
        work_set = sem("work_set")
        best_done = sem("best_done")
        at_done = sem("at_done")
        replaced = sem("replaced")
        rows_done = sem("rows_done")
        slots_set = sem("slots_set")
        ROUNDS = CAP // 8

        block = ctx.enter_context(nc.Block())

        @block.sync
        def _(sp):
            sp.dma_start(ident[:], ident_in).then_inc(const_in, 16)
            sp.dma_start(row0[:], first_row).then_inc(const_in, 16)

        @block.tensor
        def _(pe):
            pe.wait_ge(const_in, 32)
            pe.wait_ge(softmax_step, 5)
            for g in range(GROUPS):
                for t in range(TT):
                    last = nc.tensor.transpose(by_expert[g // 2][:, g % 2, t * P:(t + 1) * P], scores[:, t, g * P:(g + 1) * P], ident[:])
                last.then_inc(turned_done, 1)

        @block.scalar
        def _(act):
            act.wait_ge(softmax_step, 2)
            nc.scalar.activation(expd[:], shifted[:], ACT.Exp).then_inc(expd_done, 1)
            act.wait_ge(turned_done, GROUPS)
            for n in range(GROUPS // 2):
                nc.scalar.activation(work[:, 2 * n:2 * n + 2, :], by_expert[n][:], ACT.Copy).then_inc(work_set, 1)

        @block.vector
        def _(dve):
            def over_experts(v):
                return v[:].unsqueeze(2).broadcast_to([P, ROWS, E1])

            rows_of = logits[:].rearrange("p t (b e) -> p (t b) e", e=E1)
            nc.vector.tensor_reduce(top[:], rows_of, AX_X, ALU.max).then_inc(softmax_step, 1)
            dve.wait_ge(softmax_step, 1)
            nc.vector.tensor_tensor(shifted[:], rows_of, over_experts(top), ALU.subtract).then_inc(softmax_step, 1)
            dve.wait_ge(expd_done, 1)
            nc.vector.tensor_reduce(exp_sum[:], expd[:], AX_X, ALU.add).then_inc(softmax_step, 1)
            dve.wait_ge(softmax_step, 3)
            nc.vector.reciprocal(exp_inv[:], exp_sum[:]).then_inc(softmax_step, 1)
            dve.wait_ge(softmax_step, 4)
            nc.vector.tensor_tensor(scores[:].rearrange("p t (b e) -> p (t b) e", e=E1), expd[:], over_experts(exp_inv),
                                    ALU.mult).then_inc(softmax_step, 1)
            dve.wait_ge(const_in, 32)
            dve.wait_ge(work_set, GROUPS // 2)
            for r in range(ROUNDS):
                eight = slice(8 * r, 8 * r + 8)
                for g in range(GROUPS):
                    until(dve, replaced, GROUPS * (r - 1) + g + 1)
                    nc.vector.max(vals[:, g, eight], work[:, g, :]).then_inc(best_done, 1)
                for g in range(GROUPS):
                    dve.wait_ge(best_done, GROUPS * r + g + 1)
                    nc.vector.max_index(at[:, g, eight], vals[:, g, eight], work[:, g, :]).then_inc(at_done, 1)
                if r < ROUNDS - 1:
                    for g in range(GROUPS):
                        dve.wait_ge(at_done, GROUPS * r + g + 1)
                        nc.vector.match_replace(work[:, g, :], vals[:, g, eight], work[:, g, :], -1.0).then_inc(replaced, 1)
            dve.wait_ge(at_done, GROUPS * ROUNDS)
            nc.vector.tensor_tensor(rows[:], at[:], row0[:].unsqueeze(2).broadcast_to([P, GROUPS, CAP]), ALU.add).then_inc(rows_done, 1)
            dve.wait_ge(rows_done, 1)
            for g in range(GROUPS):
                nc.vector.transpose(rows_t[:, g, :], rows[:, g, :]).then_inc(rows_done, 1)
            for g in range(GROUPS):
                nc.vector.transpose(slot_weight[:, g, :], vals[:, g, :]).then_inc(slots_set, 1)
            dve.wait_ge(rows_done, GROUPS + 1)
            nc.vector.tensor_copy(slot_row[:], rows_t[:]).then_inc(slots_set, 1)
            dve.wait_ge(slots_set, GROUPS + 1)


def experts_phase(nc, sem, hs_rows, slot_row, slot_weight, w_gu, w_dn, gu_raw, dn_raw, gu_in, dn_in, ident_in, out_rows):
    GU = 2 * KT * H1
    DN = HT1 * D
    CT = TILES // 2
    CN = CT * P
    with ExitStack() as ctx:
        def sb(name, shape, dt=F32):
            return ctx.enter_context(nc.sbuf_tensor(name, shape, dt))

        def bank(name, shape):
            return ctx.enter_context(nc.psum_tensor(name, shape, F32))

        ident = sb("ex_ident", [P, P])
        gu_hi = [sb(f"gu_hi{p}", [P, GU], F32R) for p in range(2)]
        gu_lo = [sb(f"gu_lo{p}", [P, GU], F32R) for p in range(2)]
        dn_hi = [sb(f"ex_dn_hi{p}", [P, DN], F32R) for p in range(2)]
        dn_lo = [sb(f"ex_dn_lo{p}", [P, DN], F32R) for p in range(2)]
        row_get = [sb(f"row_get{p}", [P, TILES], U32) for p in range(2)]
        row_put = [sb(f"row_put{p}", [P, TILES], U32) for p in range(2)]
        weight_now = [sb(f"weight_now{p}", [P, TILES]) for p in range(2)]
        toks = [sb(f"toks{c}", [P, CT, D]) for c in range(2)]
        xt_hi = [sb(f"ex_xt_hi{c}", [P, KT, CN], F32R) for c in range(2)]
        xt_lo = [sb(f"ex_xt_lo{c}", [P, KT, CN], F32R) for c in range(2)]
        gelu = [sb(f"gelu{q}", [P, CN]) for q in range(2)]
        hid = [sb(f"ex_hid{q}", [P, CN]) for q in range(2)]
        hid_hi = [sb(f"ex_hid_hi{c}", [P, HT1, CN], F32R) for c in range(2)]
        hid_lo = [sb(f"ex_hid_lo{c}", [P, HT1, CN], F32R) for c in range(2)]
        eo = [sb(f"eo{c}", [P, CT, D]) for c in range(2)]
        turned = [bank(f"ex_turned{k}", [P, CN]) for k in range(KT)]
        gate_ps = [bank(f"ex_gate_ps{q}", [P, CN]) for q in range(2)]
        up_ps = [bank(f"ex_up_ps{q}", [P, CN]) for q in range(2)]
        down_ps = [bank(f"ex_down_ps{n}", [P, 2, D]) for n in range(2)]

        const_in = sem("ex_const_in")
        gu_hi_done = sem("ex_gu_hi_done")
        gu_lo_done = sem("ex_gu_lo_done")
        dn_hi_done = sem("ex_dn_hi_done")
        dn_lo_done = sem("ex_dn_lo_done")
        get_set = sem("ex_get_set")
        put_set = sem("ex_put_set")
        toks_in = [sem(f"ex_toks_in{c}") for c in range(2)]
        xt_done = sem("ex_xt_done")
        xt_hi_done = sem("ex_xt_hi_done")
        xt_lo_done = sem("ex_xt_lo_done")
        gate_up_done = sem("ex_gate_up_done")
        gelu_done = sem("ex_gelu_done")
        hid_done = sem("ex_hid_done")
        hid_hi_done = sem("ex_hid_hi_done")
        hid_lo_done = sem("ex_hid_lo_done")
        down_done = sem("ex_down_done")
        eo_done = sem("ex_eo_done")
        added = [sem(f"ex_added{c}") for c in range(2)]

        EPAIRS = E1 // 2

        def chunk_after(j, par, c):
            return (j, par, 1) if c == 0 else (j, 1, 0) if par == 0 else (j + 1, 0, 0)

        def expert_after(j, par):
            return (j, 1) if par == 0 else (j + 1, 0)

        def by_expert(engine, first, body, last):
            first()
            body(0, 0, False, True)
            body(0, 1, True, True)
            with engine.Fori(1, EPAIRS - 1) as j:
                body(j, 0, True, True)
                body(j, 1, True, True)
            body(EPAIRS - 1, 0, True, True)
            body(EPAIRS - 1, 1, True, False)
            last()

        block = ctx.enter_context(nc.Block())

        @block.sync
        def _(sp):
            sp.dma_start(ident[:], ident_in).then_inc(const_in, 16)

            def load(e):
                until(sp, gu_hi_done, e)
                until(sp, gu_lo_done, e)
                sp.dma_start(gu_raw[:], w_gu[bass.ds(e, 1)].rearrange("e p n -> (e p) n")).then_inc(gu_in, 16)
                until(sp, dn_hi_done, e)
                until(sp, dn_lo_done, e)
                sp.dma_start(dn_raw[:], w_dn[bass.ds(e, 1)].rearrange("e p n -> (e p) n")).then_inc(dn_in, 16)

            with sp.Fori(1, E1) as e:
                load(e)

        @block.gpsimd
        def _(pool):
            def gather(j, par, c):
                e = 2 * j + par
                pool.wait_ge(get_set, e + 1)
                until(pool, xt_done, 2 * (2 * e + c) - 2)
                alone(pool)
                for n in range(CT):
                    at = row_get[par][:, CT * c + n:CT * c + n + 1]
                    nc.gpsimd.indirect_dma_start(out=toks[c][:, n, :], out_offset=None, in_=hs_rows,
                                                 in_offset=bass.IndirectOffsetOnAxis(ap=at, axis=0)).then_inc(toks_in[c], 16)

            def add(j, par, c):
                e = 2 * j + par
                pool.wait_ge(eo_done, CT * (2 * e + c) + CT)
                until(pool, added[c], 16 * CT * e)
                alone(pool)
                for n in range(CT):
                    at = row_put[par][:, CT * c + n:CT * c + n + 1]
                    nc.gpsimd.indirect_dma_start(out=out_rows, out_offset=bass.IndirectOffsetOnAxis(ap=at, axis=0),
                                                 in_=eo[c][:, n, :], in_offset=None, compute_op=ALU.add).then_inc(added[c], 16)

            def first():
                gather(0, 0, 0)
                gather(0, 0, 1)

            def body(j, par, has_prev, has_next):
                if has_prev:
                    add(*before(j, par), 1)
                if has_next:
                    gather(*expert_after(j, par), 0)
                add(j, par, 0)
                if has_next:
                    gather(*expert_after(j, par), 1)

            by_expert(pool, first, body, lambda: add(EPAIRS - 1, 1, 1))
            for c in range(2):
                pool.wait_ge(added[c], 16 * CT * E1)

        @block.scalar
        def _(act):
            def gu_high(j, par):
                e = 2 * j + par
                act.wait_ge(gu_in, 16 * e + 16)
                until(act, gate_up_done, 8 * e - 8)
                nc.scalar.activation(gu_hi[par][:], gu_raw[:], ACT.Copy).then_inc(gu_hi_done, 1)

            def dn_high(j, par):
                e = 2 * j + par
                act.wait_ge(dn_in, 16 * e + 16)
                until(act, down_done, 4 * e - 4)
                nc.scalar.activation(dn_hi[par][:], dn_raw[:], ACT.Copy).then_inc(dn_hi_done, 1)

            def xt_high(j, par, c):
                n = 2 * (2 * j + par) + c
                until(act, gate_up_done, 4 * n - 4)
                for k in range(KT):
                    act.wait_ge(xt_done, 2 * n + k + 1)
                    nc.scalar.activation(xt_hi[c][:, k, :], turned[k][:], ACT.Copy).then_inc(xt_hi_done, 1)

            def gelus(j, par, c, f):
                n = 2 * (2 * j + par) + c
                act.wait_ge(gate_up_done, 4 * n + f + 1)
                until(act, hid_done, 4 * n + f - 1)
                nc.scalar.activation(gelu[f % 2][:], gate_ps[f % 2][:], ACT.Gelu).then_inc(gelu_done, 1)

            def hid_high(j, par, c, f):
                n = 2 * (2 * j + par) + c
                act.wait_ge(hid_done, 4 * n + f + 1)
                until(act, down_done, 2 * n - 2)
                nc.scalar.activation(hid_hi[c][:, f, :], hid[f % 2][:], ACT.Copy).then_inc(hid_hi_done, 1)

            def weigh(j, par, c):
                e = 2 * j + par
                n = 2 * e + c
                act.wait_ge(put_set, 2 * e + 2)
                until(act, added[c], 16 * CT * e)
                for m in range(CT):
                    act.wait_ge(down_done, 2 * n + m // 2 + 1)
                    nc.scalar.activation(eo[c][:, m, :], down_ps[m // 2][:, m % 2, :], ACT.Copy,
                                         scale=weight_now[par][:, CT * c + m:CT * c + m + 1]).then_inc(eo_done, 1)

            def first():
                gu_high(0, 0)
                xt_high(0, 0, 0)
                dn_high(0, 0)

            def body(j, par, has_prev, has_next):
                for c in range(2):
                    gelus(j, par, c, 0)
                    gelus(j, par, c, 1)
                    hid_high(j, par, c, 0)
                    hid_high(j, par, c, 1)
                    if c == 1:
                        weigh(j, par, 0)
                    elif has_prev:
                        weigh(*before(j, par), 1)
                    if c == 0 or has_next:
                        xt_high(*chunk_after(j, par, c))
                    gelus(j, par, c, 2)
                    gelus(j, par, c, 3)
                    hid_high(j, par, c, 2)
                    hid_high(j, par, c, 3)
                    if c == 0 and has_next:
                        gu_high(*expert_after(j, par))
                        dn_high(*expert_after(j, par))

            by_expert(act, first, body, lambda: weigh(EPAIRS - 1, 1, 1))

        @block.vector
        def _(dve):
            def column(per_slot, e):
                return per_slot.rearrange("p g (b e) -> p (g b) e", b=GB // GQ)[:, :, bass.ds(e, 1)]

            def rows_to_get(j, par):
                e = 2 * j + par
                for c in range(2):
                    until(dve, toks_in[c], 16 * CT * (e - 1))
                alone(dve)
                nc.vector.tensor_copy(row_get[par][:].unsqueeze(2), column(slot_row, e)).then_inc(get_set, 1)

            def rows_to_put(j, par):
                e = 2 * j + par
                for c in range(2):
                    until(dve, added[c], 16 * CT * (e - 1))
                alone(dve)
                nc.vector.tensor_copy(row_put[par][:].unsqueeze(2), column(slot_row, e)).then_inc(put_set, 1)
                until(dve, eo_done, 2 * CT * (e - 1))
                alone(dve)
                nc.vector.tensor_copy(weight_now[par][:].unsqueeze(2), column(slot_weight, e)).then_inc(put_set, 1)

            def gu_low(j, par):
                e = 2 * j + par
                dve.wait_ge(gu_hi_done, e + 1)
                nc.vector.tensor_tensor(gu_lo[par][:], gu_raw[:], gu_hi[par][:].bitcast(F32), ALU.subtract).then_inc(gu_lo_done, 1)

            def dn_low(j, par):
                e = 2 * j + par
                dve.wait_ge(dn_hi_done, e + 1)
                nc.vector.tensor_tensor(dn_lo[par][:], dn_raw[:], dn_hi[par][:].bitcast(F32), ALU.subtract).then_inc(dn_lo_done, 1)

            def xt_low(j, par, c):
                n = 2 * (2 * j + par) + c
                for k in range(KT):
                    dve.wait_ge(xt_hi_done, 2 * n + k + 1)
                    nc.vector.tensor_tensor(xt_lo[c][:, k, :], turned[k][:], xt_hi[c][:, k, :].bitcast(F32), ALU.subtract).then_inc(xt_lo_done, 1)

            def hidden(j, par, c, f):
                n = 2 * (2 * j + par) + c
                dve.wait_ge(gelu_done, 4 * n + f + 1)
                until(dve, hid_lo_done, 4 * n + f - 1)
                nc.vector.tensor_tensor(hid[f % 2][:], up_ps[f % 2][:], gelu[f % 2][:], ALU.mult).then_inc(hid_done, 1)

            def hid_low(j, par, c, f):
                n = 2 * (2 * j + par) + c
                dve.wait_ge(hid_hi_done, 4 * n + f + 1)
                nc.vector.tensor_tensor(hid_lo[c][:, f, :], hid[f % 2][:], hid_hi[c][:, f, :].bitcast(F32), ALU.subtract).then_inc(hid_lo_done, 1)

            def first():
                rows_to_get(0, 0)
                rows_to_put(0, 0)
                gu_low(0, 0)
                xt_low(0, 0, 0)
                dn_low(0, 0)

            def body(j, par, has_prev, has_next):
                for c in range(2):
                    if c == 0 and has_next:
                        rows_to_get(*expert_after(j, par))
                    hidden(j, par, c, 0)
                    hidden(j, par, c, 1)
                    hid_low(j, par, c, 0)
                    hid_low(j, par, c, 1)
                    if c == 0 or has_next:
                        xt_low(*chunk_after(j, par, c))
                    hidden(j, par, c, 2)
                    hidden(j, par, c, 3)
                    hid_low(j, par, c, 2)
                    hid_low(j, par, c, 3)
                    if c == 0 and has_next:
                        gu_low(*expert_after(j, par))
                        dn_low(*expert_after(j, par))
                        rows_to_put(*expert_after(j, par))

            by_expert(dve, first, body, lambda: None)

        @block.tensor
        def _(pe):
            def turn(j, par, c):
                e = 2 * j + par
                n = 2 * e + c
                pe.wait_ge(toks_in[c], 16 * CT * e + 16 * CT)
                until(pe, xt_lo_done, 2 * n)
                for k in range(KT):
                    for m in range(CT):
                        last = nc.tensor.transpose(turned[k][:, m * P:(m + 1) * P], toks[c][:, m, k * P:(k + 1) * P], ident[:])
                    last.then_inc(xt_done, 1)

            def gate_up(j, par, c, f):
                e = 2 * j + par
                n = 2 * e + c
                if f == 0:
                    pe.wait_ge(gu_lo_done, e + 1)
                    pe.wait_ge(xt_lo_done, 2 * n + 2)
                until(pe, hid_done, 4 * n + f - 1)
                hi = gu_hi[par][:].rearrange("p (g k h) -> p g k h", g=2, k=KT)
                lo = gu_lo[par][:].rearrange("p (g k h) -> p g k h", g=2, k=KT)
                cols = slice(f * P, (f + 1) * P)
                for g, ps in ((0, gate_ps[f % 2]), (1, up_ps[f % 2])):
                    for k in range(KT):
                        last = exact_product(nc, ps[:], (hi[:, g, k, cols], lo[:, g, k, cols]),
                                             (xt_hi[c][:, k, :], xt_lo[c][:, k, :]), k == 0, k == KT - 1)
                last.then_inc(gate_up_done, 1)

            def down(j, par, c):
                e = 2 * j + par
                n = 2 * e + c
                pe.wait_ge(dn_lo_done, e + 1)
                pe.wait_ge(hid_lo_done, 4 * n + 4)
                hi = dn_hi[par][:].rearrange("p (h d) -> p h d", h=HT1)
                lo = dn_lo[par][:].rearrange("p (h d) -> p h d", h=HT1)
                for m in range(CT):
                    if m % 2 == 0:
                        until(pe, eo_done, CT * (n - 1) + m + 2)
                    cols = slice(m * P, (m + 1) * P)
                    for f in range(HT1):
                        last = exact_product(nc, down_ps[m // 2][:, m % 2, :], (hid_hi[c][:, f, cols], hid_lo[c][:, f, cols]),
                                             (hi[:, f, :], lo[:, f, :]), f == 0, f == HT1 - 1)
                    if m % 2:
                        last.then_inc(down_done, 1)

            def first():
                pe.wait_ge(const_in, 16)
                turn(0, 0, 0)

            def body(j, par, has_prev, has_next):
                for c in range(2):
                    gate_up(j, par, c, 0)
                    gate_up(j, par, c, 1)
                    if c == 1:
                        down(j, par, 0)
                    elif has_prev:
                        down(*before(j, par), 1)
                    if c == 0 or has_next:
                        turn(*chunk_after(j, par, c))
                    gate_up(j, par, c, 2)
                    gate_up(j, par, c, 3)

            by_expert(pe, first, body, lambda: down(EPAIRS - 1, 1, 1))


def block_program(nc, t):
    with ExitStack() as ctx:
        def sem(name):
            return ctx.enter_context(nc.semaphore(name))

        def scratch(name, shape, dt=F32):
            return nc.dram_tensor(name, shape, dt).ap()

        expert_dram = scratch("expert_dram", [B, 1], U32)
        c0 = scratch("c0", [B, P, TT, D])
        h = scratch("h", [B, P, TT, D])
        x1 = scratch("x1", [B, P, TT, D])
        hs = scratch("hs", [B, S, D])
        rows = "b s d -> (b s) d"

        moe_w = ctx.enter_context(nc.sbuf_tensor("moe_w", [P, KT, EM * D], F32))
        shared_gu, expert_gu = (ctx.enter_context(nc.sbuf_tensor(n, [P, 2 * KT * H1], F32)) for n in ("shared_gu", "expert_gu"))
        shared_d, expert_d = (ctx.enter_context(nc.sbuf_tensor(n, [P, HT1 * D], F32)) for n in ("shared_d", "expert_d"))
        moe_w_in, shared_in, expert_gu_in, expert_d_in = (sem(n) for n in ("moe_w_in", "shared_in", "expert_gu_in", "expert_d_in"))
        later_weights = ((moe_w, t["moe_w"], moe_w_in), (shared_gu, t["shared_gu"], shared_in), (shared_d, t["shared_d"], shared_in),
                         (expert_gu, t["expert_gu"][0], expert_gu_in), (expert_d, t["expert_d"][0], expert_d_in))

        cond_ffn_phase(nc, sem, t["x_t"], t["w_ug"], t["w_dn"], t["cond"], expert_dram, c0)
        attention_phase(nc, sem, c0, t["attn_norm_w"], t["w_qkv"], t["w_o"], t["ident"], t["causal"], h, later_weights)
        moe_phase(nc, sem, h, t["x"], t["ffn_norm_w"], t["moe_gate_w"], moe_w, moe_w_in, t["ident"], t["expert_iota"], x1)
        logits = ctx.enter_context(nc.sbuf_tensor("route_logits", [P, TT, B * E1], F32))
        slot_row = ctx.enter_context(nc.sbuf_tensor("slot_row", [P, GROUPS, CAP], U32))
        slot_weight = ctx.enter_context(nc.sbuf_tensor("slot_weight", [P, GROUPS, CAP], F32))
        lora_shared_phase(nc, sem, x1, t["cond_er"], t["w_base"], t["b_base"], t["lora_a"], t["lora_b"], t["route_w"],
                          shared_gu, shared_d, shared_in, t["ident"], hs, logits, t["out"])
        topk_phase(nc, sem, logits, t["first_row"], t["ident"], slot_row, slot_weight)
        experts_phase(nc, sem, hs.rearrange(rows), slot_row, slot_weight, t["expert_gu"], t["expert_d"],
                      expert_gu, expert_d, expert_gu_in, expert_d_in, t["ident"],
                      t["out"].rearrange(rows))


def lay_out(inputs):
    import numpy as np
    a = {n: np.asarray(v) for n, v in inputs.items()}

    def by_rows(w):
        w = np.swapaxes(w, -1, -2)
        w = w.reshape(w.shape[:-2] + (w.shape[-2] // P, P, w.shape[-1]))
        return np.swapaxes(w, -3, -2).reshape(w.shape[:-3] + (P, -1))

    def to_all(v):
        return np.broadcast_to(v, (P,) + v.shape)

    def by_slice(b):
        return b.reshape(E0, HT0, P).transpose(0, 2, 1)

    x = a["x"]
    L0, F0, C1, F1 = "L0_cond_", "L0_ffn_", "L1_cond_", "L1_ffn_"
    eye = np.eye(P, dtype=np.float32)
    later = np.arange(P)[None, :] > np.arange(P)[:, None]
    d = {
        "x_t": x.reshape(B, S, KT, P).transpose(0, 3, 2, 1),
        "x": x.reshape(B, TT, P, D).transpose(0, 2, 1, 3),
        "w_ug": np.concatenate([by_rows(a[L0 + "W_up"]), by_rows(a[L0 + "W_gate"]),
                                by_slice(a[L0 + "b_up"]), by_slice(a[L0 + "b_gate"])], 2),
        "w_dn": np.concatenate([by_rows(a[L0 + "W_down"]), np.broadcast_to(a[L0 + "b_down"][:, None], (E0, P, D))], 2),
        "cond": a["cond_8"],
        "attn_norm_w": to_all(a[F0 + "attn_norm_w"]),
        "ffn_norm_w": to_all(a[F0 + "ffn_norm_w"]),
        "w_qkv": by_rows(np.concatenate([a[F0 + "wq"], a[F0 + "wk"], a[F0 + "wv"]], 0)).reshape(P, KT, QKV),
        "w_o": by_rows(a[F0 + "wo"]).reshape(P, KT, D),
        "moe_gate_w": by_rows(a[F0 + "gate_w"]).reshape(P, KT, EM),
        "moe_w": by_rows(a[F0 + "expert_w"].reshape(EM * D, D)).reshape(P, KT, EM * D),
        "cond_er": np.repeat(a["cond_8"].T, ER // E0, axis=0),
        "w_base": by_rows(a[C1 + "W_base"]).reshape(P, KT, D),
        "b_base": to_all(a[C1 + "b_base"]),
        "lora_a": a[C1 + "As"].reshape(ER, D),
        "lora_b": a[C1 + "Bs"].transpose(0, 2, 1).reshape(ER, D),
        "route_w": by_rows(a[F1 + "gate_w"]).reshape(P, KT, E1),
        "shared_gu": np.concatenate([by_rows(a[F1 + "Ws_g"]), by_rows(a[F1 + "Ws_u"])], 1),
        "shared_d": by_rows(a[F1 + "Ws_d"]),
        "expert_gu": np.concatenate([by_rows(a[F1 + "Wg"]), by_rows(a[F1 + "Wu"])], 2),
        "expert_d": by_rows(a[F1 + "Wd"]),
        "ident": eye,
        "causal": np.where(later, MASKED, 0.0).astype(np.float32),
        "expert_iota": to_all(np.arange(EM, dtype=np.float32)),
        "first_row": np.repeat(S * np.arange(B, dtype=np.float32).reshape(GROUPS, GB).T, E1, axis=0),
    }
    return {n: np.ascontiguousarray(v) for n, v in d.items()}


def kernel(**inputs):
    import concourse.bacc as _bacc
    from concourse import mybir as _mybir
    from concourse.bass_utils import run_bass_kernel_spmd as _run

    nc = _bacc.Bacc("TRN2", target_bir_lowering=False, num_devices=1)
    arrays, t = {}, {}
    for name, a in lay_out(inputs).items():
        arrays[f"in_{name}"] = a
        t[name] = nc.dram_tensor(f"in_{name}", a.shape, _mybir.dt.from_np(a.dtype), kind="ExternalInput").ap()
    t["out"] = nc.dram_tensor("out", [B, S, D], F32, kind="ExternalOutput").ap()
    block_program(nc, t)
    r = _run(nc, [arrays], core_ids=[0])
    return r.results[0]["out"]
```
